# Optimizing a Trainium2 kernel written in Bass

```python
import numpy as np
import jax
import jax.numpy as jnp

def _softmax(x, axis=-1):
    return jax.nn.softmax(x, axis=axis)

def _gelu(x):
    return jax.nn.gelu(x, approximate=True)

def _silu(x):
    return jax.nn.silu(x)

def _sigmoid(x):
    return jax.nn.sigmoid(x)

def _layernorm(x, axis=-1, eps=1e-05):
    m = jnp.mean(x, axis=axis, keepdims=True)
    v = jnp.var(x, axis=axis, keepdims=True)
    return (x - m) / jnp.sqrt(v + eps)

def _scatter_add(tgt, idx, src, axis=0):
    return tgt.at[idx].add(src)

def _segment_sum(src, seg, n):
    return jax.ops.segment_sum(src, seg, n)
kernel_name = 'mk_decoder_postln_d1_seqx_r4_422b66'

def setup_inputs(seed: int=0):
    np.random.seed(seed)
    _w = jnp.asarray

    def _rec_inputs():
        import jax
        import jax.numpy as jnp
        _rk = jax.random.key(seed)
        x = -0.0003929 + 0.9999 * jax.random.normal(jax.random.fold_in(_rk, 1), (16, 128, 1024), jnp.float32)
        _lenS = 128 - jax.random.randint(jax.random.fold_in(_rk, 7), (16,), 0, max(1, 128 // 4) + 1, jnp.int32)
        _lenS2 = 128 - jax.random.randint(jax.random.fold_in(_rk, 8), (16,), 0, max(1, 128 // 4) + 1, jnp.int32)
        _ctx_4096P = jax.random.normal(jax.random.fold_in(_rk, 11), (16, 16, 1024), jnp.float32)
        _ctx_4096c = jax.random.dirichlet(jax.random.fold_in(_rk, 511), 0.3 * jnp.ones((16,), jnp.float32), (16, 128))
        _ctx_4096t = jnp.einsum('bsk,bkd->bsd', _ctx_4096c, _ctx_4096P)
        _ctx_4096t = _ctx_4096t * jax.lax.rsqrt(jnp.mean(jnp.square(_ctx_4096t)) + 1e-12) * 0.953939
        ctx_4096 = 2.81802e-05 + 1.00001 * (_ctx_4096t + 0.3 * jax.random.normal(jax.random.fold_in(_rk, 611), (16, 128, 1024), jnp.float32))
        return (x, ctx_4096)
    x, ctx_4096 = _rec_inputs()

    def _L0_attn_setup():
        import jax, jax.numpy as jnp
        import numpy as np
        H = 1024
        D_IN = 2048
        N = 16
        K = 4
        R = 64
        EPS = 1e-06

        def rms_forward(x, eps=EPS):
            xf = x.astype(jnp.float32)
            var = jnp.mean(xf * xf, axis=-1, keepdims=True)
            return (xf * jax.lax.rsqrt(var + eps)).astype(x.dtype)
        key = jax.random.key(seed)
        ks = jax.random.split(key, 10)
        s = 0.02
        hidden_states = jax.random.normal(ks[0], (2, 256, H), dtype=jnp.float32)
        W_in = jax.random.normal(ks[1], (2 * D_IN, H), dtype=jnp.float32) * s
        conv_w = jax.random.normal(ks[2], (D_IN, K), dtype=jnp.float32) * 0.2
        conv_b = jax.random.normal(ks[3], (D_IN,), dtype=jnp.float32) * 0.02
        W_x = jax.random.normal(ks[4], (R + 2 * N, D_IN), dtype=jnp.float32) * s
        W_dt = jax.random.normal(ks[5], (D_IN, R), dtype=jnp.float32) * s
        b_dt = jax.random.normal(ks[6], (D_IN,), dtype=jnp.float32) * 0.02
        A_log = jnp.log(jnp.broadcast_to(jnp.arange(1, N + 1, dtype=jnp.float32)[None, :], (D_IN, N)))
        D = jnp.ones((D_IN,), dtype=jnp.float32)
        W_out = jax.random.normal(ks[7], (H, D_IN), dtype=jnp.float32) * s
        return {'hidden_states': hidden_states, 'W_in': W_in, 'conv_w': conv_w, 'conv_b': conv_b, 'W_x': W_x, 'W_dt': W_dt, 'b_dt': b_dt, 'A_log': A_log, 'D': D, 'W_out': W_out}
    _L0_attn_all = _L0_attn_setup()
    _L0_attn_in = {k: v for k, v in _L0_attn_all.items() if k in ('W_in', 'conv_w', 'conv_b', 'W_x', 'W_dt', 'b_dt', 'A_log', 'D', 'W_out')}
    del _L0_attn_all

    def _L0_xattn_setup():
        import jax, jax.numpy as jnp
        import numpy as np
        DIM = 128
        HEADS = 8
        DIM_HEAD = 64
        HIDDEN = HEADS * DIM_HEAD
        SCALE = DIM_HEAD ** (-0.5)
        key = jax.random.key(seed)
        ks = jax.random.split(key, 9)
        b, n = (8, 1024)
        std = 1.0 / np.sqrt(DIM)
        return {'q': jax.random.normal(ks[0], (b, DIM, n), jnp.float32), 'k': jax.random.normal(ks[1], (b, DIM, n), jnp.float32), 'v': jax.random.normal(ks[2], (b, DIM, n), jnp.float32), 'Wq': jax.random.normal(ks[3], (HIDDEN, DIM), jnp.float32) * std, 'Wk': jax.random.normal(ks[4], (HIDDEN, DIM), jnp.float32) * std, 'Wv': jax.random.normal(ks[5], (HIDDEN, DIM), jnp.float32) * std, 'Wo': jax.random.normal(ks[6], (DIM, HIDDEN), jnp.float32) * (1.0 / np.sqrt(HIDDEN)), 'bo': jax.random.normal(ks[7], (DIM,), jnp.float32) * 0.01, 'g': jnp.ones((1, DIM, 1), jnp.float32)}
    _L0_xattn_all = _L0_xattn_setup()
    _L0_xattn_in = {k: v for k, v in _L0_xattn_all.items() if k in ('Wq', 'Wk', 'Wv', 'Wo', 'bo', 'g')}
    del _L0_xattn_all

    def _L0_ffn_setup():
        import jax, jax.numpy as jnp
        import numpy as np
        LORA_SCALE = 16.0 / jnp.sqrt(16.0)
        TOP_K = 2
        key = jax.random.key(seed)
        k1, k2, k3, k4 = jax.random.split(key, 4)
        B_, S, D, O, E, R = (4, 512, 1024, 1024, 4, 16)
        x = jax.random.normal(k1, (B_, S, D), dtype=jnp.float32)
        router_w = jax.random.normal(k2, (E, D), dtype=jnp.float32) * 0.02
        A = jax.random.normal(k3, (E, R, D), dtype=jnp.float32) * 0.02
        B = jax.random.normal(k4, (O,), dtype=jnp.float32)
        B = jax.random.normal(k4, (E, O, R), dtype=jnp.float32) * 0.02
        return {'x': x, 'router_w': router_w, 'A': A, 'B': B}
    _L0_ffn_all = _L0_ffn_setup()
    _L0_ffn_in = {k: v for k, v in _L0_ffn_all.items() if k in ('router_w', 'A', 'B')}
    del _L0_ffn_all
    return {'x': x, 'ctx_4096': ctx_4096, 'L0_attn_W_in': _L0_attn_in['W_in'], 'L0_attn_conv_w': _L0_attn_in['conv_w'], 'L0_attn_conv_b': _L0_attn_in['conv_b'], 'L0_attn_W_x': _L0_attn_in['W_x'], 'L0_attn_W_dt': _L0_attn_in['W_dt'], 'L0_attn_b_dt': _L0_attn_in['b_dt'], 'L0_attn_A_log': _L0_attn_in['A_log'], 'L0_attn_D': _L0_attn_in['D'], 'L0_attn_W_out': _L0_attn_in['W_out'], 'L0_xattn_Wq': _L0_xattn_in['Wq'], 'L0_xattn_Wk': _L0_xattn_in['Wk'], 'L0_xattn_Wv': _L0_xattn_in['Wv'], 'L0_xattn_Wo': _L0_xattn_in['Wo'], 'L0_xattn_bo': _L0_xattn_in['bo'], 'L0_xattn_g': _L0_xattn_in['g'], 'L0_ffn_router_w': _L0_ffn_in['router_w'], 'L0_ffn_A': _L0_ffn_in['A'], 'L0_ffn_B': _L0_ffn_in['B']}

def reference(x, ctx_4096, L0_attn_W_in, L0_attn_conv_w, L0_attn_conv_b, L0_attn_W_x, L0_attn_W_dt, L0_attn_b_dt, L0_attn_A_log, L0_attn_D, L0_attn_W_out, L0_xattn_Wq, L0_xattn_Wk, L0_xattn_Wv, L0_xattn_Wo, L0_xattn_bo, L0_xattn_g, L0_ffn_router_w, L0_ffn_A, L0_ffn_B):
    import jax
    import jax.numpy as jnp

    def _L0_attn_ref(hidden_states, W_in, conv_w, conv_b, W_x, W_dt, b_dt, A_log, D, W_out):
        import jax, jax.numpy as jnp
        import numpy as np
        H = 1024
        D_IN = 2048
        N = 16
        K = 4
        R = 64
        EPS = 1e-06

        def rms_forward(x, eps=EPS):
            xf = x.astype(jnp.float32)
            var = jnp.mean(xf * xf, axis=-1, keepdims=True)
            return (xf * jax.lax.rsqrt(var + eps)).astype(x.dtype)
        b, L, _ = hidden_states.shape
        proj = hidden_states @ W_in.T
        x, gate = (proj[..., :D_IN], proj[..., D_IN:])
        xpad = jnp.pad(x, ((0, 0), (K - 1, 0), (0, 0)))
        xc = conv_b
        for j in range(K):
            xc = xc + conv_w[:, j] * xpad[:, j:j + L, :]
        x = jax.nn.silu(xc)
        ssm = x @ W_x.T
        ts, Bm, Cm = (ssm[..., :R], ssm[..., R:R + N], ssm[..., R + N:])
        ts = rms_forward(ts)
        Bm = rms_forward(Bm)
        Cm = rms_forward(Cm)
        dt = jax.nn.softplus(ts @ W_dt.T + b_dt)
        A = -jnp.exp(A_log.astype(jnp.float32))

        def step(state, inp):
            dt_t, B_t, C_t, u_t = inp
            dA = jnp.exp(dt_t[..., None] * A)
            state = state * dA + (dt_t * u_t)[..., None] * B_t[:, None, :]
            y = jnp.einsum('bdn,bn->bd', state, C_t)
            return (state, y)
        init = jnp.zeros((b, D_IN, N), dtype=jnp.float32)
        xs = (dt.transpose(1, 0, 2), Bm.transpose(1, 0, 2), Cm.transpose(1, 0, 2), x.transpose(1, 0, 2))
        _, ys = jax.lax.scan(step, init, xs)
        y = ys.transpose(1, 0, 2) + x * D
        y = y * jax.nn.silu(gate)
        return y @ W_out.T

    def _L0_xattn_ref(q, k, v, Wq, Wk, Wv, Wo, bo, g):
        import jax, jax.numpy as jnp
        import numpy as np
        DIM = 128
        HEADS = 8
        DIM_HEAD = 64
        HIDDEN = HEADS * DIM_HEAD
        SCALE = DIM_HEAD ** (-0.5)
        b = q.shape[0]
        qh = jnp.einsum('bcn,oc->bon', q, Wq).reshape(b, HEADS, DIM_HEAD, -1)
        kh = jnp.einsum('bcn,oc->bon', k, Wk).reshape(b, HEADS, DIM_HEAD, -1)
        vh = jnp.einsum('bcn,oc->bon', v, Wv).reshape(b, HEADS, DIM_HEAD, -1)
        qh = jax.nn.softmax(qh, axis=-2) * SCALE
        kh = jax.nn.softmax(kh, axis=-1)
        context = jnp.einsum('bhdn,bhen->bhde', kh, vh)
        out = jnp.einsum('bhde,bhdn->bhen', context, qh)
        out = out.reshape(b, HIDDEN, -1)
        out = jnp.einsum('bcn,oc->bon', out, Wo) + bo[None, :, None]
        norm = jnp.maximum(jnp.sqrt(jnp.sum(out * out, axis=1, keepdims=True)), 1e-12)
        return out / norm * g * np.sqrt(DIM)

    def _L0_ffn_ref(x, router_w, A, B):
        import jax, jax.numpy as jnp
        import numpy as np
        LORA_SCALE = 16.0 / jnp.sqrt(16.0)
        TOP_K = 2
        D = x.shape[-1]
        flat = x.reshape(-1, D)
        logits = flat @ router_w.T
        topk_vals, topk_idx = jax.lax.top_k(logits, TOP_K)
        sparse = jnp.full_like(logits, -jnp.inf)
        rows = jnp.arange(logits.shape[0])[:, None]
        sparse = sparse.at[rows, topk_idx].set(topk_vals)
        gates = jax.nn.softmax(sparse, axis=-1)
        mid = jnp.einsum('tf,erf->ter', flat, A)
        all_deltas = jnp.einsum('ter,eor->teo', mid, B) * LORA_SCALE
        delta = jnp.einsum('te,teo->to', gates, all_deltas)
        return delta.reshape(*x.shape[:-1], -1)
    x = _layernorm(x + _L0_attn_ref(x, L0_attn_W_in, L0_attn_conv_w, L0_attn_conv_b, L0_attn_W_x, L0_attn_W_dt, L0_attn_b_dt, L0_attn_A_log, L0_attn_D, L0_attn_W_out), axis=-1)
    x = _layernorm(x + _L0_xattn_ref(x, ctx_4096, ctx_4096, L0_xattn_Wq, L0_xattn_Wk, L0_xattn_Wv, L0_xattn_Wo, L0_xattn_bo, L0_xattn_g), axis=-1)
    x = _layernorm(x + _L0_ffn_ref(x, L0_ffn_router_w, L0_ffn_A, L0_ffn_B), axis=-1)
    return x

_drawn_inputs = setup_inputs


def setup_inputs(seed=0):
    import zlib

    import numpy as np

    out = dict(_drawn_inputs(seed))
    spreads = {'L0_attn_D': (1.0, 0.6), 'L0_xattn_g': (1.0, 0.2)}
    factors = {'L0_attn_conv_b': 2.869, 'L0_attn_W_dt': 2.726, 'L0_attn_b_dt': 21.689}
    for name, (base, spread) in spreads.items():
        noise = np.random.default_rng([zlib.crc32(name.encode()), seed]).standard_normal(out[name].shape)
        drawn = base * np.exp(spread * noise) if base else spread * noise
        out[name] = jnp.asarray(drawn.astype(out[name].dtype))
    for name, factor in factors.items():
        out[name] = (out[name] * factor).astype(out[name].dtype)
    return out
```

```python
from contextlib import ExitStack

import numpy as np

import concourse.bass as bass
from concourse import mybir

ALU = mybir.AluOpType
ACT = mybir.ActivationFunctionType
F32 = mybir.dt.float32
AX_X = mybir.AxisListType.X
LN_EXP_SET = "natural_log_exp_and_others"
SILU_SET = "silu_and_others"

P = 128
BATCH, SEQ, H = 16, 128, 1024
TOK = BATCH * SEQ
D_IN, N, R = 2048, 16, 64
DT = D_IN // P
KC = H // P
GB = 4
GT = GB * SEQ
NG = TOK // GT
QD = 4
NQ = DT // QD
TT = TOK // P
SS = R + 2 * N
HEADS, DH = 8, 64
HID = HEADS * DH
OT = HID // P
NT = H // P
NE, ER = 4, 16
RA = NE + NE * ER
HALF = 512
LN_EPS, RMS_EPS = 1e-5, 1e-6
GATE_STEPS = 12

X_MM, CONV, SS_ADD = 8, 8, 4
T_DONE, SCAN, ACCD, R_ADD, FIN1, FIN, Z_MM, BM = 13, 2, 2, 2, 2, 5, 2, 13
ONE = 1

SEMS = """const_loaded pool_const rows_set bdt_loaded a_exp a_neg x_mm conv_base conv_tap conv_done u_done
ss_mm ss_added ss_square ss_sum ss_mean ss_rstd ss_normed bt_mm bt_rows b_stored wx_loaded0 wx_loaded1 u_stored0 u_stored1
phase0_zero phase0_c da_zero xg_loaded wz_loaded0 wz_loaded1 wo_loaded u_loaded0 u_loaded1 r_loaded
brep_loaded0 brep_loaded1 brep_loaded2 brep_loaded3 dt_mm dt_abs dt_exp dt_ln dt_ok dtu_ok cg_ok exp_ok bm_ok
scan_ok t_done acc_ok yt_mm fin1 fin z_mm z_copied z_silu o_mm r_added ln_stats ln_aggr ln_eps ln_rstd
ln_ok x1_stored
p2_const ph_mm ph_ok gs_ok cn_loaded ct_loaded x1_loaded xres_loaded out_stored
k_mm k_max k_neg k_exp et_mm et_act et_dve g_mm g_ok rk1 rk2 mt_mm mt_ok
q_mm q_max q_sub q_exp q_sum q_rec q_norm qt_mm qs_act qs_dve out_mm ob_ok sq_ok
ssq_mm ssq_max ssq_pow dg_ok bc_mm y2a y2_ok l2_stats l2_aggr l2_eps l2_rstd x2_ok x2t_mm x2t_ok
ra_mm gate_step lg_neg gate_exp mg_ok mgt_mm mgt_ok delta_mm x3_add x3_ok""".split()


def program(nc, a, out):
    u_d = nc.dram_tensor("u_scratch", (DT, P, TOK), F32, kind="Internal").ap()
    b_d = nc.dram_tensor("b_scratch", (N, TOK), F32, kind="Internal").ap()
    x1_d = nc.dram_tensor("x1_scratch", (NG + 1, GB, P, H), F32, kind="Internal").ap()

    with ExitStack() as ctx:
        def sb(name, shape):
            return ctx.enter_context(nc.sbuf_tensor(name, shape, F32))

        S = {name: ctx.enter_context(nc.semaphore(name)) for name in SEMS}

        arena = sb("arena", [P, 43008])

        def at(off, *dims):
            v = arena[:, off:off + int(np.prod(dims))]
            if len(dims) == 1:
                return v
            names = "abcd"[:len(dims)]
            return v.rearrange("p (%s) -> p %s" % (" ".join(names), " ".join(names)),
                               **dict(zip(names[1:], dims[1:])))

        xT = at(0, KC, TOK)
        wxc = [at(26624 + 1536 + 1040 * i, H + 5) for i in range(2)]
        wx = [v[:, 0:H].rearrange("p (k m) -> p k m", k=KC) for v in wxc]
        ust = [at(18432 + 2048 * i, TOK) for i in range(2)]
        cv = [at(22528 + GT * i, GT) for i in range(2)]
        wxT = at(23552, DT, SS)
        ssacc = at(25088, TT, SS)
        sssq = at(26624, TT, SS)
        brep = at(0, N, GT)
        hb = [at(8192 + 2048 * i, QD * GT) for i in range(4)]
        xg = at(16384, KC, GT)
        wz = [at(20480 + 1024 * i, KC, P) for i in range(2)]
        wo = at(22528, QD, H)
        uq = [at(26624 + 2048 * i, QD, GT) for i in range(2)]
        dt = [at(30720 + 2048 * i, QD, GT) for i in range(2)]
        dtu = at(34816, QD, GT)
        zs = at(36864, QD, GT)
        acc = at(38912, GB, QD * P)
        yq = at(40960, QD, GT)
        x1 = at(0, H)
        xres = at(1024, H)
        cn = at(2048, H)
        cT = at(3072, NT, P)
        ek = at(4096, OT, H)
        ekT = at(8192, NT, HID)
        gT = at(12288, HID)
        mt = at(12800, OT, P)
        qe = at(13312, NT, HID)
        qs = at(17408, OT, H)
        ob = at(21504, H)
        sq = at(22528, H)
        dg = at(23552, NT, P)
        x2 = at(24576, H)
        x2T = at(25600, KC, P)
        mg = at(26624, P)
        mgT = at(26752, P)
        x3 = at(26880, H)
        wq = at(27904, HID)
        wk = at(28416, HID)
        ph = at(28928, HEADS, P)
        wvh = at(29952, HEADS, P)
        woh = at(30976, HEADS, P)
        rat = at(32000, KC, RA)
        bful = at(32544, H)

        rbuf = sb("rbuf", [P, GB, H])
        wdt = sb("wdt", [P, D_IN])
        tsb = sb("tsb", [P, TOK])
        a_sb = sb("a_sb", [P, DT, N])
        cbt = sb("cbt", [P, TT, N])
        cg = sb("cg", [P, GB, N])
        dsk = sb("dsk", [P, DT])
        idle = sb("idle", [P, 1])
        ident = sb("ident", [P, P])
        ones = sb("ones", [P, P])
        mhalf = sb("mhalf", [P, 3 * TT])
        ss3 = sb("ss3", [P, 3, TT])
        st1 = sb("st1", [P, GB, 2, 6])
        mv1 = sb("mv1", [P, GB, 2])
        ve1 = sb("ve1", [P, GB])
        bov = sb("bov", [P, 2])
        gs = sb("gs", [P, 1])
        km = sb("km", [P, OT])
        nkm = sb("nkm", [P, OT])
        ksum = sb("ksum", [P, OT])
        rk = sb("rk", [P, OT])
        qm = sb("qm", [P, 2, HEADS])
        qz = sb("qz", [P, 2, HEADS])
        qr = sb("qr", [P, 2, HEADS])
        rn = sb("rn", [P, NT])
        lg = sb("lg", [P, NE])
        nlm = sb("nlm", [P, 1])
        lex = sb("lex", [P, NE])
        cgt = sb("cgt", [P, NE, NE])
        cge = sb("cge", [P, NE, NE])
        upper = sb("upper", [P, NE, NE])
        lower = sb("lower", [P, NE, NE])
        rank = sb("rank", [P, NE])
        gate = sb("gate", [P, NE])
        gsum = sb("gsum", [P, 1])

        banks = [ctx.enter_context(nc.psum_tensor(f"banks{i}", [P, 2 * HALF], F32)) for i in range(4)]

        def bank(i):
            return banks[i // 2][:, (i % 2) * HALF:(i % 2 + 1) * HALF]

        def by_seq(ap):
            return ap.rearrange("p (b t) -> p b t", b=GB)

        consts0 = [(xT, "xT"), (wxT, "WxT"), (wdt[0:R, :], "WdtT"), (a_sb[:, :, :], "A_log"),
                   (dsk[:, :], "D")]
        consts2 = [(wq, "WqT"), (wk, "WkT"), (wvh[0:DH], "Wvh"), (woh[0:DH], "Woh"), (rat, "RAT"),
                   (bful[0:NE * ER, :], "Bf"), (bov[:, 0:1], "bo"), (bov[:, 1:2], "g")]
        C0, C2 = 16 * len(consts0), 16 * len(consts2)

        def sync_step(sp, g, q):
            s = NQ * g + q
            sp.wait_ge(S["fin"], 4 * s - 4 + FIN)
            sp.dma_start(uq[q % 2], u_d[QD * q:QD * (q + 1), :, bass.ds(g * GT, GT)]
                         .rearrange("d p t -> p d t")).then_inc(S[f"u_loaded{q % 2}"], 16)
            if q == 0:
                sp.wait_ge(S["z_mm"], 16 * g + Z_MM)
                sp.dma_start(xg, a["xT"][:, :, bass.ds(g * GT, GT)]).then_inc(S["xg_loaded"], 16)

            def gate_weights(i):
                sp.wait_ge(S["z_mm"], 4 * s + i - 1 + Z_MM)
                sp.dma_start(wz[i % 2], a["WinZ"][QD * q + i]).then_inc(S[f"wz_loaded{i % 2}"], 16)

            gate_weights(0)
            gate_weights(1)
            if q == 0:
                for j in range(4):
                    sp.wait_ge(S["bm_ok"], 64 * g + 4 * j - 12 + BM)
                    sp.dma_start(brep[:, 4 * j:4 * j + 4, :],
                                 b_d[4 * j:4 * j + 4, bass.ds(g * GT, GT)].partition_broadcast(P))\
                        .then_inc(S[f"brep_loaded{j}"], 16)
            gate_weights(2)
            gate_weights(3)
            sp.wait_ge(S["o_mm"], 8 * s + ONE)
            sp.dma_start(wo, a["WoutT"][(q - 1) % NQ]).then_inc(S["wo_loaded"], 16)
            if q == 1:
                sp.wait_ge(S["ln_ok"], GB * (g + 1))
                sp.dma_start(x1_d[bass.ds(g, 1)].rearrange("a b p h -> p (a b) h"), rbuf[:, :, :])\
                    .then_inc(S["x1_stored"], 16)
                sp.wait_ge(S["x1_stored"], 16 * (g + 1))
                sp.dma_start(rbuf[:, :, :], a["x"][bass.ds(g, 1)].rearrange("a p b h -> (a p) b h"))\
                    .then_inc(S["r_loaded"], 16)

        def sync_store(sp, b):
            sp.wait_ge(S["x3_ok"], b + 1)
            sp.dma_start(out[bass.ds(b, 1)].rearrange("a p h -> (a p) h"), x3)\
                .then_inc(S["out_stored"], 16)

        def sync_seq(sp, b, store=None):
            sp.wait_ge(S["k_mm"], 4 * b)
            sp.dma_start(cn, a["ctx"][bass.ds(b, 1)].rearrange("a p n -> (a p) n"))\
                .then_inc(S["cn_loaded"], 16)
            sp.wait_ge(S["g_mm"], b)
            sp.dma_start(cT, a["ctxT"][bass.ds(b, 1)].rearrange("a p n c -> (a p) n c"))\
                .then_inc(S["ct_loaded"], 16)
            row = x1_d.rearrange("g b p h -> (g b) p h")[bass.ds(b + GB, 1)].rearrange("a p h -> (a p) h")
            sp.wait_ge(S["q_mm"], 8 * b)
            sp.dma_start(x1, row).then_inc(S["x1_loaded"], 16)
            if store is not None:
                sync_store(sp, store)
            sp.wait_ge(S["y2_ok"], b)
            sp.dma_start(xres, row).then_inc(S["xres_loaded"], 16)

        def pe_dt(pe, g, q, i):
            d = QD * q + i
            nc.tensor.matmul(bank(4 + i % 2), wdt[:, d * P:(d + 1) * P], tsb[:, bass.ds(g * GT, GT)],
                             start=True, stop=True).then_inc(S["dt_mm"], 1)

        def pe_out(pe, s, c, ks, last_quad=False):
            for k in ks:
                if k == 0:
                    if last_quad or c >= 2:
                        pe.wait_ge(S["r_added"], 8 * s + c - 1 + R_ADD)
                    if c < 2:
                        pe.wait_ge(S["z_copied"], 4 * s if last_quad else 4 * s + 3 + c)
                last = nc.tensor.matmul(bank(6 + c % 2), yq[:, k, (c // 2) * P:(c // 2 + 1) * P],
                                        wo[:, k, (c % 2) * HALF:(c % 2 + 1) * HALF],
                                        start=(k == 0), stop=(k == QD - 1))
                if k == QD - 1:
                    last.then_inc(S["o_mm"], 1)

        def pe_step(pe, g, q):
            s = NQ * g + q
            if q == 0:
                pe.wait_ge(S["xg_loaded"], 16 * g + 16)
            for n in range(N):
                U = N * s + n

                def turn(b):
                    pe.wait_ge(S["acc_ok"], 4 * U + b - 1 + ACCD)
                    for i in range(QD):
                        last = nc.tensor.transpose(bank(2 + b % 2)[:, i * P:(i + 1) * P],
                                                   hb[n % 4][:, i * GT + b * P:i * GT + (b + 1) * P],
                                                   ident[:, :])
                    last.then_inc(S["t_done"], 1)

                def filler(part):
                    if n < 8:
                        i = n // 2
                        if n % 2 == 0 and part == 0:
                            pe.wait_ge(S[f"wz_loaded{i % 2}"], 16 * (2 * s + i // 2 + 1))
                            if i < 2:
                                pe.wait_ge(S["r_added"], 8 * s + i - 1 + R_ADD)
                            else:
                                pe.wait_ge(S["z_copied"], 4 * s + i - 1)
                        for k in range(4 * (n % 2) + 2 * part, 4 * (n % 2) + 2 * part + 2):
                            last = nc.tensor.matmul(bank(6 + i % 2), wz[i % 2][:, k, :], xg[:, k, :],
                                                    start=(k == 0), stop=(k == KC - 1))
                        if k == KC - 1:
                            last.then_inc(S["z_mm"], 1)
                    else:
                        if n == 8 and part == 0:
                            pe.wait_ge(S["wo_loaded"], 16 * s + 16)
                        pe_out(pe, s, n - 8, range(2 * part, 2 * part + 2))

                pe.wait_ge(S["scan_ok"], 4 * U + 4 + SCAN)
                turn(0)
                turn(1)
                filler(0)
                turn(2)
                turn(3)
                filler(1)
                if q < NQ - 1 and n in (7, 11):
                    for i in ((0, 1) if n == 7 else (2, 3)):
                        if i >= 2:
                            pe.wait_ge(S["dt_ok"], 4 * (s + 1) + i - 1)
                        elif q == 0:
                            pe.wait_ge(S["dt_ok"], 4 * s + 3 + i)
                        else:
                            pe.wait_ge(S["fin1"], 4 * s + i - 1 + FIN1)
                        pe_dt(pe, g, q + 1, i)
            pe.wait_ge(S["acc_ok"], 4 * (N * s + N) + ACCD)
            for i in range(QD):
                if i < 2 and q < NQ - 1:
                    pe.wait_ge(S["dt_ok"], 4 * (s + 1) + 3 + i)
                else:
                    pe.wait_ge(S["fin1"], 4 * s + i - 1 + FIN1)
                for b in range(GB):
                    last = nc.tensor.transpose(bank(4 + i % 2)[:, b * P:(b + 1) * P],
                                               acc[:, b, i * P:(i + 1) * P], ident[:, :])
                last.then_inc(S["yt_mm"], 1)

        def pe_keys1(pe, b):
            pe.wait_ge(S["cn_loaded"], 16 * b + 16)
            for o in range(OT):
                if o == 0:
                    pe.wait_ge(S["q_sub"], 8 * b)
                elif o == 1:
                    pe.wait_ge(S["sq_ok"], b)
                    pe.wait_ge(S["ob_ok"], b)
                else:
                    pe.wait_ge(S["k_exp"], 4 * b + o - 1)
                for h in range(2):
                    last = nc.tensor.matmul(bank(2 * (o % 2) + h), wk[:, o * P:(o + 1) * P],
                                            cn[:, h * HALF:(h + 1) * HALF], start=True, stop=True)
                last.then_inc(S["k_mm"], 1)

        def pe_keys2(pe, b):
            pe.wait_ge(S["k_exp"], 4 * b + 4)
            for t in range(NT):
                ev = "et_act" if t % 2 == 0 else "et_dve"
                if t < 2:
                    pe.wait_ge(S["qs_act" if t == 0 else "qs_dve"], 4 * b)
                else:
                    pe.wait_ge(S[ev], 4 * b + t // 2)
                for o in range(OT):
                    last = nc.tensor.transpose(bank(4 + t % 2)[:, o * P:(o + 1) * P],
                                               ek[:, o, t * P:(t + 1) * P], ident[:, :])
                last.then_inc(S["et_mm"], 1)

        def pe_keys3(pe, b):
            pe.wait_ge(S["ct_loaded"], 16 * b + 16)
            pe.wait_ge(S["et_act"], 4 * b + 4)
            pe.wait_ge(S["et_dve"], 4 * b + 4)
            pe.wait_ge(S["g_ok"], b)
            for t in range(NT):
                last = nc.tensor.matmul(bank(6), cT[:, t, :], ekT[:, t, :], start=(t == 0),
                                        stop=(t == NT - 1))
            last.then_inc(S["g_mm"], 1)

        def pe_keys4(pe, b):
            pe.wait_ge(S["g_ok"], b + 1)
            for o in range(OT):
                last = nc.tensor.matmul(banks[0][:, o * 2 * P:(o + 1) * 2 * P], gT[:, o * P:(o + 1) * P],
                                        ph[:, 2 * o:2 * o + 2, :].rearrange("p a c -> p (a c)"),
                                        start=True, stop=True)
            last.then_inc(S["mt_mm"], 1)

        def pe_queries(pe, b):
            pe.wait_ge(S["x1_loaded"], 16 * b + 16)

            def project(t):
                if t < 2:
                    pe.wait_ge(S["mt_ok"], 2 * b + 2)
                else:
                    pe.wait_ge(S["q_sub"], 8 * b + t - 1)
                nc.tensor.matmul(bank(t % 2), x1[:, t * P:(t + 1) * P], wq, start=True, stop=True)\
                    .then_inc(S["q_mm"], 1)

            def turn(t):
                pe.wait_ge(S["q_norm"], 8 * b + t + 1)
                if t >= 2:
                    pe.wait_ge(S["qs_act" if t % 2 == 0 else "qs_dve"], 4 * b + t // 2)
                for o in range(OT):
                    last = nc.tensor.transpose(bank(4 + t % 2)[:, o * P:(o + 1) * P],
                                               qe[:, t, o * P:(o + 1) * P], ident[:, :])
                last.then_inc(S["qt_mm"], 1)

            for t in range(NT + 3):
                if t < NT:
                    project(t)
                if t >= 3:
                    turn(t - 3)

        def pe_attend(pe, b):
            pe.wait_ge(S["qs_act"], 4 * b + 4)
            pe.wait_ge(S["qs_dve"], 4 * b + 4)
            pe.wait_ge(S["x3_add"], b + ONE)
            for h in range(2):
                for o in range(OT):
                    last = nc.tensor.matmul(bank(2 + h), mt[:, o, :], qs[:, o, h * HALF:(h + 1) * HALF],
                                            start=(o == 0), stop=(o == OT - 1))
                last.then_inc(S["out_mm"], 1)

        def pe_tail1(pe, b):
            pe.wait_ge(S["sq_ok"], b + 1)
            pe.wait_ge(S["mgt_ok"], b + ONE)
            for t in range(NT):
                last = nc.tensor.matmul(bank(7)[:, t:t + 1], sq[:, t * P:(t + 1) * P], ones[:, 0:1],
                                        start=True, stop=True)
            last.then_inc(S["ssq_mm"], 1)

        def pe_tail2(pe, b):
            pe.wait_ge(S["dg_ok"], b + 1 + ONE)
            for h in range(2):
                last = nc.tensor.matmul(bank(2 + h), ones[:, :],
                                        dg[:, 4 * h:4 * h + 4, :].rearrange("p a c -> p (a c)"),
                                        start=True, stop=True)
            last.then_inc(S["bc_mm"], 1)

        def pe_tail3(pe, b):
            pe.wait_ge(S["x2_ok"], b + 1)
            for k in range(KC):
                last = nc.tensor.transpose(banks[1][:, k * P:(k + 1) * P], x2[:, k * P:(k + 1) * P],
                                           ident[:, :])
            last.then_inc(S["x2t_mm"], 1)
            pe.wait_ge(S["x2t_ok"], b + 1)
            for k in range(KC):
                last = nc.tensor.matmul(bank(7)[:, P:P + RA], x2T[:, k, :], rat[:, k, :], start=(k == 0),
                                        stop=(k == KC - 1))
            last.then_inc(S["ra_mm"], 1)

        def pe_tail4(pe, b):
            pe.wait_ge(S["mg_ok"], b + 1)
            nc.tensor.transpose(bank(7)[:, 2 * P:3 * P], mg, ident[:, :]).then_inc(S["mgt_mm"], 1)
            pe.wait_ge(S["mgt_ok"], b + 1 + ONE)
            for h in range(2):
                last = nc.tensor.matmul(bank(2 + h), mgT, bful[:, h * HALF:(h + 1) * HALF], start=True,
                                        stop=True)
            last.then_inc(S["delta_mm"], 1)

        def act_softplus(act, g, q, tiles):
            s = NQ * g + q
            if tiles[0] == 0:
                act.wait_ge(S["dtu_ok"], s + ONE)
            for i in tiles:
                d = dt[q % 2][:, i, :]
                act.wait_ge(S["dt_mm"], 4 * s + i + 1)
                nc.scalar.activation(d, bank(4 + i % 2), ACT.Abs).then_inc(S["dt_abs"], 1)
                act.wait_ge(S["dt_abs"], 4 * s + i + 1)
                nc.scalar.activation(d, d, ACT.Exp, scale=-1.0).then_inc(S["dt_exp"], 1)
                act.wait_ge(S["dt_exp"], 4 * s + i + 1)
                nc.scalar.activation(d, d, ACT.Ln, bias=1.0).then_inc(S["dt_ln"], 1)

        def act_step(act, g, q):
            s = NQ * g + q
            for n in range(N):
                for i in range(QD):
                    e = 4 * (N * s + n) + i
                    if n == 0:
                        act.wait_ge(S["dt_ok"], 4 * s + i + 1)
                    act.wait_ge(S["scan_ok"], e - 1 + SCAN)
                    nc.scalar.activation(by_seq(bank(i % 2))[:, :, 1:SEQ],
                                         by_seq(dt[q % 2][:, i, :])[:, :, 1:SEQ], ACT.Exp,
                                         scale=a_sb[:, QD * q + i, n:n + 1]).then_inc(S["exp_ok"], 1)
                if n in (3, 5, 7, 9):
                    i = (n - 3) // 2
                    if i == 0:
                        act.wait_ge(S["fin"], 4 * s + FIN)
                    act.wait_ge(S["z_mm"], 4 * s + i + 1 + Z_MM)
                    nc.scalar.activation(zs[:, i, :], bank(6 + i % 2), ACT.Copy).then_inc(S["z_copied"], 1)
                if n == 10:
                    act.wait_ge(S["z_copied"], 4 * s + 4)
                    nc.scalar.activation(zs, zs, ACT.Silu).then_inc(S["z_silu"], 1)
                    act.preload_act_table_set(LN_EXP_SET)
                if q < NQ - 1 and n in (11, 13):
                    act_softplus(act, g, q + 1, (0, 1) if n == 11 else (2, 3))

        def act_keys1(act, b):
            for o in range(OT):
                act.wait_ge(S["k_neg"], 4 * b + o + 1)
                if o == 0:
                    act.wait_ge(S["et_mm"], 8 * b)
                    act.wait_ge(S["rk1"], b)
                nc.scalar.activation(ek[:, o, :], banks[o % 2][:, :], ACT.Exp, bias=nkm[:, o:o + 1],
                                     accum_out=ksum[:, o:o + 1]).then_inc(S["k_exp"], 1)

        def act_keys23(act, b):
            for t in range(0, NT, 2):
                act.wait_ge(S["et_mm"], 8 * b + t + 1)
                if t == 0:
                    act.wait_ge(S["g_mm"], b)
                nc.scalar.activation(ekT[:, t, :], bank(4), ACT.Copy).then_inc(S["et_act"], 1)
            act.wait_ge(S["g_mm"], b + 1)
            act.wait_ge(S["mt_mm"], b)
            nc.scalar.activation(gT, bank(6), ACT.Copy).then_inc(S["g_ok"], 1)

        def act_keys(act, b):
            act_keys1(act, b)
            act_keys23(act, b)

        def act_queries(act, b):
            for t in range(NT + 3):
                if t < NT:
                    act.wait_ge(S["q_sub"], 8 * b + t + 1)
                    nc.scalar.activation(qe[:, t, :], qe[:, t, :], ACT.Exp).then_inc(S["q_exp"], 1)
                if t >= 3 and (t - 3) % 2 == 0:
                    r = t - 3
                    act.wait_ge(S["qt_mm"], 8 * b + r + 1)
                    if r == 0:
                        act.wait_ge(S["out_mm"], 2 * b)
                    nc.scalar.activation(qs[:, :, r * P:(r + 1) * P],
                                         bank(4).rearrange("p (o n) -> p o n", o=OT), ACT.Copy)\
                        .then_inc(S["qs_act"], 1)

        def act_attend(act, b):
            act.wait_ge(S["out_mm"], 2 * b + 2)
            act.wait_ge(S["y2_ok"], b)
            nc.scalar.activation(ob, banks[1][:, :], ACT.Identity, bias=bov[:, 0:1])\
                .then_inc(S["ob_ok"], 1)
            act.wait_ge(S["ssq_mm"], b)
            nc.scalar.activation(sq, banks[1][:, :], ACT.Square, bias=bov[:, 0:1]).then_inc(S["sq_ok"], 1)

        def act_tail3(act, b):
            act.wait_ge(S["x2t_mm"], b + 1)
            nc.scalar.activation(x2T, banks[1][:, :].rearrange("p (k t) -> p k t", k=KC), ACT.Copy)\
                .then_inc(S["x2t_ok"], 1)
            act.wait_ge(S["lg_neg"], b + 1)
            nc.scalar.activation(lex[:, :], lg[:, :], ACT.Exp, bias=nlm[:, :]).then_inc(S["gate_exp"], 1)

        def act_tail4(act, b):
            act.wait_ge(S["mgt_mm"], b + 1)
            nc.scalar.activation(mgT, bank(7)[:, 2 * P:3 * P], ACT.Copy).then_inc(S["mgt_ok"], 1)

        def pool_rstd(pool, g):
            pool.wait_ge(S["ln_eps"], g + 1)
            nc.gpsimd.tensor_tensor(ve1[:, :], ve1[:, :], mhalf[:, 0:GB], ALU.pow).then_inc(S["ln_rstd"], 1)

        def pool_queries(pool, b):
            for t in range(NT):
                pool.wait_ge(S["q_rec"], 8 * b + t + 1)
                v = qe[:, t, :].rearrange("p (h d) -> p h d", h=HEADS)
                nc.gpsimd.tensor_tensor(v, v, qr[:, t % 2, :][:, :, None].broadcast_to([P, HEADS, DH]),
                                        ALU.mult).then_inc(S["q_norm"], 1)

        def pool_tail12(pool, b):
            pool.wait_ge(S["ssq_max"], b + 1)
            nc.gpsimd.tensor_tensor(rn[:, :], rn[:, :], mhalf[:, 0:NT], ALU.pow).then_inc(S["ssq_pow"], 1)
            pool.wait_ge(S["ssq_pow"], b + 1)
            pool.wait_ge(S["bc_mm"], b + ONE)
            nc.gpsimd.tensor_tensor(dg, ident[:, :][:, None, :].broadcast_to([P, NT, P]),
                                    rn[:, :][:, :, None].broadcast_to([P, NT, P]), ALU.mult)\
                .then_inc(S["dg_ok"], 1)
            pool.wait_ge(S["l2_eps"], 2 * b + 1)
            nc.gpsimd.tensor_tensor(ve1[:, 0:1], ve1[:, 0:1], mhalf[:, 0:1], ALU.pow)\
                .then_inc(S["l2_rstd"], 1)

        def pool_tail4(pool, b):
            pool.wait_ge(S["l2_eps"], 2 * b + 2)
            nc.gpsimd.tensor_tensor(ve1[:, 0:1], ve1[:, 0:1], mhalf[:, 0:1], ALU.pow)\
                .then_inc(S["l2_rstd"], 1)

        def dve_dt(dve, g, q, tiles):
            s = NQ * g + q
            for i in tiles:
                d = dt[q % 2][:, i, :]
                dve.wait_ge(S["dt_ln"], 4 * s + i + 1)
                nc.vector.scalar_tensor_tensor(d, bank(4 + i % 2), 0.0, d, ALU.max, ALU.add)\
                    .then_inc(S["dt_ok"], 1)

        def dve_scan(dve, g, q, n, i):
            U = N * (NQ * g + q) + n
            if i == 0:
                dve.wait_ge(S["bm_ok"], U + 1 + BM)
            dve.wait_ge(S["exp_ok"], 4 * U + i + 1)
            h = hb[n % 4][:, i * GT:(i + 1) * GT]
            nc.vector.tensor_tensor_scan(h, bank(i % 2), h, 0.0, ALU.mult, ALU.add)\
                .then_inc(S["scan_ok"], 1)

        def dve_acc(dve, g, q, n, b):
            s = NQ * g + q
            k = 4 * (N * s + n) + b
            dve.wait_ge(S["t_done"], k + 1 + T_DONE)
            c = cg[:, b, n:n + 1]
            if n == 0:
                if b == 0:
                    dve.wait_ge(S["yt_mm"], 4 * s + ONE)
                    dve.wait_ge(S["cg_ok"], g + 1)
                last = nc.vector.tensor_scalar(acc[:, b, :], bank(2 + b % 2), c, None, ALU.mult)
            else:
                dve.wait_ge(S["acc_ok"], k - 3 + ACCD)
                last = nc.vector.scalar_tensor_tensor(acc[:, b, :], bank(2 + b % 2), c, acc[:, b, :],
                                                      ALU.mult, ALU.add)
            last.then_inc(S["acc_ok"], 1)

        def dve_out(dve, s, c):
            v = rbuf[:, c // 2, (c % 2) * HALF:(c % 2 + 1) * HALF]
            dve.wait_ge(S["o_mm"], 8 * s + c + 1 + ONE)
            dve.wait_ge(S["r_added"], 8 * s + R_ADD)
            nc.vector.tensor_tensor(v, bank(6 + c % 2), v, ALU.add).then_inc(S["r_added"], 1)

        def dve_ln_stats(dve, g):
            dve.wait_ge(S["r_added"], 8 * (NQ * g + 1) + R_ADD)
            for t in range(GB):
                for h in range(2):
                    nc.vector.bn_stats(st1[:, t, h, :], rbuf[:, t, h * HALF:(h + 1) * HALF])\
                        .then_inc(S["ln_stats"], 1)
            dve.wait_ge(S["ln_stats"], 8 * g + 8)
            nc.vector.memset(idle[:, :], 0.0)
            for t in range(GB):
                nc.vector.bn_aggr(mv1[:, t, :], st1[:, t, :, :].rearrange("p a s -> p (a s)"))\
                    .then_inc(S["ln_aggr"], 1)
            dve.wait_ge(S["ln_aggr"], 4 * g + 4)
            nc.vector.tensor_scalar(ve1[:, :], mv1[:, :, 1:2].rearrange("p a b -> p (a b)"), LN_EPS, None,
                                    ALU.add).then_inc(S["ln_eps"], 1)

        def dve_ln_apply(dve, g):
            dve.wait_ge(S["ln_rstd"], g + 1)
            for t in range(GB):
                nc.vector.tensor_scalar(rbuf[:, t, :], rbuf[:, t, :], mv1[:, t, 0:1], ve1[:, t:t + 1],
                                        ALU.subtract, ALU.mult).then_inc(S["ln_ok"], 1)

        def dve_step(dve, g, q):
            s = NQ * g + q
            for n in range(N):
                ahead = q * N + n + 2
                scans = [(ahead // N, ahead % N, i) for i in range(QD)] if ahead < NQ * N else []
                if q == 1 and n == 8:
                    dve.wait_ge(S["r_loaded"], 16 * g + 16)
                for part in range(2):
                    dve_acc(dve, g, q, n, 2 * part)
                    dve_acc(dve, g, q, n, 2 * part + 1)
                    for qq, nn, i in scans[2 * part:2 * part + 2]:
                        dve_scan(dve, g, qq, nn, i)
                if n >= 8:
                    dve_out(dve, s, n - 8)
                if q < NQ - 1 and n in (10, 12):
                    dve_dt(dve, g, q + 1, (0, 1) if n == 10 else (2, 3))
                if q == 1 and n == 1:
                    dve_ln_stats(dve, g)
                if q == 1 and n == 3:
                    dve_ln_apply(dve, g)
            dve.wait_ge(S["o_mm"], 8 * s + 8 + ONE)
            dve.wait_ge(S["z_silu"], s + 1)

            def skip(i):
                dve.wait_ge(S["yt_mm"], 4 * s + i + 1 + ONE)
                nc.vector.scalar_tensor_tensor(yq[:, i, :], uq[q % 2][:, i, :],
                                               dsk[:, QD * q + i:QD * q + i + 1], bank(4 + i % 2),
                                               ALU.mult, ALU.add).then_inc(S["fin1"], 1)

            skip(0)
            for i in range(QD):
                if i < QD - 1:
                    skip(i + 1)
                dve.wait_ge(S["fin1"], 4 * s + i + 1 + FIN1)
                nc.vector.tensor_tensor(yq[:, i, :], yq[:, i, :], zs[:, i, :], ALU.mult)\
                    .then_inc(S["fin"], 1)

        def dve_keys1(dve, b):
            for o in range(OT):
                dve.wait_ge(S["k_mm"], 4 * b + o + 1)
                nc.vector.tensor_reduce(km[:, o:o + 1], banks[o % 2][:, :], AX_X, ALU.max)\
                    .then_inc(S["k_max"], 1)
                dve.wait_ge(S["k_max"], 4 * b + o + 1)
                if o == 0:
                    dve.wait_ge(S["k_exp"], 4 * b)
                nc.vector.tensor_scalar(nkm[:, o:o + 1], km[:, o:o + 1], -1.0, None, ALU.mult)\
                    .then_inc(S["k_neg"], 1)

        def dve_keys2(dve, b):
            for t in range(1, NT, 2):
                dve.wait_ge(S["et_mm"], 8 * b + t + 1)
                if t == 1:
                    dve.wait_ge(S["g_mm"], b)
                nc.vector.tensor_copy(ekT[:, t, :], bank(5)).then_inc(S["et_dve"], 1)

        def dve_keys4(dve, b):
            dve.wait_ge(S["k_exp"], 4 * b + 4)
            nc.vector.reciprocal(rk[:, :], ksum[:, :]).then_inc(S["rk1"], 1)
            dve.wait_ge(S["rk1"], b + 1)
            nc.vector.tensor_scalar(rk[:, :], rk[:, :], DH ** -0.5, None, ALU.mult).then_inc(S["rk2"], 1)
            dve.wait_ge(S["rk2"], b + 1)
            dve.wait_ge(S["mt_mm"], b + 1)
            dve.wait_ge(S["out_mm"], 2 * b)
            ps = banks[0][:, :].rearrange("p (o a c) -> p o a c", o=OT, a=2)
            for a_ in range(2):
                rows = slice(DH * a_, DH * (a_ + 1))
                nc.vector.tensor_tensor(mt[rows], ps[rows, :, a_, :],
                                        rk[rows, :][:, :, None].broadcast_to([DH, OT, P]), ALU.mult)\
                    .then_inc(S["mt_ok"], 1)

        def dve_keys24(dve, b):
            dve_keys2(dve, b)
            dve_keys4(dve, b)

        def dve_queries(dve, b):
            def start(t):
                ps = bank(t % 2).rearrange("p (h d) -> p h d", h=HEADS)
                dve.wait_ge(S["q_mm"], 8 * b + t + 1)
                nc.vector.tensor_reduce(qm[:, t % 2, :], ps, AX_X, ALU.max).then_inc(S["q_max"], 1)
                dve.wait_ge(S["q_max"], 8 * b + t + 1)
                if t == 0:
                    dve.wait_ge(S["qt_mm"], 8 * b)
                nc.vector.tensor_tensor(qe[:, t, :].rearrange("p (h d) -> p h d", h=HEADS), ps,
                                        qm[:, t % 2, :][:, :, None].broadcast_to([P, HEADS, DH]),
                                        ALU.subtract).then_inc(S["q_sub"], 1)

            def denominator(t):
                dve.wait_ge(S["q_exp"], 8 * b + t + 1)
                nc.vector.tensor_reduce(qz[:, t % 2, :], qe[:, t, :].rearrange("p (h d) -> p h d", h=HEADS),
                                        AX_X, ALU.add).then_inc(S["q_sum"], 1)
                dve.wait_ge(S["q_sum"], 8 * b + t + 1)
                if t >= 2:
                    dve.wait_ge(S["q_norm"], 8 * b + t - 1)
                nc.vector.reciprocal(qr[:, t % 2, :], qz[:, t % 2, :]).then_inc(S["q_rec"], 1)

            for t in range(NT + 3):
                if t < NT:
                    start(t)
                if 1 <= t <= NT:
                    denominator(t - 1)
                if t >= 3 and (t - 3) % 2 == 1:
                    r = t - 3
                    dve.wait_ge(S["qt_mm"], 8 * b + r + 1)
                    if r == 1:
                        dve.wait_ge(S["out_mm"], 2 * b)
                    nc.vector.tensor_copy(qs[:, :, r * P:(r + 1) * P],
                                          bank(5).rearrange("p (o n) -> p o n", o=OT))\
                        .then_inc(S["qs_dve"], 1)

        def dve_tail1(dve, b):
            dve.wait_ge(S["ssq_mm"], b + 1)
            dve.wait_ge(S["dg_ok"], b + ONE)
            nc.vector.tensor_scalar(rn[:, :], bank(7)[:, 0:NT], 1e-24, None, ALU.max)\
                .then_inc(S["ssq_max"], 1)

        def dve_norm(dve, b, k, src, dst, done):
            for h in range(2):
                nc.vector.bn_stats(st1[:, 0, h, :], src[:, h * HALF:(h + 1) * HALF])\
                    .then_inc(S["l2_stats"], 1)
            dve.wait_ge(S["l2_stats"], 4 * b + 2 * k + 2)
            nc.vector.memset(idle[:, :], 0.0)
            nc.vector.bn_aggr(mv1[:, 0, :], st1[:, 0, :, :].rearrange("p a s -> p (a s)"))\
                .then_inc(S["l2_aggr"], 1)
            dve.wait_ge(S["l2_aggr"], 2 * b + k + 1)
            nc.vector.tensor_scalar(ve1[:, 0:1], mv1[:, 0, 1:2], LN_EPS, None, ALU.add)\
                .then_inc(S["l2_eps"], 1)
            dve.wait_ge(S["l2_rstd"], 2 * b + k + 1)
            nc.vector.tensor_scalar(dst, src, mv1[:, 0, 0:1], ve1[:, 0:1], ALU.subtract, ALU.mult)\
                .then_inc(S[done], 1)

        def dve_tail2(dve, b):
            dve.wait_ge(S["bc_mm"], b + 1 + ONE)
            dve.wait_ge(S["ob_ok"], b + 1)
            dve.wait_ge(S["gs_ok"], 1)
            nc.vector.scalar_tensor_tensor(ob, ob, gs[:, 0:1], banks[1][:, :], ALU.mult, ALU.mult)\
                .then_inc(S["y2a"], 1)
            dve.wait_ge(S["y2a"], b + 1)
            dve.wait_ge(S["xres_loaded"], 16 * b + 16)
            dve.wait_ge(S["x3_add"], b + ONE)
            nc.vector.tensor_tensor(x2, ob, xres, ALU.add).then_inc(S["y2_ok"], 1)
            dve.wait_ge(S["y2_ok"], b + 1)
            dve_norm(dve, b, 0, x2, x2, "x2_ok")

        def dve_tail3(dve, b):
            step = [0]

            def small(ins):
                step[0] += 1
                ins.then_inc(S["gate_step"], 1)
                dve.wait_ge(S["gate_step"], GATE_STEPS * b + step[0])

            ra = bank(7)[:, P:P + RA]
            of_j = lg[:, :][:, None, :].broadcast_to([P, NE, NE])
            of_e = lg[:, :][:, :, None].broadcast_to([P, NE, NE])
            dve.wait_ge(S["ra_mm"], b + 1)
            small(nc.vector.tensor_copy(lg[:, :], ra[:, 0:NE]))
            small(nc.vector.tensor_reduce(nlm[:, :], lg[:, :], AX_X, ALU.max))
            nc.vector.tensor_scalar(nlm[:, :], nlm[:, :], -1.0, None, ALU.mult).then_inc(S["lg_neg"], 1)
            small(nc.vector.tensor_tensor(cgt[:, :, :], of_j, of_e, ALU.is_gt))
            small(nc.vector.tensor_tensor(cge[:, :, :], of_j, of_e, ALU.is_ge))
            small(nc.vector.tensor_tensor(cgt[:, :, :], cgt[:, :, :], upper[:, :, :], ALU.mult))
            small(nc.vector.tensor_tensor(cge[:, :, :], cge[:, :, :], lower[:, :, :], ALU.mult))
            small(nc.vector.tensor_tensor(cgt[:, :, :], cgt[:, :, :], cge[:, :, :], ALU.add))
            small(nc.vector.tensor_reduce(rank[:, :], cgt[:, :, :], AX_X, ALU.add))
            dve.wait_ge(S["gate_exp"], b + 1)
            small(nc.vector.scalar_tensor_tensor(gate[:, :], rank[:, :], 2.0, lex[:, :], ALU.is_lt, ALU.mult))
            small(nc.vector.tensor_reduce(gsum[:, :], gate[:, :], AX_X, ALU.add))
            small(nc.vector.reciprocal(gsum[:, :], gsum[:, :]))
            small(nc.vector.tensor_scalar(gate[:, :], gate[:, :], gsum[:, :], 4.0, ALU.mult, ALU.mult))
            nc.vector.tensor_tensor(mg[:, 0:NE * ER].rearrange("p (e r) -> p e r", e=NE),
                                    ra[:, NE:RA].rearrange("p (e r) -> p e r", e=NE),
                                    gate[:, :][:, :, None].broadcast_to([P, NE, ER]), ALU.mult)\
                .then_inc(S["mg_ok"], 1)
            assert step[0] == GATE_STEPS

        def dve_tail4(dve, b):
            dve.wait_ge(S["delta_mm"], b + 1)
            dve.wait_ge(S["out_stored"], 16 * b + ONE)
            nc.vector.tensor_tensor(x3, banks[1][:, :], x2, ALU.add).then_inc(S["x3_add"], 1)
            dve.wait_ge(S["x3_add"], b + 1 + ONE)
            dve_norm(dve, b, 1, x3, x3, "x3_ok")

        block = ctx.enter_context(nc.Block())

        @block.sync
        def _(sp):
            for name in ("out_stored", "u_stored0", "u_stored1"):
                sp.sem_inc(S[name], ONE)
            for dst, name in consts0:
                sp.dma_start(dst, a[name]).then_inc(S["const_loaded"], 16)
            sp.wait_ge(S["rows_set"], 1)
            sp.dma_start(wdt[96:97, :], a["b_dt"]).then_inc(S["bdt_loaded"], 16)
            with nc.sync.Fori(0, DT // 2) as mp:
                for par in range(2):
                    m = 2 * mp + par
                    sp.wait_ge(S["x_mm"], 4 * m - 4 + X_MM)
                    sp.wait_ge(S["conv_done"], 4 * m - 4 + CONV)
                    sp.dma_start(wxc[par], a["WinX"][bass.ds(m, 1)].rearrange("a p k -> (a p) k"))\
                        .then_inc(S[f"wx_loaded{par}"], 16)
                for par in range(2):
                    m = 2 * mp + par
                    sp.wait_ge(S["u_done"], 4 * m + 4)
                    sp.dma_start(u_d[bass.ds(m, 1)].rearrange("a p t -> (a p) t"), ust[par])\
                        .then_inc(S[f"u_stored{par}"], 16)
            sp.wait_ge(S["bt_rows"], TT // 4)
            sp.dma_start(b_d[:, :], tsb[R:R + N, :]).then_inc(S["b_stored"], 16)

            sp.wait_ge(S["b_stored"], 16)
            sp.wait_ge(S["u_stored0"], 8 * 16 + ONE)
            sp.wait_ge(S["u_stored1"], 8 * 16 + ONE)
            sp.wait_ge(S["phase0_c"], 1)
            sp.wait_ge(S["bt_mm"], TT // 4)
            with nc.sync.Fori(0, NG) as g:
                for q in range(NQ):
                    sync_step(sp, g, q)
            sp.wait_ge(S["o_mm"], 8 * NG * NQ + ONE)
            sp.dma_start(wo, a["WoutT"][NQ - 1]).then_inc(S["wo_loaded"], 16)
            sp.wait_ge(S["ln_ok"], GB * (NG + 1))
            sp.dma_start(x1_d[NG].rearrange("b p h -> p b h"), rbuf[:, :, :]).then_inc(S["x1_stored"], 16)

            sp.wait_ge(S["x1_stored"], 16 * (NG + 1))
            sp.wait_ge(S["o_mm"], 8 * (NG * NQ + 1) + ONE)
            for dst, name in consts2:
                sp.dma_start(dst, a[name]).then_inc(S["p2_const"], 16)
            for b in range(2):
                sync_seq(sp, b)
            with nc.sync.Fori(2, BATCH) as b:
                sync_seq(sp, b, store=b - 2)
            sync_store(sp, BATCH - 2)
            sync_store(sp, BATCH - 1)
            sp.wait_ge(S["out_stored"], 16 * BATCH + ONE)

        @block.tensor
        def _(pe):
            pe.sem_inc(S["x_mm"], X_MM)
            for name in ("ss_mm", "o_mm", "yt_mm", "bc_mm"):
                pe.sem_inc(S[name], ONE)
            pe.sem_inc(S["t_done"], T_DONE)
            pe.sem_inc(S["z_mm"], Z_MM)
            pe.wait_ge(S["const_loaded"], C0)
            pe.wait_ge(S["pool_const"], 1)
            with nc.tensor.Fori(0, DT // 2) as mp:
                for par in range(2):
                    m = 2 * mp + par
                    pe.wait_ge(S[f"wx_loaded{par}"], 16 * mp + 16)
                    for tg in range(NG):
                        pe.wait_ge(S["conv_done"], 4 * m + tg - 3 + CONV)
                        for k in range(KC):
                            last = nc.tensor.matmul(bank(tg), wx[par][:, k, :],
                                                    xT[:, k, tg * GT:(tg + 1) * GT],
                                                    start=(k == 0), stop=(k == KC - 1))
                        last.then_inc(S["x_mm"], 1)
                for par in range(2):
                    m = 2 * mp + par
                    for j in range(4):
                        pe.wait_ge(S["u_done"], 4 * m + j + 1)
                        pe.wait_ge(S["ss_added"], 4 * m + j + 1)
                        for i in range(4):
                            t = 4 * j + i
                            last = nc.tensor.matmul(bank(4 + j)[:, i * SS:(i + 1) * SS],
                                                    ust[par][:, t * P:(t + 1) * P],
                                                    wxT[:, bass.ds(m, 1), :].rearrange("p a s -> p (a s)"),
                                                    start=True, stop=True)
                        last.then_inc(S["ss_mm"], 1)
            pe.wait_ge(S["ss_normed"], 3)
            for j in range(TT // 4):
                for i in range(4):
                    last = nc.tensor.transpose(bank(j)[0:SS, i * P:(i + 1) * P], ssacc[:, 4 * j + i, :],
                                               ident[:, :])
                last.then_inc(S["bt_mm"], 1)

            pe.wait_ge(S["bt_rows"], TT // 4)
            pe.wait_ge(S["bdt_loaded"], 16)
            pe.wait_ge(S["rows_set"], 2)
            with nc.tensor.Fori(0, NG) as g:
                for i in range(QD):
                    if i < 2:
                        pe.wait_ge(S["fin1"], 16 * g + i - 1 + FIN1)
                    else:
                        pe.wait_ge(S["dt_ok"], 16 * g + i - 1)
                    pe_dt(pe, g, 0, i)
                for q in range(NQ):
                    pe_step(pe, g, q)
            pe.wait_ge(S["fin"], 4 * NG * NQ + FIN)
            pe.wait_ge(S["wo_loaded"], 16 * (NG * NQ + 1))
            for c in range(8):
                pe_out(pe, NG * NQ, c, range(4), last_quad=True)

            pe.wait_ge(S["p2_const"], C2)
            pe.wait_ge(S["rows_set"], 4)
            pe.wait_ge(S["r_added"], 8 * (NG * NQ + 1) + R_ADD)
            for h in range(HEADS):
                last = nc.tensor.matmul(bank(h // 4)[:, (h % 4) * P:(h % 4 + 1) * P], wvh[0:DH, h, :],
                                        woh[0:DH, h, :], start=True, stop=True)
            last.then_inc(S["ph_mm"], 1)
            pe.wait_ge(S["ph_ok"], 1)
            pe_keys1(pe, 0)
            pe_keys2(pe, 0)
            pe_keys3(pe, 0)
            pe_keys4(pe, 0)
            pe_queries(pe, 0)
            pe_attend(pe, 0)
            with nc.tensor.Fori(1, BATCH) as b:
                pe_keys1(pe, b)
                pe_tail1(pe, b - 1)
                pe_keys2(pe, b)
                pe.wait_ge(S["k_exp"], 4 * b + 4)
                pe_tail2(pe, b - 1)
                pe_keys3(pe, b)
                pe_keys4(pe, b)
                pe_tail3(pe, b - 1)
                pe_queries(pe, b)
                pe_tail4(pe, b - 1)
                pe_attend(pe, b)
            for tail in (pe_tail1, pe_tail2, pe_tail3, pe_tail4):
                tail(pe, BATCH - 1)

        @block.scalar
        def _(act):
            for name in ("mgt_ok",):
                act.sem_inc(S[name], ONE)
            act.wait_ge(S["const_loaded"], C0)
            act.preload_act_table_set(LN_EXP_SET)
            nc.scalar.activation(a_sb[:, :, :], a_sb[:, :, :], ACT.Exp).then_inc(S["a_exp"], 1)
            act.preload_act_table_set(SILU_SET)
            with nc.scalar.Fori(0, DT // 2) as mp:
                for x in range(8):
                    par, tg = divmod(x, 4)
                    m = 2 * mp + par
                    count = 8 * mp + x + 1
                    act.wait_ge(S["x_mm"], count + X_MM)
                    nc.scalar.activation(cv[x % 2], bank(tg), ACT.Identity, bias=wxc[par][:, H + 4:H + 5],
                                         scale=wxc[par][:, H + 3:H + 4])\
                        .then_inc(S["conv_base"], 1)
                    if tg == 0:
                        act.wait_ge(S[f"u_stored{par}"], 16 * mp + ONE)
                        act.wait_ge(S["ss_mm"], 8 * mp + ONE)
                    act.wait_ge(S["conv_done"], count + CONV)
                    nc.scalar.activation(ust[par][:, tg * GT:(tg + 1) * GT], cv[x % 2], ACT.Silu)\
                        .then_inc(S["u_done"], 1)

            act.preload_act_table_set(LN_EXP_SET)
            act.wait_ge(S["da_zero"], 1)
            act.wait_ge(S["a_neg"], 1)
            with nc.scalar.Fori(0, NG) as g:
                act_softplus(act, g, 0, range(QD))
                for q in range(NQ):
                    act_step(act, g, q)

            act.wait_ge(S["p2_const"], C2)
            act_keys(act, 0)
            act_queries(act, 0)
            act_attend(act, 0)
            with nc.scalar.Fori(1, BATCH) as b:
                act_keys1(act, b)
                act_keys23(act, b)
                act_tail3(act, b - 1)
                act_queries(act, b)
                act_tail4(act, b - 1)
                act_attend(act, b)
            act_tail3(act, BATCH - 1)
            act_tail4(act, BATCH - 1)

        @block.gpsimd
        def _(pool):
            pool.sem_inc(S["bm_ok"], BM)
            for name in ("dtu_ok", "dg_ok"):
                pool.sem_inc(S[name], ONE)
            nc.gpsimd.memset(ident[:, :], 0.0)
            nc.gpsimd.memset(ones[:, :], 1.0)
            nc.gpsimd.memset(mhalf[:, :], -0.5)
            nc.gpsimd.memset(rbuf[:, :, :], 0.0)
            nc.gpsimd.memset(upper[:, :, :], 0.0)
            nc.gpsimd.memset(lower[:, :, :], 0.0).then_inc(S["phase0_zero"], 1)
            pool.wait_ge(S["phase0_zero"], 1)
            for e in range(NE):
                if e < NE - 1:
                    nc.gpsimd.memset(upper[:, e, e + 1:NE], 1.0)
                if e > 0:
                    nc.gpsimd.memset(lower[:, e, 0:e], 1.0)
            nc.gpsimd.affine_select(out=ident[:, :], in_=ident[:, :], compare_op=ALU.not_equal, fill=1.0,
                                    base=0, pattern=[[-1, P]], channel_multiplier=1)\
                .then_inc(S["pool_const"], 1)
            pool.wait_ge(S["ss_mean"], 2)
            flat3 = ss3[:, :, :].rearrange("p a t -> p (a t)")
            nc.gpsimd.tensor_tensor(flat3, flat3, mhalf[:, :], ALU.pow).then_inc(S["ss_rstd"], 1)

            nc.gpsimd.memset(yq, 0.0).then_inc(S["phase0_zero"], 1)
            with nc.gpsimd.Fori(0, NG) as g:
                for q in range(NQ):
                    s = NQ * g + q
                    pool.wait_ge(S["dt_ok"], 4 * s + 4)
                    pool.wait_ge(S[f"u_loaded{q % 2}"], 16 * (2 * g + q // 2 + 1))
                    pool.wait_ge(S["bm_ok"], N * s + BM)
                    nc.gpsimd.tensor_tensor(dtu, dt[q % 2], uq[q % 2], ALU.mult).then_inc(S["dtu_ok"], 1)
                    pool.wait_ge(S["dtu_ok"], s + 1 + ONE)
                    for n in range(N):
                        if q == 0 and n % 4 == 0:
                            pool.wait_ge(S[f"brep_loaded{n // 4}"], 16 * g + 16)
                        pool.wait_ge(S["t_done"], 4 * (N * s + n) - 12 + T_DONE)
                        nc.gpsimd.tensor_tensor(
                            hb[n % 4].rearrange("p (i t) -> p i t", i=QD), dtu,
                            brep[:, n:n + 1, :].broadcast_to([P, QD, GT]), ALU.mult)\
                            .then_inc(S["bm_ok"], 1)
                        if q == 1 and n == 4:
                            pool_rstd(pool, g)
            pool_rstd(pool, NG)

            pool.wait_ge(S["o_mm"], 8 * (NG * NQ + 1) + ONE)
            pool_queries(pool, 0)
            with nc.gpsimd.Fori(1, BATCH) as b:
                pool_tail12(pool, b - 1)
                pool_queries(pool, b)
                pool_tail4(pool, b - 1)
            pool_tail12(pool, BATCH - 1)
            pool_tail4(pool, BATCH - 1)

        @block.vector
        def _(dve):
            dve.sem_inc(S["conv_done"], CONV)
            for name in ("x3_add",):
                dve.sem_inc(S[name], ONE)
            dve.sem_inc(S["ss_added"], SS_ADD)
            dve.sem_inc(S["scan_ok"], SCAN)
            dve.sem_inc(S["acc_ok"], ACCD)
            dve.sem_inc(S["r_added"], R_ADD)
            dve.sem_inc(S["fin1"], FIN1)
            dve.sem_inc(S["fin"], FIN)
            nc.vector.memset(wdt[R:P, :], 0.0).then_inc(S["rows_set"], 1)
            nc.vector.memset(tsb[SS:P, :], 1.0).then_inc(S["rows_set"], 1)
            dve.wait_ge(S["const_loaded"], C0)
            dve.wait_ge(S["a_exp"], 1)
            nc.vector.tensor_scalar(a_sb[:, :, :], a_sb[:, :, :], -1.0, None, ALU.mult).then_inc(S["a_neg"], 1)
            nc.vector.memset(ssacc, 0.0).then_inc(S["ss_square"], 1)
            dve.wait_ge(S["ss_square"], 1)
            with nc.vector.Fori(0, DT // 2) as mp:
                for x in range(8):
                    par, tg = divmod(x, 4)
                    m = 2 * mp + par
                    count = 8 * mp + x
                    dve.wait_ge(S["conv_base"], count + 1)
                    c = by_seq(cv[x % 2])
                    for sh in range(1, 4):
                        if sh > 1:
                            dve.wait_ge(S["conv_tap"], 2 * count + sh - 1)
                        last = nc.vector.scalar_tensor_tensor(
                            c[:, :, sh:SEQ], by_seq(bank(tg))[:, :, 0:SEQ - sh],
                            wxc[par][:, H + 3 - sh:H + 4 - sh],
                            c[:, :, sh:SEQ], ALU.mult, ALU.add)
                        last.then_inc(S["conv_tap" if sh < 3 else "conv_done"], 1)
                for par in range(2):
                    m = 2 * mp + par
                    for j in range(4):
                        dve.wait_ge(S["ss_mm"], 4 * m + j + 1 + ONE)
                        dve.wait_ge(S["ss_added"], 4 * m + j + 1)
                        v = ssacc[:, 4 * j:4 * j + 4, :].rearrange("p a s -> p (a s)")
                        nc.vector.tensor_tensor(v, v, bank(4 + j)[:, 0:4 * SS], ALU.add)\
                            .then_inc(S["ss_added"], 1)
            dve.wait_ge(S["ss_added"], 4 * DT + SS_ADD)
            nc.vector.tensor_tensor(sssq, ssacc, ssacc, ALU.mult).then_inc(S["ss_square"], 1)
            dve.wait_ge(S["ss_square"], 2)
            parts = ((0, R), (R, R + N), (R + N, SS))
            for j, (lo, hi) in enumerate(parts):
                nc.vector.tensor_reduce(ss3[:, j, :], sssq[:, :, lo:hi], AX_X, ALU.add)\
                    .then_inc(S["ss_sum"], 1)
            dve.wait_ge(S["ss_sum"], 3)
            nc.vector.tensor_scalar(ss3[:, 0, :], ss3[:, 0, :], 1.0 / R, RMS_EPS, ALU.mult, ALU.add)\
                .then_inc(S["ss_mean"], 1)
            nc.vector.tensor_scalar(ss3[:, 1:3, :], ss3[:, 1:3, :], 1.0 / N, RMS_EPS, ALU.mult, ALU.add)\
                .then_inc(S["ss_mean"], 1)
            dve.wait_ge(S["ss_rstd"], 1)
            for j, (lo, hi) in enumerate(parts):
                v = ssacc[:, :, lo:hi]
                nc.vector.tensor_tensor(v, v, ss3[:, j, :][:, :, None].broadcast_to([P, TT, hi - lo]),
                                        ALU.mult).then_inc(S["ss_normed"], 1)
            dve.wait_ge(S["ss_normed"], 3)
            nc.vector.tensor_copy(cbt[:, :, :], ssacc[:, :, R + N:SS]).then_inc(S["phase0_c"], 1)
            dve.wait_ge(S["pool_const"], 1)
            for j in range(TT // 4):
                dve.wait_ge(S["bt_mm"], j + 1)
                nc.vector.tensor_copy(tsb[0:SS, j * HALF:(j + 1) * HALF], bank(j)[0:SS, :])\
                    .then_inc(S["bt_rows"], 1)

            dve.wait_ge(S["bt_rows"], TT // 4)
            for i in range(2):
                last = nc.vector.memset(by_seq(bank(i))[:, :, 0:1], 0.0)
            last.then_inc(S["da_zero"], 1)
            dve.wait_ge(S["phase0_c"], 1)
            dve.wait_ge(S["phase0_zero"], 2)
            with nc.vector.Fori(0, NG) as g:
                dve.wait_ge(S["acc_ok"], 64 * 4 * g + ACCD)
                nc.vector.tensor_copy(cg[:, :, :], cbt[:, bass.ds(GB * g, GB), :]).then_inc(S["cg_ok"], 1)
                dve_dt(dve, g, 0, range(QD))
                for i in range(2 * QD):
                    dve_scan(dve, g, 0, i // QD, i % QD)
                for q in range(NQ):
                    dve_step(dve, g, q)
            for c in range(8):
                dve_out(dve, NG * NQ, c)
            dve_ln_stats(dve, NG)
            dve_ln_apply(dve, NG)

            dve.wait_ge(S["p2_const"], C2)
            nc.vector.memset(bful[NE * ER:P, :], 0.0).then_inc(S["rows_set"], 1)
            nc.vector.memset(mg[:, NE * ER:P], 0.0).then_inc(S["rows_set"], 1)
            dve.wait_ge(S["ph_mm"], 1)
            nc.vector.tensor_copy(ph, banks[0][:, :].rearrange("p (h c) -> p h c", h=HEADS))\
                .then_inc(S["ph_ok"], 1)
            nc.vector.tensor_scalar(gs[:, :], bov[:, 1:2], float(np.sqrt(SEQ)), None, ALU.mult)\
                .then_inc(S["gs_ok"], 1)
            dve_keys1(dve, 0)
            dve_keys24(dve, 0)
            dve_queries(dve, 0)
            with nc.vector.Fori(1, BATCH) as b:
                dve_keys1(dve, b)
                dve_tail1(dve, b - 1)
                dve_keys2(dve, b)
                dve_tail2(dve, b - 1)
                dve_keys4(dve, b)
                dve_tail3(dve, b - 1)
                dve_queries(dve, b)
                dve_tail4(dve, b - 1)
            for tail in (dve_tail1, dve_tail2, dve_tail3, dve_tail4):
                tail(dve, BATCH - 1)


def _layouts(i):
    f = np.ascontiguousarray
    x = np.asarray(i["x"])
    ctx = np.asarray(i["ctx_4096"])
    tok = x.reshape(TOK, H)
    win = np.asarray(i["L0_attn_W_in"])
    tiles = win.reshape(2 * DT, P, KC, P).transpose(0, 3, 2, 1)
    taps = np.concatenate([np.asarray(i["L0_attn_conv_w"]), np.asarray(i["L0_attn_conv_b"])[:, None]],
                          axis=1).reshape(DT, P, 5)
    per_tile = lambda v: f(np.asarray(v).reshape(DT, P, -1).transpose(1, 0, 2))
    heads = lambda w: f(w.reshape(HEADS, DH, P).transpose(1, 0, 2))
    return {
        "xT": f(tok.T.reshape(KC, P, TOK).transpose(1, 0, 2)),
        "x": f(x.reshape(NG, GB, SEQ, H).transpose(0, 2, 1, 3)),
        "ctx": f(ctx),
        "ctxT": f(ctx.reshape(BATCH, SEQ, NT, P).transpose(0, 3, 2, 1)),
        "WinX": f(np.concatenate([tiles[:DT].reshape(DT, P, H), taps], axis=2)),
        "WinZ": f(tiles[DT:]),
        "WxT": f(np.asarray(i["L0_attn_W_x"]).reshape(SS, DT, P).transpose(2, 1, 0)),
        "WdtT": f(np.asarray(i["L0_attn_W_dt"]).T),
        "b_dt": f(np.asarray(i["L0_attn_b_dt"]).reshape(1, D_IN)),
        "A_log": per_tile(i["L0_attn_A_log"]),
        "D": per_tile(i["L0_attn_D"]).reshape(P, DT),
        "WoutT": f(np.asarray(i["L0_attn_W_out"]).T.reshape(NQ, QD, P, H).transpose(0, 2, 1, 3)),
        "WqT": f(np.asarray(i["L0_xattn_Wq"]).T),
        "WkT": f(np.asarray(i["L0_xattn_Wk"]).T),
        "Wvh": heads(np.asarray(i["L0_xattn_Wv"])),
        "Woh": heads(f(np.asarray(i["L0_xattn_Wo"]).T)),
        "bo": f(np.asarray(i["L0_xattn_bo"]).reshape(P, 1)),
        "g": f(np.asarray(i["L0_xattn_g"]).reshape(P, 1)),
        "RAT": f(np.concatenate([np.asarray(i["L0_ffn_router_w"]),
                                 np.asarray(i["L0_ffn_A"]).reshape(NE * ER, H)])
                 .T.reshape(KC, P, RA).transpose(1, 0, 2)),
        "Bf": f(np.asarray(i["L0_ffn_B"]).transpose(0, 2, 1).reshape(NE * ER, H)),
    }


def kernel(**inputs):
    import concourse.bacc as bacc
    from concourse.bass_utils import run_bass_kernel_spmd

    nc = bacc.Bacc("TRN2", target_bir_lowering=False, num_devices=1)
    arrays = {f"in_{k}": v for k, v in _layouts(inputs).items()}
    aps = {k[3:]: nc.dram_tensor(k, v.shape, mybir.dt.from_np(v.dtype), kind="ExternalInput").ap()
           for k, v in arrays.items()}
    out = nc.dram_tensor("out", (BATCH, SEQ, H), F32, kind="ExternalOutput").ap()
    program(nc, aps, out)
    r = run_bass_kernel_spmd(nc, [arrays], core_ids=[0])
    return r.results[0]["out"]
```

```python
from contextlib import ExitStack

import numpy as np

import concourse.bass as bass
from concourse import mybir

ALU = mybir.AluOpType
ACT = mybir.ActivationFunctionType
F32 = mybir.dt.float32
AX_X = mybir.AxisListType.X
LN_EXP_SET = "natural_log_exp_and_others"
SILU_SET = "silu_and_others"

P = 128
BATCH, SEQ, H = 16, 128, 1024
TOK = BATCH * SEQ
D_IN, N, R = 2048, 16, 64
DT = D_IN // P
KC = H // P
GB = 4
GT = GB * SEQ
NG = TOK // GT
QD = 4
NQ = DT // QD
TT = TOK // P
SS = R + 2 * N
HEADS, DH = 8, 64
HID = HEADS * DH
OT = HID // P
NT = H // P
NE, ER = 4, 16
RA = NE + NE * ER
HALF = 512
LN_EPS, RMS_EPS = 1e-5, 1e-6
GATE_STEPS = 12

X_MM, CONV, SS_ADD = 8, 8, 4
T_DONE, SCAN, ACCD, R_ADD, FIN1, FIN, Z_MM, BM = 13, 2, 2, 2, 2, 5, 2, 13
ONE = 1

SEMS = """const_loaded xt_loaded0 xt_loaded1 xt_loaded2 xt_loaded3 pool_const rows_set bdt_loaded a_exp a_neg x_mm conv_base conv_tap conv_done u_done
ss_mm ss_added ss_square ss_sum ss_mean ss_rstd ss_normed bt_mm bt_rows b_stored wx_loaded0 wx_loaded1 u_stored0 u_stored1
phase0_zero phase0_c da_zero xg_loaded wz_loaded0 wz_loaded1 wo_loaded u_loaded0 u_loaded1 r_loaded
brep_loaded0 brep_loaded1 brep_loaded2 brep_loaded3 dt_mm dt_abs dt_exp dt_ln dt_ok dtu_ok cg_ok exp_ok bm_ok
scan_ok t_done acc_ok yt_mm fin1 fin z_mm z_copied z_silu o_mm r_added ln_stats ln_aggr ln_eps ln_rstd
ln_ok x1_stored
p2_const ph_mm ph_ok gs_ok cn_loaded ct_loaded x1_loaded xres_loaded out_stored
k_mm k_max k_neg k_exp et_mm et_ok g_mm g_ok rk1 rk2 mt_mm mt_ok
q_mm q_max q_sub q_exp q_sum q_rec q_norm qt_mm qs_ok out_mm ob_ok sq_ok
ssq_mm ssq_max ssq_pow dg_ok bc_mm y2a y2_ok l2_stats l2_aggr l2_eps l2_rstd x2_ok x2t_mm x2t_ok
ra_mm gate_step lg_neg gate_exp mg_ok mgt_mm mgt_ok delta_mm x3_add x3_ok""".split()


def program(nc, a, out):
    u_d = nc.dram_tensor("u_scratch", (DT, P, TOK), F32, kind="Internal").ap()
    b_d = nc.dram_tensor("b_scratch", (N, TOK), F32, kind="Internal").ap()
    x1_d = nc.dram_tensor("x1_scratch", (NG + 1, GB, P, H), F32, kind="Internal").ap()

    with ExitStack() as ctx:
        def sb(name, shape):
            return ctx.enter_context(nc.sbuf_tensor(name, shape, F32))

        S = {name: ctx.enter_context(nc.semaphore(name)) for name in SEMS}

        arena = sb("arena", [P, 43008])

        def at(off, *dims):
            v = arena[:, off:off + int(np.prod(dims))]
            if len(dims) == 1:
                return v
            names = "abcd"[:len(dims)]
            return v.rearrange("p (%s) -> p %s" % (" ".join(names), " ".join(names)),
                               **dict(zip(names[1:], dims[1:])))

        xT = at(0, KC, TOK)
        wxc = [at(26624 + 1536 + 1040 * i, H + 5) for i in range(2)]
        wx = [v[:, 0:H].rearrange("p (k m) -> p k m", k=KC) for v in wxc]
        ust = [at(18432 + 2048 * i, TOK) for i in range(2)]
        cv = [at(22528 + GT * i, GT) for i in range(2)]
        wxT = at(23552, DT, SS)
        ssacc = at(25088, TT, SS)
        sssq = at(26624, TT, SS)
        brep = at(0, N, GT)
        hb = [at(8192 + 2048 * i, QD * GT) for i in range(4)]
        xg = at(16384, KC, GT)
        wz = [at(20480 + 1024 * i, KC, P) for i in range(2)]
        wo = at(22528, QD, H)
        uq = [at(26624 + 2048 * i, QD, GT) for i in range(2)]
        dt = [at(30720 + 2048 * i, QD, GT) for i in range(2)]
        dtu = at(34816, QD, GT)
        zs = at(36864, QD, GT)
        acc = at(38912, GB, QD * P)
        yq = at(40960, QD, GT)
        x1 = at(0, H)
        xres = at(1024, H)
        cn = at(2048, H)
        cT = at(3072, NT, P)
        ek = at(4096, OT, H)
        ekT = at(8192, NT, HID)
        gT = at(12288, HID)
        mt = at(12800, OT, P)
        qe = at(13312, NT, HID)
        qs = at(17408, OT, H)
        ob = at(21504, H)
        sq = at(22528, H)
        dg = at(23552, NT, P)
        x2 = at(24576, H)
        x2T = at(25600, KC, P)
        mg = at(26624, P)
        mgT = at(26752, P)
        x3 = at(26880, H)
        wq = at(27904, HID)
        wk = at(28416, HID)
        ph = at(28928, HEADS, P)
        wvh = at(29952, HEADS, P)
        woh = at(30976, HEADS, P)
        rat = at(32000, KC, RA)
        bful = at(32544, H)

        rbuf = sb("rbuf", [P, GB, H])
        wdt = sb("wdt", [P, D_IN])
        tsb = sb("tsb", [P, TOK])
        a_sb = sb("a_sb", [P, DT, N])
        cbt = sb("cbt", [P, TT, N])
        cg = sb("cg", [P, GB, N])
        dsk = sb("dsk", [P, DT])
        idle = sb("idle", [P, 1])
        ident = sb("ident", [P, P])
        ones = sb("ones", [P, P])
        mhalf = sb("mhalf", [P, 3 * TT])
        ss3 = sb("ss3", [P, 3, TT])
        st1 = sb("st1", [P, GB, 2, 6])
        mv1 = sb("mv1", [P, GB, 2])
        ve1 = sb("ve1", [P, GB])
        bov = sb("bov", [P, 2])
        gs = sb("gs", [P, 1])
        km = sb("km", [P, OT])
        nkm = sb("nkm", [P, OT])
        ksum = sb("ksum", [P, OT])
        rk = sb("rk", [P, OT])
        qm = sb("qm", [P, 2, HEADS])
        qz = sb("qz", [P, 2, HEADS])
        qr = sb("qr", [P, 2, HEADS])
        rn = sb("rn", [P, NT])
        lg = sb("lg", [P, NE])
        nlm = sb("nlm", [P, 1])
        lex = sb("lex", [P, NE])
        cgt = sb("cgt", [P, NE, NE])
        cge = sb("cge", [P, NE, NE])
        upper = sb("upper", [P, NE, NE])
        lower = sb("lower", [P, NE, NE])
        rank = sb("rank", [P, NE])
        gate = sb("gate", [P, NE])
        gsum = sb("gsum", [P, 1])

        banks = [ctx.enter_context(nc.psum_tensor(f"banks{i}", [P, 2 * HALF], F32)) for i in range(4)]

        def bank(i):
            return banks[i // 2][:, (i % 2) * HALF:(i % 2 + 1) * HALF]

        def following(g, q):
            return (g, q + 1) if q < NQ - 1 else (g + 1, 0)

        def by_seq(ap):
            return ap.rearrange("p (b t) -> p b t", b=GB)

        consts0 = [(wxT, "WxT"), (wdt[0:R, :], "WdtT"), (a_sb[:, :, :], "A_log"),
                   (dsk[:, :], "D")]
        consts2 = [(wq, "WqT"), (wk, "WkT"), (wvh[0:DH], "Wvh"), (woh[0:DH], "Woh"), (rat, "RAT"),
                   (bful[0:NE * ER, :], "Bf"), (bov[:, 0:1], "bo"), (bov[:, 1:2], "g")]
        C0, C2 = 16 * len(consts0), 16 * len(consts2)

        def sync_tile(sp, mp, par):
            m = 2 * mp + par
            sp.wait_ge(S["x_mm"], 4 * m - 4 + X_MM)
            sp.wait_ge(S["conv_done"], 4 * m - 4 + CONV)
            sp.dma_start(wxc[par], a["WinX"][bass.ds(m, 1)].rearrange("a p k -> (a p) k"))\
                .then_inc(S[f"wx_loaded{par}"], 16)

        def sync_store_u(sp, mp, par):
            m = 2 * mp + par
            sp.wait_ge(S["u_done"], 4 * m + 4)
            sp.dma_start(u_d[bass.ds(m, 1)].rearrange("a p t -> (a p) t"), ust[par])\
                .then_inc(S[f"u_stored{par}"], 16)

        def sync_step(sp, g, q):
            s = NQ * g + q
            sp.wait_ge(S["fin"], 4 * s - 4 + FIN)
            sp.dma_start(uq[q % 2], u_d[QD * q:QD * (q + 1), :, bass.ds(g * GT, GT)]
                         .rearrange("d p t -> p d t")).then_inc(S[f"u_loaded{q % 2}"], 16)
            if q == 0:
                sp.wait_ge(S["z_mm"], 16 * g + Z_MM)
                sp.dma_start(xg, a["xT"][:, :, bass.ds(g * GT, GT)]).then_inc(S["xg_loaded"], 16)

            def gate_weights(i):
                sp.wait_ge(S["z_mm"], 4 * s + i - 1 + Z_MM)
                sp.dma_start(wz[i % 2], a["WinZ"][QD * q + i]).then_inc(S[f"wz_loaded{i % 2}"], 16)

            gate_weights(0)
            gate_weights(1)
            if q == 0:
                for j in range(4):
                    sp.wait_ge(S["bm_ok"], 64 * g + 4 * j - 12 + BM)
                    sp.dma_start(brep[:, 4 * j:4 * j + 4, :],
                                 b_d[4 * j:4 * j + 4, bass.ds(g * GT, GT)].partition_broadcast(P))\
                        .then_inc(S[f"brep_loaded{j}"], 16)
            gate_weights(2)
            gate_weights(3)
            sp.wait_ge(S["o_mm"], 8 * s + ONE)
            sp.dma_start(wo, a["WoutT"][(q - 1) % NQ]).then_inc(S["wo_loaded"], 16)
            if q == 1:
                sp.wait_ge(S["ln_ok"], GB * (g + 1))
                sp.dma_start(x1_d[bass.ds(g, 1)].rearrange("a b p h -> p (a b) h"), rbuf[:, :, :])\
                    .then_inc(S["x1_stored"], 16)
                sp.wait_ge(S["x1_stored"], 16 * (g + 1))
                sp.dma_start(rbuf[:, :, :], a["x"][bass.ds(g, 1)].rearrange("a p b h -> (a p) b h"))\
                    .then_inc(S["r_loaded"], 16)

        def sync_store(sp, b):
            sp.wait_ge(S["x3_ok"], b + 1)
            sp.dma_start(out[bass.ds(b, 1)].rearrange("a p h -> (a p) h"), x3)\
                .then_inc(S["out_stored"], 16)

        def sync_context(sp, b):
            sp.wait_ge(S["k_mm"], 4 * b)
            sp.dma_start(cn, a["ctx"][bass.ds(b, 1)].rearrange("a p n -> (a p) n"))\
                .then_inc(S["cn_loaded"], 16)

        def sync_seq(sp, b, store=None, context=True):
            row = x1_d.rearrange("g b p h -> (g b) p h")[bass.ds(b + GB, 1)].rearrange("a p h -> (a p) h")
            sp.wait_ge(S["q_mm"], 8 * b)
            sp.dma_start(x1, row).then_inc(S["x1_loaded"], 16)
            sp.wait_ge(S["g_mm"], b)
            sp.dma_start(cT, a["ctxT"][bass.ds(b, 1)].rearrange("a p n c -> (a p) n c"))\
                .then_inc(S["ct_loaded"], 16)
            if store is not None:
                sync_store(sp, store)
            if context:
                sync_context(sp, b + 1)
            sp.wait_ge(S["y2_ok"], b)
            sp.dma_start(xres, row).then_inc(S["xres_loaded"], 16)

        def pe_dt(pe, g, q, i):
            d = QD * q + i
            nc.tensor.matmul(bank(4 + i % 2), wdt[:, d * P:(d + 1) * P], tsb[:, bass.ds(g * GT, GT)],
                             start=True, stop=True).then_inc(S["dt_mm"], 1)

        def pe_out(pe, s, c, ks, last_quad=False):
            for k in ks:
                if k == 0:
                    if last_quad or c >= 2:
                        pe.wait_ge(S["r_added"], 8 * s + c - 1 + R_ADD)
                    if c < 2:
                        pe.wait_ge(S["z_copied"], 4 * s if last_quad else 4 * s + 3 + c)
                last = nc.tensor.matmul(bank(6 + c % 2), yq[:, k, (c // 2) * P:(c // 2 + 1) * P],
                                        wo[:, k, (c % 2) * HALF:(c % 2 + 1) * HALF],
                                        start=(k == 0), stop=(k == QD - 1))
                if k == QD - 1:
                    last.then_inc(S["o_mm"], 1)

        def pe_step(pe, g, q, last=False):
            s = NQ * g + q
            if q == 0:
                pe.wait_ge(S["xg_loaded"], 16 * g + 16)
            for n in range(N):
                U = N * s + n

                def turn(b):
                    pe.wait_ge(S["acc_ok"], 4 * U + b - 1 + ACCD)
                    for i in range(QD):
                        last = nc.tensor.transpose(bank(2 + b % 2)[:, i * P:(i + 1) * P],
                                                   hb[n % 4][:, i * GT + b * P:i * GT + (b + 1) * P],
                                                   ident[:, :])
                    last.then_inc(S["t_done"], 1)

                def filler(part):
                    if n < 8:
                        i = n // 2
                        if n % 2 == 0 and part == 0:
                            pe.wait_ge(S[f"wz_loaded{i % 2}"], 16 * (2 * s + i // 2 + 1))
                            if i < 2:
                                pe.wait_ge(S["r_added"], 8 * s + i - 1 + R_ADD)
                            else:
                                pe.wait_ge(S["z_copied"], 4 * s + i - 1)
                        for k in range(4 * (n % 2) + 2 * part, 4 * (n % 2) + 2 * part + 2):
                            last = nc.tensor.matmul(bank(6 + i % 2), wz[i % 2][:, k, :], xg[:, k, :],
                                                    start=(k == 0), stop=(k == KC - 1))
                        if k == KC - 1:
                            last.then_inc(S["z_mm"], 1)
                    else:
                        if n == 8 and part == 0:
                            pe.wait_ge(S["wo_loaded"], 16 * s + 16)
                        pe_out(pe, s, n - 8, range(2 * part, 2 * part + 2))

                pe.wait_ge(S["scan_ok"], 4 * U + 4 + SCAN)
                turn(0)
                turn(1)
                filler(0)
                turn(2)
                turn(3)
                filler(1)
                if not last and n in (7, 11):
                    for i in ((0, 1) if n == 7 else (2, 3)):
                        if i >= 2:
                            pe.wait_ge(S["dt_ok"], 4 * (s + 1) + i - 1)
                        else:
                            pe.wait_ge(S["fin1"], 4 * s + i - 1 + FIN1)
                        pe_dt(pe, *following(g, q), i)
            pe.wait_ge(S["acc_ok"], 4 * (N * s + N) + ACCD)
            for i in range(QD):
                if i < 2 and not last:
                    pe.wait_ge(S["dt_ok"], 4 * (s + 1) + 3 + i)
                else:
                    pe.wait_ge(S["fin1"], 4 * s + i - 1 + FIN1)
                for b in range(GB):
                    last = nc.tensor.transpose(bank(4 + i % 2)[:, b * P:(b + 1) * P],
                                               acc[:, b, i * P:(i + 1) * P], ident[:, :])
                last.then_inc(S["yt_mm"], 1)

        def pe_keys(pe, b, o):
            if o == 0:
                pe.wait_ge(S["cn_loaded"], 16 * b + 16)
            else:
                pe.wait_ge(S["k_exp"], 4 * b + o)
            for h in range(2):
                last = nc.tensor.matmul(bank(2 + h), wk[:, o * P:(o + 1) * P],
                                        cn[:, h * HALF:(h + 1) * HALF], start=True, stop=True)
            last.then_inc(S["k_mm"], 1)

        def pe_keys_turn(pe, b, t):
            if t == 0:
                pe.wait_ge(S["k_exp"], 4 * b + 4)
            pe.wait_ge(S["et_ok"], 8 * b + t)
            for o in range(OT):
                last = nc.tensor.transpose(bank(5)[:, o * P:(o + 1) * P], ek[:, o, t * P:(t + 1) * P],
                                           ident[:, :])
            last.then_inc(S["et_mm"], 1)

        def pe_context(pe, b, ts):
            if ts[0] == 0:
                pe.wait_ge(S["ct_loaded"], 16 * b + 16)
                pe.wait_ge(S["et_ok"], 8 * b + 8)
                pe.wait_ge(S["mt_ok"], b)
            for t in ts:
                last = nc.tensor.matmul(bank(6), cT[:, t, :], ekT[:, t, :], start=(t == 0),
                                        stop=(t == NT - 1))
            if ts[-1] == NT - 1:
                last.then_inc(S["g_mm"], 1)

        def pe_values(pe, b):
            pe.wait_ge(S["g_ok"], b + 1)
            for h in range(HEADS):
                rows = slice(DH * (h % 2), DH * (h % 2 + 1))
                last = nc.tensor.matmul(bank(6)[rows, (h // 2) * P:(h // 2 + 1) * P],
                                        gT[:, h * DH:(h + 1) * DH], ph[:, h, :], start=True, stop=True)
            last.then_inc(S["mt_mm"], 1)

        def pe_sequence(pe, b, keys, tail):
            pe.wait_ge(S["x1_loaded"], 16 * b + 16)
            for t in range(NT + 3):
                if t < NT:
                    if t < 2:
                        pe.wait_ge(S["q_sub"], 8 * b)
                        pe.wait_ge(S["x3_add"], b - 1 + ONE)
                    else:
                        pe.wait_ge(S["q_sub"], 8 * b + t - 1)
                    nc.tensor.matmul(bank(t % 2), x1[:, t * P:(t + 1) * P], wq, start=True, stop=True)\
                        .then_inc(S["q_mm"], 1)
                if t < 4:
                    pe_keys_turn(pe, b, 2 * t)
                    pe_keys_turn(pe, b, 2 * t + 1)
                if tail and t in PE_TAIL:
                    PE_TAIL[t](pe, b - 1)
                if keys and 4 <= t < 8:
                    if t == 4:
                        pe.wait_ge(S["ob_ok"], b)
                        pe.wait_ge(S["sq_ok"], b)
                        if tail:
                            pe.wait_ge(S["x2t_ok"], b)
                    pe_keys(pe, b + 1, t - 4)
                if 5 <= t < 9:
                    pe_context(pe, b, (2 * t - 10, 2 * t - 9))
                if t >= 3:
                    r = t - 3
                    pe.wait_ge(S["q_norm"], 8 * b + r + 1)
                    pe.wait_ge(S["qs_ok"], 8 * b + r)
                    for o in range(OT):
                        last = nc.tensor.transpose(bank(4)[:, o * P:(o + 1) * P],
                                                   qe[:, r, o * P:(o + 1) * P], ident[:, :])
                    last.then_inc(S["qt_mm"], 1)
                if tail and t == 9:
                    pe_tail5(pe, b - 1, 8 * b + 8)
                if t == 9:
                    pe_values(pe, b)
            pe.wait_ge(S["mt_ok"], b + 1)
            pe.wait_ge(S["qs_ok"], 8 * b + 8)
            if keys:
                pe.wait_ge(S["k_exp"], 4 * b + 8)
            else:
                pe.wait_ge(S["x2t_ok"], b)
            for h in range(2):
                for o in range(OT):
                    last = nc.tensor.matmul(bank(2 + h), mt[:, o, :], qs[:, o, h * HALF:(h + 1) * HALF],
                                            start=(o == 0), stop=(o == OT - 1))
                last.then_inc(S["out_mm"], 1)

        def pe_tail1(pe, b):
            pe.wait_ge(S["sq_ok"], b + 1)
            pe.wait_ge(S["mgt_ok"], b + ONE)
            for t in range(NT):
                last = nc.tensor.matmul(bank(7)[:, t:t + 1], sq[:, t * P:(t + 1) * P], ones[:, 0:1],
                                        start=True, stop=True)
            last.then_inc(S["ssq_mm"], 1)

        def pe_tail2(pe, b):
            pe.wait_ge(S["dg_ok"], b + 1 + ONE)
            pe.wait_ge(S["ob_ok"], b + 1)
            for h in range(2):
                last = nc.tensor.matmul(bank(2 + h), ones[:, :],
                                        dg[:, 4 * h:4 * h + 4, :].rearrange("p a c -> p (a c)"),
                                        start=True, stop=True)
            last.then_inc(S["bc_mm"], 1)

        def pe_tail3(pe, b):
            pe.wait_ge(S["x2_ok"], b + 1)
            for k in range(KC):
                last = nc.tensor.transpose(banks[1][:, k * P:(k + 1) * P], x2[:, k * P:(k + 1) * P],
                                           ident[:, :])
            last.then_inc(S["x2t_mm"], 1)

        def pe_tail4(pe, b):
            pe.wait_ge(S["x2t_ok"], b + 1)
            for k in range(KC):
                last = nc.tensor.matmul(bank(7)[:, P:P + RA], x2T[:, k, :], rat[:, k, :], start=(k == 0),
                                        stop=(k == KC - 1))
            last.then_inc(S["ra_mm"], 1)

        def pe_tail_gated(pe, b):
            pe.wait_ge(S["mg_ok"], b + 1)
            nc.tensor.transpose(bank(7)[:, 2 * P:3 * P], mg, ident[:, :]).then_inc(S["mgt_mm"], 1)

        def pe_tail5(pe, b, queries_read):
            pe.wait_ge(S["mgt_ok"], b + 1 + ONE)
            pe.wait_ge(S["q_sub"], queries_read)
            for h in range(2):
                last = nc.tensor.matmul(bank(h), mgT, bful[:, h * HALF:(h + 1) * HALF], start=True,
                                        stop=True)
            last.then_inc(S["delta_mm"], 1)

        PE_TAIL = {0: pe_tail1, 1: pe_tail2, 3: pe_tail3, 4: pe_tail4, 6: pe_tail_gated}

        def act_softplus(act, g, q, tiles):
            s = NQ * g + q
            if tiles[0] == 0:
                act.wait_ge(S["dtu_ok"], s + ONE)
            for i in tiles:
                d = dt[q % 2][:, i, :]
                act.wait_ge(S["dt_mm"], 4 * s + i + 1)
                nc.scalar.activation(d, bank(4 + i % 2), ACT.Abs).then_inc(S["dt_abs"], 1)
                act.wait_ge(S["dt_abs"], 4 * s + i + 1)
                nc.scalar.activation(d, d, ACT.Exp, scale=-1.0).then_inc(S["dt_exp"], 1)
                act.wait_ge(S["dt_exp"], 4 * s + i + 1)
                nc.scalar.activation(d, d, ACT.Ln, bias=1.0).then_inc(S["dt_ln"], 1)

        def act_step(act, g, q, last=False):
            s = NQ * g + q
            for n in range(N):
                for i in range(QD):
                    e = 4 * (N * s + n) + i
                    if n == 0:
                        act.wait_ge(S["dt_ok"], 4 * s + i + 1)
                    act.wait_ge(S["scan_ok"], e - 1 + SCAN)
                    nc.scalar.activation(by_seq(bank(i % 2))[:, :, 1:SEQ],
                                         by_seq(dt[q % 2][:, i, :])[:, :, 1:SEQ], ACT.Exp,
                                         scale=a_sb[:, QD * q + i, n:n + 1]).then_inc(S["exp_ok"], 1)
                if n in (3, 5, 7, 9):
                    i = (n - 3) // 2
                    if i == 0:
                        act.wait_ge(S["fin"], 4 * s + FIN)
                    act.wait_ge(S["z_mm"], 4 * s + i + 1 + Z_MM)
                    nc.scalar.activation(zs[:, i, :], bank(6 + i % 2), ACT.Copy).then_inc(S["z_copied"], 1)
                if n == 10:
                    act.wait_ge(S["z_copied"], 4 * s + 4)
                    nc.scalar.activation(zs, zs, ACT.Silu).then_inc(S["z_silu"], 1)
                    act.preload_act_table_set(LN_EXP_SET)
                if not last and n in (11, 13):
                    act_softplus(act, *following(g, q), (0, 1) if n == 11 else (2, 3))

        def act_keys(act, b, o):
            act.wait_ge(S["k_neg"], 4 * b + o + 1)
            if o == 0:
                act.wait_ge(S["et_mm"], 8 * b)
                act.wait_ge(S["rk1"], b)
            nc.scalar.activation(ek[:, o, :], banks[1][:, :], ACT.Exp, bias=nkm[:, o:o + 1],
                                 accum_out=ksum[:, o:o + 1]).then_inc(S["k_exp"], 1)

        def act_sequence(act, b, keys, tail):
            for t in range(NT + 3):
                if t < 4:
                    for r in (2 * t, 2 * t + 1):
                        act.wait_ge(S["et_mm"], 8 * b + r + 1)
                        if r == 0:
                            act.wait_ge(S["g_mm"], b)
                        nc.scalar.activation(ekT[:, r, :], bank(5), ACT.Copy).then_inc(S["et_ok"], 1)
                if t < NT:
                    act.wait_ge(S["q_sub"], 8 * b + t + 1)
                    nc.scalar.activation(qe[:, t, :], qe[:, t, :], ACT.Exp).then_inc(S["q_exp"], 1)
                if tail and t in ACT_TAIL:
                    ACT_TAIL[t](act, b - 1)
                if t >= 3:
                    r = t - 3
                    act.wait_ge(S["qt_mm"], 8 * b + r + 1)
                    if r == 0:
                        act.wait_ge(S["out_mm"], 2 * b)
                    nc.scalar.activation(qs[:, :, r * P:(r + 1) * P],
                                         bank(4).rearrange("p (o n) -> p o n", o=OT), ACT.Copy)\
                        .then_inc(S["qs_ok"], 1)
                if keys and 4 <= t < 8:
                    act_keys(act, b + 1, t - 4)
                if t == 8:
                    act.wait_ge(S["g_mm"], b + 1)
                    act.wait_ge(S["mt_mm"], b)
                    nc.scalar.activation(gT, bank(6), ACT.Copy).then_inc(S["g_ok"], 1)
            act_attend(act, b)

        def act_attend(act, b):
            act.wait_ge(S["out_mm"], 2 * b + 2)
            act.wait_ge(S["y2_ok"], b)
            nc.scalar.activation(ob, banks[1][:, :], ACT.Identity, bias=bov[:, 0:1])\
                .then_inc(S["ob_ok"], 1)
            act.wait_ge(S["ssq_mm"], b)
            nc.scalar.activation(sq, banks[1][:, :], ACT.Square, bias=bov[:, 0:1]).then_inc(S["sq_ok"], 1)

        def act_tail3(act, b):
            act.wait_ge(S["x2t_mm"], b + 1)
            nc.scalar.activation(x2T, banks[1][:, :].rearrange("p (k t) -> p k t", k=KC), ACT.Copy)\
                .then_inc(S["x2t_ok"], 1)

        def act_tail_gate(act, b):
            act.wait_ge(S["lg_neg"], b + 1)
            nc.scalar.activation(lex[:, :], lg[:, :], ACT.Exp, bias=nlm[:, :]).then_inc(S["gate_exp"], 1)

        def act_tail_gated(act, b):
            act.wait_ge(S["mgt_mm"], b + 1)
            nc.scalar.activation(mgT, bank(7)[:, 2 * P:3 * P], ACT.Copy).then_inc(S["mgt_ok"], 1)

        ACT_TAIL = {3: act_tail3, 5: act_tail_gate, 6: act_tail_gated}

        def pool_rstd(pool, g):
            pool.wait_ge(S["ln_eps"], g + 1)
            nc.gpsimd.tensor_tensor(ve1[:, :], ve1[:, :], mhalf[:, 0:GB], ALU.pow).then_inc(S["ln_rstd"], 1)

        def pool_sequence(pool, b, tail):
            for t in range(NT):
                if tail and t == 0:
                    pool_tail1(pool, b - 1)
                pool.wait_ge(S["q_rec"], 8 * b + t + 1)
                v = qe[:, t, :].rearrange("p (h d) -> p h d", h=HEADS)
                nc.gpsimd.tensor_tensor(v, v, qr[:, t % 2, :][:, :, None].broadcast_to([P, HEADS, DH]),
                                        ALU.mult).then_inc(S["q_norm"], 1)
                if tail and t == 1:
                    pool_tail_rstd(pool, b - 1, 0)
            if tail:
                pool_tail_rstd(pool, b - 1, 1)

        def pool_tail1(pool, b):
            pool.wait_ge(S["ssq_max"], b + 1)
            nc.gpsimd.tensor_tensor(rn[:, :], rn[:, :], mhalf[:, 0:NT], ALU.pow).then_inc(S["ssq_pow"], 1)
            pool.wait_ge(S["ssq_pow"], b + 1)
            pool.wait_ge(S["bc_mm"], b + ONE)
            nc.gpsimd.tensor_tensor(dg, ident[:, :][:, None, :].broadcast_to([P, NT, P]),
                                    rn[:, :][:, :, None].broadcast_to([P, NT, P]), ALU.mult)\
                .then_inc(S["dg_ok"], 1)

        def pool_tail_rstd(pool, b, k):
            pool.wait_ge(S["l2_eps"], 2 * b + k + 1)
            nc.gpsimd.tensor_tensor(ve1[:, 0:1], ve1[:, 0:1], mhalf[:, 0:1], ALU.pow)\
                .then_inc(S["l2_rstd"], 1)

        def dve_dt(dve, g, q, tiles):
            s = NQ * g + q
            for i in tiles:
                d = dt[q % 2][:, i, :]
                dve.wait_ge(S["dt_ln"], 4 * s + i + 1)
                nc.vector.scalar_tensor_tensor(d, bank(4 + i % 2), 0.0, d, ALU.max, ALU.add)\
                    .then_inc(S["dt_ok"], 1)

        def dve_scan(dve, g, q, n, i):
            U = N * (NQ * g + q) + n
            if i == 0:
                dve.wait_ge(S["bm_ok"], U + 1 + BM)
            dve.wait_ge(S["exp_ok"], 4 * U + i + 1)
            h = hb[n % 4][:, i * GT:(i + 1) * GT]
            nc.vector.tensor_tensor_scan(h, bank(i % 2), h, 0.0, ALU.mult, ALU.add)\
                .then_inc(S["scan_ok"], 1)

        def dve_acc(dve, g, q, n, b):
            s = NQ * g + q
            k = 4 * (N * s + n) + b
            dve.wait_ge(S["t_done"], k + 1 + T_DONE)
            c = cg[:, b, n:n + 1]
            if n == 0:
                if b == 0:
                    dve.wait_ge(S["yt_mm"], 4 * s + ONE)
                    dve.wait_ge(S["cg_ok"], g + 1)
                last = nc.vector.tensor_scalar(acc[:, b, :], bank(2 + b % 2), c, None, ALU.mult)
            else:
                dve.wait_ge(S["acc_ok"], k - 3 + ACCD)
                last = nc.vector.scalar_tensor_tensor(acc[:, b, :], bank(2 + b % 2), c, acc[:, b, :],
                                                      ALU.mult, ALU.add)
            last.then_inc(S["acc_ok"], 1)

        def dve_out(dve, s, c):
            v = rbuf[:, c // 2, (c % 2) * HALF:(c % 2 + 1) * HALF]
            dve.wait_ge(S["o_mm"], 8 * s + c + 1 + ONE)
            dve.wait_ge(S["r_added"], 8 * s + R_ADD)
            nc.vector.tensor_tensor(v, bank(6 + c % 2), v, ALU.add).then_inc(S["r_added"], 1)

        def dve_ln_stats(dve, g):
            dve.wait_ge(S["r_added"], 8 * (NQ * g + 1) + R_ADD)
            for t in range(GB):
                for h in range(2):
                    nc.vector.bn_stats(st1[:, t, h, :], rbuf[:, t, h * HALF:(h + 1) * HALF])\
                        .then_inc(S["ln_stats"], 1)
            dve.wait_ge(S["ln_stats"], 8 * g + 8)
            nc.vector.memset(idle[:, :], 0.0)
            for t in range(GB):
                nc.vector.bn_aggr(mv1[:, t, :], st1[:, t, :, :].rearrange("p a s -> p (a s)"))\
                    .then_inc(S["ln_aggr"], 1)
            dve.wait_ge(S["ln_aggr"], 4 * g + 4)
            nc.vector.tensor_scalar(ve1[:, :], mv1[:, :, 1:2].rearrange("p a b -> p (a b)"), LN_EPS, None,
                                    ALU.add).then_inc(S["ln_eps"], 1)

        def dve_ln_apply(dve, g):
            dve.wait_ge(S["ln_rstd"], g + 1)
            for t in range(GB):
                nc.vector.tensor_scalar(rbuf[:, t, :], rbuf[:, t, :], mv1[:, t, 0:1], ve1[:, t:t + 1],
                                        ALU.subtract, ALU.mult).then_inc(S["ln_ok"], 1)

        def dve_group(dve, g, last):
            dve.wait_ge(S["acc_ok"], 64 * 4 * g + ACCD)
            nc.vector.tensor_copy(cg[:, :, :], cbt[:, bass.ds(GB * g, GB), :]).then_inc(S["cg_ok"], 1)
            for q in range(NQ):
                dve_step(dve, g, q, last and q == NQ - 1)

        def dve_step(dve, g, q, last):
            s = NQ * g + q
            for n in range(N):
                if n < N - 2:
                    scans = [(g, q, n + 2, i) for i in range(QD)]
                else:
                    scans = [] if last else [(*following(g, q), n + 2 - N, i) for i in range(QD)]
                if q == 1 and n == 8:
                    dve.wait_ge(S["r_loaded"], 16 * g + 16)
                for part in range(2):
                    dve_acc(dve, g, q, n, 2 * part)
                    dve_acc(dve, g, q, n, 2 * part + 1)
                    for unit in scans[2 * part:2 * part + 2]:
                        dve_scan(dve, *unit)
                if n >= 8:
                    dve_out(dve, s, n - 8)
                if not last and n in (10, 12):
                    dve_dt(dve, *following(g, q), (0, 1) if n == 10 else (2, 3))
                if q == 1 and n == 1:
                    dve_ln_stats(dve, g)
                if q == 1 and n == 3:
                    dve_ln_apply(dve, g)
            dve.wait_ge(S["o_mm"], 8 * s + 8 + ONE)
            dve.wait_ge(S["z_silu"], s + 1)

            def skip(i):
                dve.wait_ge(S["yt_mm"], 4 * s + i + 1 + ONE)
                nc.vector.scalar_tensor_tensor(yq[:, i, :], uq[q % 2][:, i, :],
                                               dsk[:, QD * q + i:QD * q + i + 1], bank(4 + i % 2),
                                               ALU.mult, ALU.add).then_inc(S["fin1"], 1)

            skip(0)
            for i in range(QD):
                if i < QD - 1:
                    skip(i + 1)
                dve.wait_ge(S["fin1"], 4 * s + i + 1 + FIN1)
                nc.vector.tensor_tensor(yq[:, i, :], yq[:, i, :], zs[:, i, :], ALU.mult)\
                    .then_inc(S["fin"], 1)

        def dve_keys(dve, b, o):
            dve.wait_ge(S["k_mm"], 4 * b + o + 1)
            nc.vector.tensor_reduce(km[:, o:o + 1], banks[1][:, :], AX_X, ALU.max).then_inc(S["k_max"], 1)
            dve.wait_ge(S["k_max"], 4 * b + o + 1)
            if o == 0:
                dve.wait_ge(S["k_exp"], 4 * b)
            nc.vector.tensor_scalar(nkm[:, o:o + 1], km[:, o:o + 1], -1.0, None, ALU.mult)\
                .then_inc(S["k_neg"], 1)

        def dve_keys_scale(dve, b):
            dve.wait_ge(S["k_exp"], 4 * b + 4)
            nc.vector.reciprocal(rk[:, :], ksum[:, :]).then_inc(S["rk1"], 1)
            dve.wait_ge(S["rk1"], b + 1)
            nc.vector.tensor_scalar(rk[:, :], rk[:, :], DH ** -0.5, None, ALU.mult).then_inc(S["rk2"], 1)

        def dve_values(dve, b):
            dve.wait_ge(S["rk2"], b + 1)
            dve.wait_ge(S["mt_mm"], b + 1)
            dve.wait_ge(S["out_mm"], 2 * b)
            nc.vector.tensor_tensor(mt, bank(6).rearrange("p (o c) -> p o c", o=OT),
                                    rk[:, :][:, :, None].broadcast_to([P, OT, P]), ALU.mult)\
                .then_inc(S["mt_ok"], 1)

        def dve_sequence(dve, b, keys, tail):
            def start(t):
                ps = bank(t % 2).rearrange("p (h d) -> p h d", h=HEADS)
                dve.wait_ge(S["q_mm"], 8 * b + t + 1)
                nc.vector.tensor_reduce(qm[:, t % 2, :], ps, AX_X, ALU.max).then_inc(S["q_max"], 1)
                dve.wait_ge(S["q_max"], 8 * b + t + 1)
                if t == 0:
                    dve.wait_ge(S["qt_mm"], 8 * b)
                nc.vector.tensor_tensor(qe[:, t, :].rearrange("p (h d) -> p h d", h=HEADS), ps,
                                        qm[:, t % 2, :][:, :, None].broadcast_to([P, HEADS, DH]),
                                        ALU.subtract).then_inc(S["q_sub"], 1)

            def denominator(t):
                dve.wait_ge(S["q_exp"], 8 * b + t + 1)
                nc.vector.tensor_reduce(qz[:, t % 2, :], qe[:, t, :].rearrange("p (h d) -> p h d", h=HEADS),
                                        AX_X, ALU.add).then_inc(S["q_sum"], 1)
                dve.wait_ge(S["q_sum"], 8 * b + t + 1)
                if t >= 2:
                    dve.wait_ge(S["q_norm"], 8 * b + t - 1)
                nc.vector.reciprocal(qr[:, t % 2, :], qz[:, t % 2, :]).then_inc(S["q_rec"], 1)

            for t in range(NT + 1):
                if t < NT:
                    start(t)
                if t >= 1:
                    denominator(t - 1)
                if tail and t in DVE_TAIL:
                    DVE_TAIL[t](dve, b - 1)
                if t == 2:
                    dve_keys_scale(dve, b)
                if keys and 4 <= t < 8:
                    dve_keys(dve, b + 1, t - 4)
            if tail:
                dve_tail4(dve, b - 1)
            dve_values(dve, b)
            if tail:
                dve_norm_apply(dve, b - 1, 1, x3, x3, "x3_ok")

        def dve_tail1(dve, b):
            dve.wait_ge(S["ssq_mm"], b + 1)
            dve.wait_ge(S["dg_ok"], b + ONE)
            nc.vector.tensor_scalar(rn[:, :], bank(7)[:, 0:NT], 1e-24, None, ALU.max)\
                .then_inc(S["ssq_max"], 1)

        def dve_norm_stats(dve, b, k, src):
            for h in range(2):
                nc.vector.bn_stats(st1[:, 0, h, :], src[:, h * HALF:(h + 1) * HALF])\
                    .then_inc(S["l2_stats"], 1)
            dve.wait_ge(S["l2_stats"], 4 * b + 2 * k + 2)
            nc.vector.memset(idle[:, :], 0.0)
            nc.vector.bn_aggr(mv1[:, 0, :], st1[:, 0, :, :].rearrange("p a s -> p (a s)"))\
                .then_inc(S["l2_aggr"], 1)
            dve.wait_ge(S["l2_aggr"], 2 * b + k + 1)
            nc.vector.tensor_scalar(ve1[:, 0:1], mv1[:, 0, 1:2], LN_EPS, None, ALU.add)\
                .then_inc(S["l2_eps"], 1)

        def dve_norm_apply(dve, b, k, src, dst, done):
            dve.wait_ge(S["l2_rstd"], 2 * b + k + 1)
            nc.vector.tensor_scalar(dst, src, mv1[:, 0, 0:1], ve1[:, 0:1], ALU.subtract, ALU.mult)\
                .then_inc(S[done], 1)

        def dve_tail2(dve, b):
            dve.wait_ge(S["bc_mm"], b + 1 + ONE)
            dve.wait_ge(S["ob_ok"], b + 1)
            dve.wait_ge(S["gs_ok"], 1)
            nc.vector.scalar_tensor_tensor(ob, ob, gs[:, 0:1], banks[1][:, :], ALU.mult, ALU.mult)\
                .then_inc(S["y2a"], 1)
            dve.wait_ge(S["y2a"], b + 1)
            dve.wait_ge(S["xres_loaded"], 16 * b + 16)
            dve.wait_ge(S["x3_add"], b + ONE)
            nc.vector.tensor_tensor(x2, ob, xres, ALU.add).then_inc(S["y2_ok"], 1)
            dve.wait_ge(S["y2_ok"], b + 1)
            dve_norm_stats(dve, b, 0, x2)

        def dve_tail_x2(dve, b):
            dve_norm_apply(dve, b, 0, x2, x2, "x2_ok")

        def dve_tail3(dve, b):
            step = [0]

            def small(ins):
                step[0] += 1
                ins.then_inc(S["gate_step"], 1)
                dve.wait_ge(S["gate_step"], GATE_STEPS * b + step[0])

            ra = bank(7)[:, P:P + RA]
            of_j = lg[:, :][:, None, :].broadcast_to([P, NE, NE])
            of_e = lg[:, :][:, :, None].broadcast_to([P, NE, NE])
            dve.wait_ge(S["ra_mm"], b + 1)
            small(nc.vector.tensor_copy(lg[:, :], ra[:, 0:NE]))
            small(nc.vector.tensor_reduce(nlm[:, :], lg[:, :], AX_X, ALU.max))
            nc.vector.tensor_scalar(nlm[:, :], nlm[:, :], -1.0, None, ALU.mult).then_inc(S["lg_neg"], 1)
            small(nc.vector.tensor_tensor(cgt[:, :, :], of_j, of_e, ALU.is_gt))
            small(nc.vector.tensor_tensor(cge[:, :, :], of_j, of_e, ALU.is_ge))
            small(nc.vector.tensor_tensor(cgt[:, :, :], cgt[:, :, :], upper[:, :, :], ALU.mult))
            small(nc.vector.tensor_tensor(cge[:, :, :], cge[:, :, :], lower[:, :, :], ALU.mult))
            small(nc.vector.tensor_tensor(cgt[:, :, :], cgt[:, :, :], cge[:, :, :], ALU.add))
            small(nc.vector.tensor_reduce(rank[:, :], cgt[:, :, :], AX_X, ALU.add))
            dve.wait_ge(S["gate_exp"], b + 1)
            small(nc.vector.scalar_tensor_tensor(gate[:, :], rank[:, :], 2.0, lex[:, :], ALU.is_lt, ALU.mult))
            small(nc.vector.tensor_reduce(gsum[:, :], gate[:, :], AX_X, ALU.add))
            small(nc.vector.reciprocal(gsum[:, :], gsum[:, :]))
            small(nc.vector.tensor_scalar(gate[:, :], gate[:, :], gsum[:, :], 4.0, ALU.mult, ALU.mult))
            nc.vector.tensor_tensor(mg[:, 0:NE * ER].rearrange("p (e r) -> p e r", e=NE),
                                    ra[:, NE:RA].rearrange("p (e r) -> p e r", e=NE),
                                    gate[:, :][:, :, None].broadcast_to([P, NE, ER]), ALU.mult)\
                .then_inc(S["mg_ok"], 1)
            assert step[0] == GATE_STEPS

        def dve_tail4(dve, b):
            dve.wait_ge(S["delta_mm"], b + 1)
            dve.wait_ge(S["out_stored"], 16 * b + ONE)
            nc.vector.tensor_tensor(x3, banks[0][:, :], x2, ALU.add).then_inc(S["x3_add"], 1)
            dve.wait_ge(S["x3_add"], b + 1 + ONE)
            dve_norm_stats(dve, b, 1, x3)

        DVE_TAIL = {0: dve_tail1, 1: dve_tail2, 2: dve_tail_x2, 5: dve_tail3}

        block = ctx.enter_context(nc.Block())

        @block.sync
        def _(sp):
            for name in ("out_stored", "u_stored0", "u_stored1"):
                sp.sem_inc(S[name], ONE)
            for i in range(NG):
                sp.dma_start(xT[:, :, i * GT:(i + 1) * GT], a["xT"][:, :, i * GT:(i + 1) * GT])\
                    .then_inc(S[f"xt_loaded{i}"], 16)
                if i == 0:
                    sync_tile(sp, 0, 0)
                    for dst, name in consts0:
                        sp.dma_start(dst, a[name]).then_inc(S["const_loaded"], 16)
            sync_tile(sp, 0, 1)
            sp.wait_ge(S["rows_set"], 1)
            sp.dma_start(wdt[96:97, :], a["b_dt"]).then_inc(S["bdt_loaded"], 16)
            with nc.sync.Fori(1, DT // 2) as mp:
                for par in range(2):
                    sync_tile(sp, mp, par)
                    sync_store_u(sp, mp - 1, par)
            for par in range(2):
                sync_store_u(sp, DT // 2 - 1, par)
            sp.wait_ge(S["bt_rows"], TT // 4)
            sp.dma_start(b_d[:, :], tsb[R:R + N, :]).then_inc(S["b_stored"], 16)

            sp.wait_ge(S["b_stored"], 16)
            sp.wait_ge(S["u_stored0"], 8 * 16 + ONE)
            sp.wait_ge(S["u_stored1"], 8 * 16 + ONE)
            sp.wait_ge(S["phase0_c"], 1)
            sp.wait_ge(S["bt_mm"], TT // 4)
            with nc.sync.Fori(0, NG) as g:
                for q in range(NQ):
                    sync_step(sp, g, q)
            sp.wait_ge(S["o_mm"], 8 * NG * NQ + ONE)
            sp.dma_start(wo, a["WoutT"][NQ - 1]).then_inc(S["wo_loaded"], 16)
            sp.wait_ge(S["ln_ok"], GB * (NG + 1))
            sp.dma_start(x1_d[NG].rearrange("b p h -> p b h"), rbuf[:, :, :]).then_inc(S["x1_stored"], 16)

            sp.wait_ge(S["x1_stored"], 16 * (NG + 1))
            sp.wait_ge(S["o_mm"], 8 * (NG * NQ + 1) + ONE)
            for dst, name in consts2:
                sp.dma_start(dst, a[name]).then_inc(S["p2_const"], 16)
            sync_context(sp, 0)
            for b in range(2):
                sync_seq(sp, b)
            with nc.sync.Fori(2, BATCH - 1) as b:
                sync_seq(sp, b, store=b - 2)
            sync_seq(sp, BATCH - 1, store=BATCH - 3, context=False)
            sync_store(sp, BATCH - 2)
            sync_store(sp, BATCH - 1)
            sp.wait_ge(S["out_stored"], 16 * BATCH + ONE)

        @block.tensor
        def _(pe):
            pe.sem_inc(S["x_mm"], X_MM)
            for name in ("ss_mm", "o_mm", "yt_mm", "bc_mm"):
                pe.sem_inc(S[name], ONE)
            pe.sem_inc(S["t_done"], T_DONE)
            pe.sem_inc(S["z_mm"], Z_MM)

            def through_wx(mp, par):
                m = 2 * mp + par
                for j in range(4):
                    pe.wait_ge(S["u_done"], 4 * m + j + 1)
                    pe.wait_ge(S["ss_added"], 4 * m + j + 1)
                    for i in range(4):
                        t = 4 * j + i
                        last = nc.tensor.matmul(bank(4 + j)[:, i * SS:(i + 1) * SS],
                                                ust[par][:, t * P:(t + 1) * P],
                                                wxT[:, bass.ds(m, 1), :].rearrange("p a s -> p (a s)"),
                                                start=True, stop=True)
                    last.then_inc(S["ss_mm"], 1)

            pe.wait_ge(S["const_loaded"], C0)
            with nc.tensor.Fori(0, DT // 2) as mp:
                for par in range(2):
                    m = 2 * mp + par
                    pe.wait_ge(S[f"wx_loaded{par}"], 16 * mp + 16)
                    for tg in range(NG):
                        if par == 0:
                            pe.wait_ge(S[f"xt_loaded{tg}"], 16)
                        if par == 1 and tg == 2:
                            through_wx(mp, 0)
                        pe.wait_ge(S["conv_done"], 4 * m + tg - 3 + CONV)
                        for k in range(KC):
                            last = nc.tensor.matmul(bank(tg), wx[par][:, k, :],
                                                    xT[:, k, tg * GT:(tg + 1) * GT],
                                                    start=(k == 0), stop=(k == KC - 1))
                        last.then_inc(S["x_mm"], 1)
                through_wx(mp, 1)
            pe.wait_ge(S["pool_const"], 1)
            pe.wait_ge(S["ss_normed"], 3)
            for j in range(TT // 4):
                for i in range(4):
                    last = nc.tensor.transpose(bank(j)[0:SS, i * P:(i + 1) * P], ssacc[:, 4 * j + i, :],
                                               ident[:, :])
                last.then_inc(S["bt_mm"], 1)

            pe.wait_ge(S["bt_rows"], TT // 4)
            pe.wait_ge(S["bdt_loaded"], 16)
            pe.wait_ge(S["rows_set"], 2)
            for i in range(QD):
                if i >= 2:
                    pe.wait_ge(S["dt_ok"], i - 1)
                pe_dt(pe, 0, 0, i)
            with nc.tensor.Fori(0, NG - 1) as g:
                for q in range(NQ):
                    pe_step(pe, g, q)
            for q in range(NQ):
                pe_step(pe, NG - 1, q, last=(q == NQ - 1))
            pe.wait_ge(S["fin"], 4 * NG * NQ + FIN)
            pe.wait_ge(S["wo_loaded"], 16 * (NG * NQ + 1))
            for c in range(8):
                pe_out(pe, NG * NQ, c, range(4), last_quad=True)

            pe.wait_ge(S["p2_const"], C2)
            pe.wait_ge(S["rows_set"], 4)
            pe.wait_ge(S["r_added"], 8 * (NG * NQ + 1) + R_ADD)
            for h in range(HEADS):
                last = nc.tensor.matmul(bank(h // 4)[:, (h % 4) * P:(h % 4 + 1) * P], wvh[0:DH, h, :],
                                        woh[0:DH, h, :], start=True, stop=True)
            last.then_inc(S["ph_mm"], 1)
            pe.wait_ge(S["ph_ok"], 1)
            for o in range(OT):
                pe_keys(pe, 0, o)
            pe_sequence(pe, 0, keys=True, tail=False)
            with nc.tensor.Fori(1, BATCH - 1) as b:
                pe_sequence(pe, b, keys=True, tail=True)
            pe_sequence(pe, BATCH - 1, keys=False, tail=True)
            for t in sorted(PE_TAIL):
                PE_TAIL[t](pe, BATCH - 1)
            pe_tail5(pe, BATCH - 1, 8 * BATCH)

        @block.scalar
        def _(act):
            for name in ("mgt_ok",):
                act.sem_inc(S[name], ONE)
            act.wait_ge(S["const_loaded"], C0)
            act.preload_act_table_set(LN_EXP_SET)
            nc.scalar.activation(a_sb[:, :, :], a_sb[:, :, :], ACT.Exp).then_inc(S["a_exp"], 1)
            act.preload_act_table_set(SILU_SET)
            with nc.scalar.Fori(0, DT // 2) as mp:
                for x in range(8):
                    par, tg = divmod(x, 4)
                    m = 2 * mp + par
                    count = 8 * mp + x + 1
                    act.wait_ge(S["x_mm"], count + X_MM)
                    nc.scalar.activation(cv[x % 2], bank(tg), ACT.Identity, bias=wxc[par][:, H + 4:H + 5],
                                         scale=wxc[par][:, H + 3:H + 4])\
                        .then_inc(S["conv_base"], 1)
                    if tg == 0:
                        act.wait_ge(S[f"u_stored{par}"], 16 * mp + ONE)
                        act.wait_ge(S["ss_mm"], 8 * mp + ONE)
                    act.wait_ge(S["conv_done"], count + CONV)
                    nc.scalar.activation(ust[par][:, tg * GT:(tg + 1) * GT], cv[x % 2], ACT.Silu)\
                        .then_inc(S["u_done"], 1)

            act.preload_act_table_set(LN_EXP_SET)
            act.wait_ge(S["da_zero"], 1)
            act.wait_ge(S["a_neg"], 1)
            act_softplus(act, 0, 0, range(QD))
            with nc.scalar.Fori(0, NG - 1) as g:
                for q in range(NQ):
                    act_step(act, g, q)
            for q in range(NQ):
                act_step(act, NG - 1, q, last=(q == NQ - 1))

            act.wait_ge(S["p2_const"], C2)
            for o in range(OT):
                act_keys(act, 0, o)
            act_sequence(act, 0, keys=True, tail=False)
            with nc.scalar.Fori(1, BATCH - 1) as b:
                act_sequence(act, b, keys=True, tail=True)
            act_sequence(act, BATCH - 1, keys=False, tail=True)
            for t in sorted(ACT_TAIL):
                ACT_TAIL[t](act, BATCH - 1)

        @block.gpsimd
        def _(pool):
            pool.sem_inc(S["bm_ok"], BM)
            for name in ("dtu_ok", "dg_ok"):
                pool.sem_inc(S[name], ONE)
            nc.gpsimd.memset(ident[:, :], 0.0)
            nc.gpsimd.memset(ones[:, :], 1.0)
            nc.gpsimd.memset(mhalf[:, :], -0.5)
            nc.gpsimd.memset(rbuf[:, :, :], 0.0)
            nc.gpsimd.memset(upper[:, :, :], 0.0)
            nc.gpsimd.memset(lower[:, :, :], 0.0).then_inc(S["phase0_zero"], 1)
            pool.wait_ge(S["phase0_zero"], 1)
            for e in range(NE):
                if e < NE - 1:
                    nc.gpsimd.memset(upper[:, e, e + 1:NE], 1.0)
                if e > 0:
                    nc.gpsimd.memset(lower[:, e, 0:e], 1.0)
            nc.gpsimd.affine_select(out=ident[:, :], in_=ident[:, :], compare_op=ALU.not_equal, fill=1.0,
                                    base=0, pattern=[[-1, P]], channel_multiplier=1)\
                .then_inc(S["pool_const"], 1)
            pool.wait_ge(S["ss_mean"], 2)
            flat3 = ss3[:, :, :].rearrange("p a t -> p (a t)")
            nc.gpsimd.tensor_tensor(flat3, flat3, mhalf[:, :], ALU.pow).then_inc(S["ss_rstd"], 1)

            nc.gpsimd.memset(yq, 0.0).then_inc(S["phase0_zero"], 1)
            with nc.gpsimd.Fori(0, NG) as g:
                for q in range(NQ):
                    s = NQ * g + q
                    pool.wait_ge(S["dt_ok"], 4 * s + 4)
                    pool.wait_ge(S[f"u_loaded{q % 2}"], 16 * (2 * g + q // 2 + 1))
                    pool.wait_ge(S["bm_ok"], N * s + BM)
                    nc.gpsimd.tensor_tensor(dtu, dt[q % 2], uq[q % 2], ALU.mult).then_inc(S["dtu_ok"], 1)
                    pool.wait_ge(S["dtu_ok"], s + 1 + ONE)
                    for n in range(N):
                        if q == 0 and n % 4 == 0:
                            pool.wait_ge(S[f"brep_loaded{n // 4}"], 16 * g + 16)
                        pool.wait_ge(S["t_done"], 4 * (N * s + n) - 12 + T_DONE)
                        nc.gpsimd.tensor_tensor(
                            hb[n % 4].rearrange("p (i t) -> p i t", i=QD), dtu,
                            brep[:, n:n + 1, :].broadcast_to([P, QD, GT]), ALU.mult)\
                            .then_inc(S["bm_ok"], 1)
                        if q == 1 and n == 4:
                            pool_rstd(pool, g)
            pool_rstd(pool, NG)

            pool.wait_ge(S["o_mm"], 8 * (NG * NQ + 1) + ONE)
            pool_sequence(pool, 0, tail=False)
            with nc.gpsimd.Fori(1, BATCH) as b:
                pool_sequence(pool, b, tail=True)
            pool_tail1(pool, BATCH - 1)
            pool_tail_rstd(pool, BATCH - 1, 0)
            pool_tail_rstd(pool, BATCH - 1, 1)

        @block.vector
        def _(dve):
            dve.sem_inc(S["conv_done"], CONV)
            for name in ("x3_add",):
                dve.sem_inc(S[name], ONE)
            dve.sem_inc(S["ss_added"], SS_ADD)
            dve.sem_inc(S["scan_ok"], SCAN)
            dve.sem_inc(S["acc_ok"], ACCD)
            dve.sem_inc(S["r_added"], R_ADD)
            dve.sem_inc(S["fin1"], FIN1)
            dve.sem_inc(S["fin"], FIN)
            nc.vector.memset(wdt[R:P, :], 0.0).then_inc(S["rows_set"], 1)
            nc.vector.memset(tsb[SS:P, :], 1.0).then_inc(S["rows_set"], 1)
            dve.wait_ge(S["const_loaded"], C0)
            dve.wait_ge(S["a_exp"], 1)
            nc.vector.tensor_scalar(a_sb[:, :, :], a_sb[:, :, :], -1.0, None, ALU.mult).then_inc(S["a_neg"], 1)
            nc.vector.memset(ssacc, 0.0).then_inc(S["ss_square"], 1)
            dve.wait_ge(S["ss_square"], 1)

            def add_ss(m):
                for j in range(4):
                    dve.wait_ge(S["ss_mm"], 4 * m + j + 1 + ONE)
                    dve.wait_ge(S["ss_added"], 4 * m + j + 1)
                    v = ssacc[:, 4 * j:4 * j + 4, :].rearrange("p a s -> p (a s)")
                    nc.vector.tensor_tensor(v, v, bank(4 + j)[:, 0:4 * SS], ALU.add)\
                        .then_inc(S["ss_added"], 1)

            with nc.vector.Fori(0, DT // 2) as mp:
                for x in range(8):
                    par, tg = divmod(x, 4)
                    m = 2 * mp + par
                    count = 8 * mp + x
                    dve.wait_ge(S["conv_base"], count + 1)
                    c = by_seq(cv[x % 2])
                    for sh in range(1, 4):
                        if sh > 1:
                            dve.wait_ge(S["conv_tap"], 2 * count + sh - 1)
                        last = nc.vector.scalar_tensor_tensor(
                            c[:, :, sh:SEQ], by_seq(bank(tg))[:, :, 0:SEQ - sh],
                            wxc[par][:, H + 3 - sh:H + 4 - sh],
                            c[:, :, sh:SEQ], ALU.mult, ALU.add)
                        last.then_inc(S["conv_tap" if sh < 3 else "conv_done"], 1)
                    if x == 5:
                        add_ss(2 * mp)
                add_ss(2 * mp + 1)
            dve.wait_ge(S["ss_added"], 4 * DT + SS_ADD)
            nc.vector.tensor_tensor(sssq, ssacc, ssacc, ALU.mult).then_inc(S["ss_square"], 1)
            dve.wait_ge(S["ss_square"], 2)
            parts = ((0, R), (R, R + N), (R + N, SS))
            for j, (lo, hi) in enumerate(parts):
                nc.vector.tensor_reduce(ss3[:, j, :], sssq[:, :, lo:hi], AX_X, ALU.add)\
                    .then_inc(S["ss_sum"], 1)
            dve.wait_ge(S["ss_sum"], 3)
            nc.vector.tensor_scalar(ss3[:, 0, :], ss3[:, 0, :], 1.0 / R, RMS_EPS, ALU.mult, ALU.add)\
                .then_inc(S["ss_mean"], 1)
            nc.vector.tensor_scalar(ss3[:, 1:3, :], ss3[:, 1:3, :], 1.0 / N, RMS_EPS, ALU.mult, ALU.add)\
                .then_inc(S["ss_mean"], 1)
            dve.wait_ge(S["ss_rstd"], 1)
            for j, (lo, hi) in enumerate(parts):
                v = ssacc[:, :, lo:hi]
                nc.vector.tensor_tensor(v, v, ss3[:, j, :][:, :, None].broadcast_to([P, TT, hi - lo]),
                                        ALU.mult).then_inc(S["ss_normed"], 1)
            dve.wait_ge(S["ss_normed"], 3)
            nc.vector.tensor_copy(cbt[:, :, :], ssacc[:, :, R + N:SS]).then_inc(S["phase0_c"], 1)
            dve.wait_ge(S["pool_const"], 1)
            for j in range(TT // 4):
                dve.wait_ge(S["bt_mm"], j + 1)
                nc.vector.tensor_copy(tsb[0:SS, j * HALF:(j + 1) * HALF], bank(j)[0:SS, :])\
                    .then_inc(S["bt_rows"], 1)

            dve.wait_ge(S["bt_rows"], TT // 4)
            for i in range(2):
                last = nc.vector.memset(by_seq(bank(i))[:, :, 0:1], 0.0)
            last.then_inc(S["da_zero"], 1)
            dve.wait_ge(S["phase0_c"], 1)
            dve.wait_ge(S["phase0_zero"], 2)
            dve_dt(dve, 0, 0, range(QD))
            for i in range(2 * QD):
                dve_scan(dve, 0, 0, i // QD, i % QD)

            with nc.vector.Fori(0, NG - 1) as g:
                dve_group(dve, g, last=False)
            dve_group(dve, NG - 1, last=True)
            for c in range(8):
                dve_out(dve, NG * NQ, c)
            dve_ln_stats(dve, NG)
            dve_ln_apply(dve, NG)

            dve.wait_ge(S["p2_const"], C2)
            nc.vector.memset(bful[NE * ER:P, :], 0.0).then_inc(S["rows_set"], 1)
            nc.vector.memset(mg[:, NE * ER:P], 0.0).then_inc(S["rows_set"], 1)
            dve.wait_ge(S["ph_mm"], 1)
            nc.vector.tensor_copy(ph, banks[0][:, :].rearrange("p (h c) -> p h c", h=HEADS))\
                .then_inc(S["ph_ok"], 1)
            nc.vector.tensor_scalar(gs[:, :], bov[:, 1:2], float(np.sqrt(SEQ)), None, ALU.mult)\
                .then_inc(S["gs_ok"], 1)
            for o in range(OT):
                dve_keys(dve, 0, o)
            dve_sequence(dve, 0, keys=True, tail=False)
            with nc.vector.Fori(1, BATCH - 1) as b:
                dve_sequence(dve, b, keys=True, tail=True)
            dve_sequence(dve, BATCH - 1, keys=False, tail=True)
            for t in sorted(DVE_TAIL):
                DVE_TAIL[t](dve, BATCH - 1)
            dve_tail4(dve, BATCH - 1)
            dve_norm_apply(dve, BATCH - 1, 1, x3, x3, "x3_ok")


def _layouts(i):
    f = np.ascontiguousarray
    x = np.asarray(i["x"])
    ctx = np.asarray(i["ctx_4096"])
    tok = x.reshape(TOK, H)
    win = np.asarray(i["L0_attn_W_in"])
    tiles = win.reshape(2 * DT, P, KC, P).transpose(0, 3, 2, 1)
    taps = np.concatenate([np.asarray(i["L0_attn_conv_w"]), np.asarray(i["L0_attn_conv_b"])[:, None]],
                          axis=1).reshape(DT, P, 5)
    per_tile = lambda v: f(np.asarray(v).reshape(DT, P, -1).transpose(1, 0, 2))
    heads = lambda w: f(w.reshape(HEADS, DH, P).transpose(1, 0, 2))
    return {
        "xT": f(tok.T.reshape(KC, P, TOK).transpose(1, 0, 2)),
        "x": f(x.reshape(NG, GB, SEQ, H).transpose(0, 2, 1, 3)),
        "ctx": f(ctx),
        "ctxT": f(ctx.reshape(BATCH, SEQ, NT, P).transpose(0, 3, 2, 1)),
        "WinX": f(np.concatenate([tiles[:DT].reshape(DT, P, H), taps], axis=2)),
        "WinZ": f(tiles[DT:]),
        "WxT": f(np.asarray(i["L0_attn_W_x"]).reshape(SS, DT, P).transpose(2, 1, 0)),
        "WdtT": f(np.asarray(i["L0_attn_W_dt"]).T),
        "b_dt": f(np.asarray(i["L0_attn_b_dt"]).reshape(1, D_IN)),
        "A_log": per_tile(i["L0_attn_A_log"]),
        "D": per_tile(i["L0_attn_D"]).reshape(P, DT),
        "WoutT": f(np.asarray(i["L0_attn_W_out"]).T.reshape(NQ, QD, P, H).transpose(0, 2, 1, 3)),
        "WqT": f(np.asarray(i["L0_xattn_Wq"]).T),
        "WkT": f(np.asarray(i["L0_xattn_Wk"]).T),
        "Wvh": heads(np.asarray(i["L0_xattn_Wv"])),
        "Woh": heads(f(np.asarray(i["L0_xattn_Wo"]).T)),
        "bo": f(np.asarray(i["L0_xattn_bo"]).reshape(P, 1)),
        "g": f(np.asarray(i["L0_xattn_g"]).reshape(P, 1)),
        "RAT": f(np.concatenate([np.asarray(i["L0_ffn_router_w"]),
                                 np.asarray(i["L0_ffn_A"]).reshape(NE * ER, H)])
                 .T.reshape(KC, P, RA).transpose(1, 0, 2)),
        "Bf": f(np.asarray(i["L0_ffn_B"]).transpose(0, 2, 1).reshape(NE * ER, H)),
    }


def kernel(**inputs):
    import concourse.bacc as bacc
    from concourse.bass_utils import run_bass_kernel_spmd

    nc = bacc.Bacc("TRN2", target_bir_lowering=False, num_devices=1)
    arrays = {f"in_{k}": v for k, v in _layouts(inputs).items()}
    aps = {k[3:]: nc.dram_tensor(k, v.shape, mybir.dt.from_np(v.dtype), kind="ExternalInput").ap()
           for k, v in arrays.items()}
    out = nc.dram_tensor("out", (BATCH, SEQ, H), F32, kind="ExternalOutput").ap()
    program(nc, aps, out)
    r = run_bass_kernel_spmd(nc, [arrays], core_ids=[0])
    return r.results[0]["out"]
```

```python
from contextlib import ExitStack

import numpy as np

import concourse.bass as bass
from concourse import mybir

ALU = mybir.AluOpType
ACT = mybir.ActivationFunctionType
F32 = mybir.dt.float32
AX_X = mybir.AxisListType.X
LN_EXP_SET = "natural_log_exp_and_others"
SILU_SET = "silu_and_others"

P = 128
BATCH, SEQ, H = 16, 128, 1024
TOK = BATCH * SEQ
D_IN, N, R = 2048, 16, 64
DT = D_IN // P
KC = H // P
GB = 4
GT = GB * SEQ
NG = TOK // GT
QD = 4
NQ = DT // QD
TT = TOK // P
SS = R + 2 * N
HEADS, DH = 8, 64
HID = HEADS * DH
OT = HID // P
NT = H // P
NE, ER = 4, 16
RA = NE + NE * ER
SLOTS = NT + 3
KEY_SLOTS = (3, 5, 7, 9)
HALF = 512
BT_BANKS = (2, 3, 6, 7)
LN_EPS, RMS_EPS = 1e-5, 1e-6
GATE_STEPS = 12

X_MM, CONV, SS_ADD = 8, 8, 4
T_DONE, SCAN, ACCD, R_ADD, FIN1, FIN, Z_MM, BM = 13, 2, 2, 2, 2, 5, 2, 13
ONE = 1

SEMS = """const_loaded xt_loaded0 xt_loaded1 xt_loaded2 xt_loaded3 pool_const rows_set bdt_loaded a_exp a_neg x_mm conv_base conv_tap conv_done u_done
ss_mm ss_added ss_square ss_sum ss_mean ss_ln ss_rstd ss_normed bt_mm bt_rows b_stored wx_loaded0 wx_loaded1 u_stored0 u_stored1
phase0_zero phase0_c da_zero xg_loaded wz_loaded0 wz_loaded1 wo_loaded u_loaded0 u_loaded1 r_loaded
brep_loaded0 brep_loaded1 brep_loaded2 brep_loaded3 dt_mm dt_abs dt_exp dt_ln dt_ok dtu_ok cg_ok exp_ok bm_ok
scan_ok t_done acc_ok yt_mm fin1 fin z_mm z_copied z_silu o_mm r_added ln_stats ln_aggr ln_eps ln_rstd
ln_ok x1_stored
p2_const ph_mm ph_ok gs_ok cn_loaded ct_loaded x1_loaded xres_loaded out_stored
k_mm k_max k_neg k_exp et_mm et_ok g_mm g_ok rk1 rk2 mt_mm mt_ok
q_mm q_max q_sub q_exp q_sum q_rec q_norm qt_mm qs_ok out_mm sq_ok
ssq_mm ssq_ln rnorm_ok y2a y2_ok l2_stats l2_aggr l2_eps l2_rstd x2_ok x2t_mm x2t_ok
ra_mm gate_step lg_neg gate_exp mg_ok mgt_mm mgt_ok delta_mm x3_add x3_ok""".split()


def program(nc, a, out):
    u_d = nc.dram_tensor("u_scratch", (DT, P, TOK), F32, kind="Internal").ap()
    b_d = nc.dram_tensor("b_scratch", (N, TOK), F32, kind="Internal").ap()
    x1_d = nc.dram_tensor("x1_scratch", (NG + 1, GB, P, H), F32, kind="Internal").ap()

    with ExitStack() as ctx:
        def sb(name, shape):
            return ctx.enter_context(nc.sbuf_tensor(name, shape, F32))

        S = {name: ctx.enter_context(nc.semaphore(name)) for name in SEMS}

        arena = sb("arena", [P, 43008])

        def at(off, *dims):
            v = arena[:, off:off + int(np.prod(dims))]
            if len(dims) == 1:
                return v
            names = "abcd"[:len(dims)]
            return v.rearrange("p (%s) -> p %s" % (" ".join(names), " ".join(names)),
                               **dict(zip(names[1:], dims[1:])))

        xT = at(0, KC, TOK)
        wxc = [at(26624 + 1536 + 1040 * i, H + 5) for i in range(2)]
        wx = [v[:, 0:H].rearrange("p (k m) -> p k m", k=KC) for v in wxc]
        ust = [at(18432 + 2048 * i, TOK) for i in range(2)]
        cv = [at(22528 + GT * i, GT) for i in range(2)]
        wxT = at(23552, DT, SS)
        ssacc = at(25088, TT, SS)
        sssq = at(26624, TT, SS)
        brep = at(0, N, GT)
        hb = [at(8192 + 2048 * i, QD * GT) for i in range(4)]
        xg = at(16384, KC, GT)
        wz = [at(20480 + 1024 * i, KC, P) for i in range(2)]
        wo = at(22528, QD, H)
        uq = [at(26624 + 2048 * i, QD, GT) for i in range(2)]
        dt = [at(30720 + 2048 * i, QD, GT) for i in range(2)]
        dtu = at(34816, QD, GT)
        zs = at(36864, QD, GT)
        acc = at(38912, GB, QD * P)
        yq = at(40960, QD, GT)
        x1 = at(0, H)
        xres = at(1024, H)
        cn = at(2048, H)
        cT = at(3072, NT, P)
        ek = at(4096, OT, H)
        ekT = at(8192, NT, HID)
        gT = at(12288, HID)
        mt = at(12800, OT, P)
        qe = at(13312, NT, HID)
        qs = at(17408, OT, H)
        ob = at(21504, H)
        sq = at(22528, H)
        rnorm = at(23552, H)
        x2 = at(24576, H)
        x2T = at(25600, KC, P)
        mg = at(26624, P)
        mgT = at(26752, P)
        x3 = at(26880, H)
        wq = at(27904, HID)
        wk = at(28416, HID)
        ph = at(28928, HEADS, P)
        wvh = at(29952, HEADS, P)
        woh = at(30976, HEADS, P)
        rat = at(32000, KC, RA)
        bful = at(32544, H)

        rbuf = sb("rbuf", [P, GB, H])
        wdt = sb("wdt", [P, D_IN])
        tsb = sb("tsb", [P, TOK])
        a_sb = sb("a_sb", [P, DT, N])
        cbt = sb("cbt", [P, TT, N])
        cg = sb("cg", [P, GB, N])
        dsk = sb("dsk", [P, DT])
        idle = sb("idle", [P, 1])
        ident = sb("ident", [P, P])
        ones = sb("ones", [P, P])
        mhalf = sb("mhalf", [P, GB])
        ss3 = sb("ss3", [P, 3, TT])
        st1 = sb("st1", [P, GB, 2, 6])
        mv1 = sb("mv1", [P, GB, 2])
        ve1 = sb("ve1", [P, GB])
        bov = sb("bov", [P, 2])
        gs = sb("gs", [P, 1])
        km = sb("km", [P, OT])
        nkm = sb("nkm", [P, OT])
        ksum = sb("ksum", [P, OT])
        rk = sb("rk", [P, OT])
        qm = sb("qm", [P, 2, HEADS])
        qz = sb("qz", [P, 2, HEADS])
        qr = sb("qr", [P, 2, HEADS])
        gb = sb("gb", [P, 1])
        lg = sb("lg", [P, NE])
        nlm = sb("nlm", [P, 1])
        lex = sb("lex", [P, NE])
        cgt = sb("cgt", [P, NE, NE])
        cge = sb("cge", [P, NE, NE])
        upper = sb("upper", [P, NE, NE])
        lower = sb("lower", [P, NE, NE])
        rank = sb("rank", [P, NE])
        gate = sb("gate", [P, NE])
        gsum = sb("gsum", [P, 1])

        banks = [ctx.enter_context(nc.psum_tensor(f"banks{i}", [P, 2 * HALF], F32)) for i in range(4)]

        def bank(i):
            return banks[i // 2][:, (i % 2) * HALF:(i % 2 + 1) * HALF]

        def following(g, q):
            return (g, q + 1) if q < NQ - 1 else (g + 1, 0)

        def by_seq(ap):
            return ap.rearrange("p (b t) -> p b t", b=GB)

        consts0 = [(wxT, "WxT"), (wdt[0:R, :], "WdtT"), (a_sb[:, :, :], "A_log"),
                   (dsk[:, :], "D")]
        consts2 = [(wq, "WqT"), (wk, "WkT"), (wvh[0:DH], "Wvh"), (woh[0:DH], "Woh"), (rat, "RAT"),
                   (bful[0:NE * ER, :], "Bf"), (bov[:, 0:1], "bo"), (bov[:, 1:2], "g")]
        C0, C2 = 16 * len(consts0), 16 * len(consts2)

        def sync_tile(sp, mp, par):
            m = 2 * mp + par
            sp.wait_ge(S["x_mm"], 4 * m - 4 + X_MM)
            sp.wait_ge(S["conv_done"], 4 * m - 4 + CONV)
            sp.dma_start(wxc[par], a["WinX"][bass.ds(m, 1)].rearrange("a p k -> (a p) k"))\
                .then_inc(S[f"wx_loaded{par}"], 16)

        def sync_store_u(sp, mp, par):
            m = 2 * mp + par
            sp.wait_ge(S["u_done"], 4 * m + 4)
            sp.dma_start(u_d[bass.ds(m, 1)].rearrange("a p t -> (a p) t"), ust[par])\
                .then_inc(S[f"u_stored{par}"], 16)

        def sync_b(sp, g, j):
            sp.wait_ge(S["bm_ok"], 64 * g + 4 * j - 12 + BM)
            sp.dma_start(brep[:, 4 * j:4 * j + 4, :],
                         b_d[4 * j:4 * j + 4, bass.ds(g * GT, GT)].partition_broadcast(P))\
                .then_inc(S[f"brep_loaded{j}"], 16)

        def sync_step(sp, g, q, first=False):
            s = NQ * g + q
            if first:
                sync_b(sp, g, 0)
            sp.wait_ge(S["fin"], 4 * s - 4 + FIN)
            sp.dma_start(uq[q % 2], u_d[QD * q:QD * (q + 1), :, bass.ds(g * GT, GT)]
                         .rearrange("d p t -> p d t")).then_inc(S[f"u_loaded{q % 2}"], 16)
            if q == 0:
                sp.wait_ge(S["z_mm"], 16 * g + Z_MM)
                sp.dma_start(xg, a["xT"][:, :, bass.ds(g * GT, GT)]).then_inc(S["xg_loaded"], 16)

            def gate_weights(i):
                sp.wait_ge(S["z_mm"], 4 * s + i - 1 + Z_MM)
                sp.dma_start(wz[i % 2], a["WinZ"][QD * q + i]).then_inc(S[f"wz_loaded{i % 2}"], 16)

            gate_weights(0)
            gate_weights(1)
            if q == 0:
                for j in range(first, 4):
                    sync_b(sp, g, j)
            gate_weights(2)
            gate_weights(3)
            sp.wait_ge(S["o_mm"], 8 * s + ONE)
            sp.dma_start(wo, a["WoutT"][(q - 1) % NQ]).then_inc(S["wo_loaded"], 16)
            if q == 1:
                sp.wait_ge(S["ln_ok"], GB * (g + 1))
                sp.dma_start(x1_d[bass.ds(g, 1)].rearrange("a b p h -> p (a b) h"), rbuf[:, :, :])\
                    .then_inc(S["x1_stored"], 16)
                sp.wait_ge(S["x1_stored"], 16 * (g + 1))
                sp.dma_start(rbuf[:, :, :], a["x"][bass.ds(g, 1)].rearrange("a p b h -> (a p) b h"))\
                    .then_inc(S["r_loaded"], 16)

        def sync_store(sp, b):
            sp.wait_ge(S["x3_ok"], b + 1)
            sp.dma_start(out[bass.ds(b, 1)].rearrange("a p h -> (a p) h"), x3)\
                .then_inc(S["out_stored"], 16)

        def sync_context(sp, b):
            sp.wait_ge(S["k_mm"], 4 * b)
            sp.dma_start(cn, a["ctx"][bass.ds(b, 1)].rearrange("a p n -> (a p) n"))\
                .then_inc(S["cn_loaded"], 16)

        def sync_seq(sp, b, store=None, context=True):
            row = x1_d.rearrange("g b p h -> (g b) p h")[bass.ds(b + GB, 1)].rearrange("a p h -> (a p) h")
            sp.wait_ge(S["q_mm"], 8 * b)
            sp.dma_start(x1, row).then_inc(S["x1_loaded"], 16)
            sp.wait_ge(S["g_mm"], b)
            sp.dma_start(cT, a["ctxT"][bass.ds(b, 1)].rearrange("a p n c -> (a p) n c"))\
                .then_inc(S["ct_loaded"], 16)
            if store is not None:
                sync_store(sp, store)
            if context:
                sync_context(sp, b + 1)
            sp.wait_ge(S["y2_ok"], b)
            sp.dma_start(xres, row).then_inc(S["xres_loaded"], 16)

        def pe_dt(pe, g, q, i):
            d = QD * q + i
            nc.tensor.matmul(bank(4 + i % 2), wdt[:, d * P:(d + 1) * P], tsb[:, bass.ds(g * GT, GT)],
                             start=True, stop=True).then_inc(S["dt_mm"], 1)

        def pe_out(pe, s, c, ks, last_quad=False):
            for k in ks:
                if k == 0:
                    if last_quad or c >= 2:
                        pe.wait_ge(S["r_added"], 8 * s + c - 1 + R_ADD)
                    if c < 2:
                        pe.wait_ge(S["z_copied"], 4 * s if last_quad else 4 * s + 3 + c)
                last = nc.tensor.matmul(bank(6 + c % 2), yq[:, k, (c // 2) * P:(c // 2 + 1) * P],
                                        wo[:, k, (c % 2) * HALF:(c % 2 + 1) * HALF],
                                        start=(k == 0), stop=(k == QD - 1))
                if k == QD - 1:
                    last.then_inc(S["o_mm"], 1)

        def pe_step(pe, g, q, last=False):
            s = NQ * g + q
            if q == 0:
                pe.wait_ge(S["xg_loaded"], 16 * g + 16)
            for n in range(N):
                U = N * s + n

                def turn(b):
                    pe.wait_ge(S["acc_ok"], 4 * U + b - 1 + ACCD)
                    for i in range(QD):
                        last = nc.tensor.transpose(bank(2 + b % 2)[:, i * P:(i + 1) * P],
                                                   hb[n % 4][:, i * GT + b * P:i * GT + (b + 1) * P],
                                                   ident[:, :])
                    last.then_inc(S["t_done"], 1)

                def filler(part):
                    if n < 8:
                        i = n // 2
                        if n % 2 == 0 and part == 0:
                            pe.wait_ge(S[f"wz_loaded{i % 2}"], 16 * (2 * s + i // 2 + 1))
                            if i < 2:
                                pe.wait_ge(S["r_added"], 8 * s + i - 1 + R_ADD)
                            else:
                                pe.wait_ge(S["z_copied"], 4 * s + i - 1)
                        for k in range(4 * (n % 2) + 2 * part, 4 * (n % 2) + 2 * part + 2):
                            last = nc.tensor.matmul(bank(6 + i % 2), wz[i % 2][:, k, :], xg[:, k, :],
                                                    start=(k == 0), stop=(k == KC - 1))
                        if k == KC - 1:
                            last.then_inc(S["z_mm"], 1)
                    else:
                        if n == 8 and part == 0:
                            pe.wait_ge(S["wo_loaded"], 16 * s + 16)
                        pe_out(pe, s, n - 8, range(2 * part, 2 * part + 2))

                pe.wait_ge(S["scan_ok"], 4 * U + 4 + SCAN)
                turn(0)
                turn(1)
                filler(0)
                turn(2)
                turn(3)
                filler(1)
                if not last and n in (7, 11):
                    for i in ((0, 1) if n == 7 else (2, 3)):
                        if i >= 2:
                            pe.wait_ge(S["dt_ok"], 4 * (s + 1) + i - 1)
                        else:
                            pe.wait_ge(S["fin1"], 4 * s + i - 1 + FIN1)
                        pe_dt(pe, *following(g, q), i)
            pe.wait_ge(S["acc_ok"], 4 * (N * s + N) + ACCD)
            for i in range(QD):
                if i < 2 and not last:
                    pe.wait_ge(S["dt_ok"], 4 * (s + 1) + 3 + i)
                else:
                    pe.wait_ge(S["fin1"], 4 * s + i - 1 + FIN1)
                for b in range(GB):
                    last = nc.tensor.transpose(bank(4 + i % 2)[:, b * P:(b + 1) * P],
                                               acc[:, b, i * P:(i + 1) * P], ident[:, :])
                last.then_inc(S["yt_mm"], 1)

        def pe_keys(pe, b, o):
            if o == 0:
                pe.wait_ge(S["cn_loaded"], 16 * b + 16)
            else:
                pe.wait_ge(S["k_exp"], 4 * b + o)
            for h in range(2):
                last = nc.tensor.matmul(bank(2 + h), wk[:, o * P:(o + 1) * P],
                                        cn[:, h * HALF:(h + 1) * HALF], start=True, stop=True)
            last.then_inc(S["k_mm"], 1)

        def pe_keys_turn(pe, b, t):
            if t == 0:
                pe.wait_ge(S["k_exp"], 4 * b + 4)
                pe.wait_ge(S["qs_ok"], 8 * b)
            elif t == 1:
                pe.wait_ge(S["mt_ok"], b)
            else:
                pe.wait_ge(S["et_ok"], 8 * b + t - 1)
            dst = bank(4 + 2 * (t % 2))
            for o in range(OT):
                last = nc.tensor.transpose(dst[:, o * P:(o + 1) * P], ek[:, o, t * P:(t + 1) * P],
                                           ident[:, :])
            last.then_inc(S["et_mm"], 1)

        def pe_context(pe, b, ts):
            if ts[0] == 0:
                pe.wait_ge(S["ct_loaded"], 16 * b + 16)
                pe.wait_ge(S["et_ok"], 8 * b + 8)
            for t in ts:
                last = nc.tensor.matmul(bank(6), cT[:, t, :], ekT[:, t, :], start=(t == 0),
                                        stop=(t == NT - 1))
            if ts[-1] == NT - 1:
                last.then_inc(S["g_mm"], 1)

        def pe_values(pe, b):
            pe.wait_ge(S["g_ok"], b + 1)
            for h in range(HEADS):
                rows = slice(DH * (h % 2), DH * (h % 2 + 1))
                last = nc.tensor.matmul(bank(6)[rows, (h // 2) * P:(h // 2 + 1) * P],
                                        gT[:, h * DH:(h + 1) * DH], ph[:, h, :], start=True, stop=True)
            last.then_inc(S["mt_mm"], 1)

        def pe_query(pe, b, t):
            if t == 0:
                pe.wait_ge(S["x1_loaded"], 16 * b + 16)
            pe.wait_ge(S["q_sub"], 8 * b + max(t - 1, 0))
            nc.tensor.matmul(bank(t % 2), x1[:, t * P:(t + 1) * P], wq, start=True, stop=True)\
                .then_inc(S["q_mm"], 1)

        def pe_query_turn(pe, b, r):
            pe.wait_ge(S["q_norm"], 8 * b + r + 1)
            if r == 0:
                pe.wait_ge(S["et_ok"], 8 * b + 7)
            else:
                pe.wait_ge(S["qs_ok"], 8 * b + r)
            for o in range(OT):
                last = nc.tensor.transpose(bank(4)[:, o * P:(o + 1) * P], qe[:, r, o * P:(o + 1) * P],
                                           ident[:, :])
            last.then_inc(S["qt_mm"], 1)

        def pe_sequence(pe, b, keys, tail):
            for t in range(SLOTS):
                if t < NT:
                    pe_query(pe, b, t)
                if keys and t in KEY_SLOTS:
                    pe_keys(pe, b + 1, KEY_SLOTS.index(t))
                if t < 4:
                    pe_keys_turn(pe, b, 2 * t)
                    pe_keys_turn(pe, b, 2 * t + 1)
                if tail and t in PE_TAIL:
                    PE_TAIL[t](pe, b - 1)
                if 4 <= t < 8:
                    pe_context(pe, b, (2 * t - 8, 2 * t - 7))
                if t >= 3:
                    pe_query_turn(pe, b, t - 3)
                if t == 8:
                    pe_values(pe, b)
                if tail and t in PE_TAIL_LATE:
                    PE_TAIL_LATE[t](pe, b - 1)

        def pe_attend(pe, b, h):
            if h == 0:
                pe.wait_ge(S["mt_ok"], b + 1)
                pe.wait_ge(S["qs_ok"], 8 * b + 8)
            pe.wait_ge(S["x3_add"], 2 * b + ONE)
            for o in range(OT):
                last = nc.tensor.matmul(bank(5 + 2 * h), mt[:, o, :], qs[:, o, h * HALF:(h + 1) * HALF],
                                        start=(o == 0), stop=(o == OT - 1))
            last.then_inc(S["out_mm"], 1)

        def pe_squares(pe, b, h):
            pe.wait_ge(S["sq_ok"], 2 * b + h + 1)
            nc.tensor.matmul(bank(5 + 2 * h), ones[:, :], sq[:, h * HALF:(h + 1) * HALF],
                             start=True, stop=True).then_inc(S["ssq_mm"], 1)

        def pe_x2_turn(pe, b):
            pe.wait_ge(S["x2_ok"], b + 1)
            pe.wait_ge(S["ssq_ln"], 2 * b + 2)
            for k in range(KC):
                last = nc.tensor.transpose(bank(5 + 2 * (k // 4))[:, k % 4 * P:(k % 4 + 1) * P],
                                           x2[:, k * P:(k + 1) * P], ident[:, :])
                if k % 4 == 3:
                    last.then_inc(S["x2t_mm"], 1)

        def pe_router(pe, b):
            pe.wait_ge(S["x2t_ok"], 2 * b + 2)
            for k in range(KC):
                last = nc.tensor.matmul(bank(5)[:, 0:RA], x2T[:, k, :], rat[:, k, :], start=(k == 0),
                                        stop=(k == KC - 1))
            last.then_inc(S["ra_mm"], 1)

        def pe_gated(pe, b):
            pe.wait_ge(S["mg_ok"], b + 1)
            nc.tensor.transpose(bank(7)[:, 0:P], mg, ident[:, :]).then_inc(S["mgt_mm"], 1)

        def pe_experts(pe, b):
            pe.wait_ge(S["mgt_ok"], b + 1)
            for h in range(2):
                nc.tensor.matmul(bank(5 + 2 * h), mgT, bful[:, h * HALF:(h + 1) * HALF], start=True,
                                 stop=True).then_inc(S["delta_mm"], 1)

        PE_TAIL = {
            0: lambda pe, b: pe_attend(pe, b, 0),
            1: lambda pe, b: pe_attend(pe, b, 1),
            2: lambda pe, b: (pe_squares(pe, b, 0), pe_squares(pe, b, 1)),
            9: pe_experts,
        }
        PE_TAIL_LATE = {5: pe_x2_turn, 6: pe_router, 8: pe_gated}

        def act_softplus(act, g, q, tiles):
            s = NQ * g + q
            if tiles[0] == 0:
                act.wait_ge(S["dtu_ok"], s + ONE)
            for i in tiles:
                d = dt[q % 2][:, i, :]
                act.wait_ge(S["dt_mm"], 4 * s + i + 1)
                nc.scalar.activation(d, bank(4 + i % 2), ACT.Abs).then_inc(S["dt_abs"], 1)
                act.wait_ge(S["dt_abs"], 4 * s + i + 1)
                nc.scalar.activation(d, d, ACT.Exp, scale=-1.0).then_inc(S["dt_exp"], 1)
                act.wait_ge(S["dt_exp"], 4 * s + i + 1)
                nc.scalar.activation(d, d, ACT.Ln, bias=1.0).then_inc(S["dt_ln"], 1)

        def act_step(act, g, q, last=False):
            s = NQ * g + q
            for n in range(N):
                for i in range(QD):
                    e = 4 * (N * s + n) + i
                    if n == 0:
                        act.wait_ge(S["dt_ok"], 4 * s + i + 1)
                    act.wait_ge(S["scan_ok"], e - 1 + SCAN)
                    nc.scalar.activation(by_seq(bank(i % 2))[:, :, 1:SEQ],
                                         by_seq(dt[q % 2][:, i, :])[:, :, 1:SEQ], ACT.Exp,
                                         scale=a_sb[:, QD * q + i, n:n + 1]).then_inc(S["exp_ok"], 1)
                if n in (3, 5, 7, 9):
                    i = (n - 3) // 2
                    if i == 0:
                        act.wait_ge(S["fin"], 4 * s + FIN)
                    act.wait_ge(S["z_mm"], 4 * s + i + 1 + Z_MM)
                    nc.scalar.activation(zs[:, i, :], bank(6 + i % 2), ACT.Copy).then_inc(S["z_copied"], 1)
                if n == 10:
                    act.wait_ge(S["z_copied"], 4 * s + 4)
                    nc.scalar.activation(zs, zs, ACT.Silu).then_inc(S["z_silu"], 1)
                    act.preload_act_table_set(LN_EXP_SET)
                if not last and n in (11, 13):
                    act_softplus(act, *following(g, q), (0, 1) if n == 11 else (2, 3))

        def act_keys(act, b, o):
            act.wait_ge(S["k_neg"], 4 * b + o + 1)
            if o == 0:
                act.wait_ge(S["et_mm"], 8 * b)
                act.wait_ge(S["rk1"], b)
            nc.scalar.activation(ek[:, o, :], banks[1][:, :], ACT.Exp, bias=nkm[:, o:o + 1],
                                 accum_out=ksum[:, o:o + 1]).then_inc(S["k_exp"], 1)

        def act_sequence(act, b, keys, tail):
            for t in range(SLOTS):
                if t < 4:
                    for r in (2 * t, 2 * t + 1):
                        act.wait_ge(S["et_mm"], 8 * b + r + 1)
                        if r == 0:
                            act.wait_ge(S["g_mm"], b)
                        nc.scalar.activation(ekT[:, r, :], bank(4 + 2 * (r % 2)), ACT.Copy)\
                            .then_inc(S["et_ok"], 1)
                if keys and t - 1 in KEY_SLOTS:
                    act_keys(act, b + 1, KEY_SLOTS.index(t - 1))
                if t < NT:
                    act.wait_ge(S["q_sub"], 8 * b + t + 1)
                    nc.scalar.activation(qe[:, t, :], qe[:, t, :], ACT.Exp).then_inc(S["q_exp"], 1)
                if tail and t in ACT_TAIL:
                    ACT_TAIL[t](act, b - 1)
                if t >= 3:
                    r = t - 3
                    act.wait_ge(S["qt_mm"], 8 * b + r + 1)
                    if r == 0:
                        act.wait_ge(S["out_mm"], 2 * b)
                    nc.scalar.activation(qs[:, :, r * P:(r + 1) * P],
                                         bank(4).rearrange("p (o n) -> p o n", o=OT), ACT.Copy)\
                        .then_inc(S["qs_ok"], 1)
                if t == 7:
                    act.wait_ge(S["g_mm"], b + 1)
                    act.wait_ge(S["mt_mm"], b)
                    nc.scalar.activation(gT, bank(6), ACT.Copy).then_inc(S["g_ok"], 1)
                if tail and t in ACT_TAIL_LATE:
                    ACT_TAIL_LATE[t](act, b - 1)

        def act_attended(act, b, h):
            half = slice(h * HALF, (h + 1) * HALF)
            act.wait_ge(S["out_mm"], 2 * b + h + 1)
            if h == 0:
                act.wait_ge(S["gs_ok"], 2)
                act.wait_ge(S["y2_ok"], b)
                act.wait_ge(S["ssq_mm"], 2 * b)
            nc.scalar.activation(sq[:, half], bank(5 + 2 * h), ACT.Square, bias=bov[:, 0:1])
            nc.scalar.activation(ob[:, half], bank(5 + 2 * h), ACT.Identity, bias=gb[:, 0:1],
                                 scale=gs[:, 0:1]).then_inc(S["sq_ok"], 1)

        def act_norm(act, b):
            act.wait_ge(S["y2a"], b)
            for h in range(2):
                act.wait_ge(S["ssq_mm"], 2 * b + h + 1)
                nc.scalar.activation(rnorm[:, h * HALF:(h + 1) * HALF], bank(5 + 2 * h), ACT.Ln)\
                    .then_inc(S["ssq_ln"], 1)
            act.wait_ge(S["ssq_ln"], 2 * b + 2)
            nc.scalar.activation(rnorm, rnorm, ACT.Exp, scale=-0.5).then_inc(S["rnorm_ok"], 1)

        def act_x2_turned(act, b):
            for h in range(2):
                act.wait_ge(S["x2t_mm"], 2 * b + h + 1)
                if h == 0:
                    act.wait_ge(S["ra_mm"], b)
                nc.scalar.activation(x2T[:, 4 * h:4 * h + 4, :],
                                     bank(5 + 2 * h).rearrange("p (k t) -> p k t", k=4), ACT.Copy)\
                    .then_inc(S["x2t_ok"], 1)

        def act_gate(act, b):
            act.wait_ge(S["lg_neg"], b + 1)
            nc.scalar.activation(lex[:, :], lg[:, :], ACT.Exp, bias=nlm[:, :]).then_inc(S["gate_exp"], 1)

        def act_gated_turned(act, b):
            act.wait_ge(S["mgt_mm"], b + 1)
            nc.scalar.activation(mgT, bank(7)[:, 0:P], ACT.Copy).then_inc(S["mgt_ok"], 1)

        ACT_TAIL = {
            0: lambda act, b: act_attended(act, b, 0),
            1: lambda act, b: act_attended(act, b, 1),
            2: act_norm,
            7: act_gate,
        }
        ACT_TAIL_LATE = {5: act_x2_turned, 8: act_gated_turned}

        def pool_rstd(pool, g):
            pool.wait_ge(S["ln_eps"], g + 1)
            nc.gpsimd.tensor_tensor(ve1[:, :], ve1[:, :], mhalf[:, 0:GB], ALU.pow).then_inc(S["ln_rstd"], 1)

        def pool_sequence(pool, b, tail):
            for t in range(NT):
                pool.wait_ge(S["q_rec"], 8 * b + t + 1)
                v = qe[:, t, :].rearrange("p (h d) -> p h d", h=HEADS)
                nc.gpsimd.tensor_tensor(v, v, qr[:, t % 2, :][:, :, None].broadcast_to([P, HEADS, DH]),
                                        ALU.mult).then_inc(S["q_norm"], 1)
                if tail and t == 2:
                    pool_rstd2(pool, b - 1, 0)
            if tail:
                pool_rstd2(pool, b - 1, 1)

        def pool_rstd2(pool, b, k):
            pool.wait_ge(S["l2_eps"], 2 * b + k + 1)
            nc.gpsimd.tensor_tensor(ve1[:, 0:1], ve1[:, 0:1], mhalf[:, 0:1], ALU.pow)\
                .then_inc(S["l2_rstd"], 1)

        def dve_dt(dve, g, q, tiles):
            s = NQ * g + q
            for i in tiles:
                d = dt[q % 2][:, i, :]
                dve.wait_ge(S["dt_ln"], 4 * s + i + 1)
                nc.vector.scalar_tensor_tensor(d, bank(4 + i % 2), 0.0, d, ALU.max, ALU.add)\
                    .then_inc(S["dt_ok"], 1)

        def dve_scan(dve, g, q, n, i):
            U = N * (NQ * g + q) + n
            if i == 0:
                dve.wait_ge(S["bm_ok"], U + 1 + BM)
            dve.wait_ge(S["exp_ok"], 4 * U + i + 1)
            h = hb[n % 4][:, i * GT:(i + 1) * GT]
            nc.vector.tensor_tensor_scan(h, bank(i % 2), h, 0.0, ALU.mult, ALU.add)\
                .then_inc(S["scan_ok"], 1)

        def dve_acc(dve, g, q, n, b):
            s = NQ * g + q
            k = 4 * (N * s + n) + b
            dve.wait_ge(S["t_done"], k + 1 + T_DONE)
            c = cg[:, b, n:n + 1]
            if n == 0:
                if b == 0:
                    dve.wait_ge(S["yt_mm"], 4 * s + ONE)
                    dve.wait_ge(S["cg_ok"], g + 1)
                last = nc.vector.tensor_scalar(acc[:, b, :], bank(2 + b % 2), c, None, ALU.mult)
            else:
                dve.wait_ge(S["acc_ok"], k - 3 + ACCD)
                last = nc.vector.scalar_tensor_tensor(acc[:, b, :], bank(2 + b % 2), c, acc[:, b, :],
                                                      ALU.mult, ALU.add)
            last.then_inc(S["acc_ok"], 1)

        def dve_out(dve, s, c):
            v = rbuf[:, c // 2, (c % 2) * HALF:(c % 2 + 1) * HALF]
            dve.wait_ge(S["o_mm"], 8 * s + c + 1 + ONE)
            dve.wait_ge(S["r_added"], 8 * s + R_ADD)
            nc.vector.tensor_tensor(v, bank(6 + c % 2), v, ALU.add).then_inc(S["r_added"], 1)

        def dve_ln_stats(dve, g):
            dve.wait_ge(S["r_added"], 8 * (NQ * g + 1) + R_ADD)
            for t in range(GB):
                for h in range(2):
                    nc.vector.bn_stats(st1[:, t, h, :], rbuf[:, t, h * HALF:(h + 1) * HALF])\
                        .then_inc(S["ln_stats"], 1)
            dve.wait_ge(S["ln_stats"], 8 * g + 8)
            nc.vector.memset(idle[:, :], 0.0)
            for t in range(GB):
                nc.vector.bn_aggr(mv1[:, t, :], st1[:, t, :, :].rearrange("p a s -> p (a s)"))\
                    .then_inc(S["ln_aggr"], 1)
            dve.wait_ge(S["ln_aggr"], 4 * g + 4)
            nc.vector.tensor_scalar(ve1[:, :], mv1[:, :, 1:2].rearrange("p a b -> p (a b)"), LN_EPS, None,
                                    ALU.add).then_inc(S["ln_eps"], 1)

        def dve_ln_apply(dve, g):
            dve.wait_ge(S["ln_rstd"], g + 1)
            for t in range(GB):
                nc.vector.tensor_scalar(rbuf[:, t, :], rbuf[:, t, :], mv1[:, t, 0:1], ve1[:, t:t + 1],
                                        ALU.subtract, ALU.mult).then_inc(S["ln_ok"], 1)

        def dve_group(dve, g, last):
            dve.wait_ge(S["acc_ok"], 64 * 4 * g + ACCD)
            nc.vector.tensor_copy(cg[:, :, :], cbt[:, bass.ds(GB * g, GB), :]).then_inc(S["cg_ok"], 1)
            for q in range(NQ):
                dve_step(dve, g, q, last and q == NQ - 1)

        def dve_step(dve, g, q, last):
            s = NQ * g + q
            for n in range(N):
                if n < N - 2:
                    scans = [(g, q, n + 2, i) for i in range(QD)]
                else:
                    scans = [] if last else [(*following(g, q), n + 2 - N, i) for i in range(QD)]
                if q == 1 and n == 8:
                    dve.wait_ge(S["r_loaded"], 16 * g + 16)
                for part in range(2):
                    dve_acc(dve, g, q, n, 2 * part)
                    dve_acc(dve, g, q, n, 2 * part + 1)
                    for unit in scans[2 * part:2 * part + 2]:
                        dve_scan(dve, *unit)
                if n >= 8:
                    dve_out(dve, s, n - 8)
                if not last and n in (10, 12):
                    dve_dt(dve, *following(g, q), (0, 1) if n == 10 else (2, 3))
                if q == 1 and n == 1:
                    dve_ln_stats(dve, g)
                if q == 1 and n == 3:
                    dve_ln_apply(dve, g)
            dve.wait_ge(S["o_mm"], 8 * s + 8 + ONE)
            dve.wait_ge(S["z_silu"], s + 1)

            def skip(i):
                dve.wait_ge(S["yt_mm"], 4 * s + i + 1 + ONE)
                nc.vector.scalar_tensor_tensor(yq[:, i, :], uq[q % 2][:, i, :],
                                               dsk[:, QD * q + i:QD * q + i + 1], bank(4 + i % 2),
                                               ALU.mult, ALU.add).then_inc(S["fin1"], 1)

            skip(0)
            for i in range(QD):
                if i < QD - 1:
                    skip(i + 1)
                dve.wait_ge(S["fin1"], 4 * s + i + 1 + FIN1)
                nc.vector.tensor_tensor(yq[:, i, :], yq[:, i, :], zs[:, i, :], ALU.mult)\
                    .then_inc(S["fin"], 1)

        def dve_keys(dve, b, o):
            dve.wait_ge(S["k_mm"], 4 * b + o + 1)
            nc.vector.tensor_reduce(km[:, o:o + 1], banks[1][:, :], AX_X, ALU.max).then_inc(S["k_max"], 1)
            dve.wait_ge(S["k_max"], 4 * b + o + 1)
            if o == 0:
                dve.wait_ge(S["k_exp"], 4 * b)
            nc.vector.tensor_scalar(nkm[:, o:o + 1], km[:, o:o + 1], -1.0, None, ALU.mult)\
                .then_inc(S["k_neg"], 1)

        def dve_keys_scale(dve, b):
            dve.wait_ge(S["k_exp"], 4 * b + 4)
            nc.vector.reciprocal(rk[:, :], ksum[:, :]).then_inc(S["rk1"], 1)
            dve.wait_ge(S["rk1"], b + 1)
            nc.vector.tensor_scalar(rk[:, :], rk[:, :], DH ** -0.5, None, ALU.mult).then_inc(S["rk2"], 1)

        def dve_values(dve, b):
            dve.wait_ge(S["rk2"], b + 1)
            dve.wait_ge(S["mt_mm"], b + 1)
            dve.wait_ge(S["out_mm"], 2 * b)
            nc.vector.tensor_tensor(mt, bank(6).rearrange("p (o c) -> p o c", o=OT),
                                    rk[:, :][:, :, None].broadcast_to([P, OT, P]), ALU.mult)\
                .then_inc(S["mt_ok"], 1)

        def dve_sequence(dve, b, keys, tail):
            def start(t):
                ps = bank(t % 2).rearrange("p (h d) -> p h d", h=HEADS)
                dve.wait_ge(S["q_mm"], 8 * b + t + 1)
                nc.vector.tensor_reduce(qm[:, t % 2, :], ps, AX_X, ALU.max).then_inc(S["q_max"], 1)
                dve.wait_ge(S["q_max"], 8 * b + t + 1)
                if tail:
                    dve.wait_ge(S["qt_mm"], 8 * b - 7 + t)
                nc.vector.tensor_tensor(qe[:, t, :].rearrange("p (h d) -> p h d", h=HEADS), ps,
                                        qm[:, t % 2, :][:, :, None].broadcast_to([P, HEADS, DH]),
                                        ALU.subtract).then_inc(S["q_sub"], 1)

            def denominator(t):
                dve.wait_ge(S["q_exp"], 8 * b + t + 1)
                nc.vector.tensor_reduce(qz[:, t % 2, :], qe[:, t, :].rearrange("p (h d) -> p h d", h=HEADS),
                                        AX_X, ALU.add).then_inc(S["q_sum"], 1)
                dve.wait_ge(S["q_sum"], 8 * b + t + 1)
                if t >= 2:
                    dve.wait_ge(S["q_norm"], 8 * b + t - 1)
                nc.vector.reciprocal(qr[:, t % 2, :], qz[:, t % 2, :]).then_inc(S["q_rec"], 1)

            for t in range(SLOTS):
                if t < NT:
                    start(t)
                if 1 <= t <= NT:
                    denominator(t - 1)
                if t == 8:
                    dve_values(dve, b)
                if keys and t in KEY_SLOTS:
                    dve_keys(dve, b + 1, KEY_SLOTS.index(t))
                if tail and t in DVE_TAIL:
                    DVE_TAIL[t](dve, b - 1)
                if t == 2:
                    dve_keys_scale(dve, b)

        def dve_norm_stats(dve, b, k, src):
            for h in range(2):
                nc.vector.bn_stats(st1[:, 0, h, :], src[:, h * HALF:(h + 1) * HALF])\
                    .then_inc(S["l2_stats"], 1)
            dve.wait_ge(S["l2_stats"], 4 * b + 2 * k + 2)
            nc.vector.memset(idle[:, :], 0.0)
            nc.vector.bn_aggr(mv1[:, 0, :], st1[:, 0, :, :].rearrange("p a s -> p (a s)"))\
                .then_inc(S["l2_aggr"], 1)
            dve.wait_ge(S["l2_aggr"], 2 * b + k + 1)
            nc.vector.tensor_scalar(ve1[:, 0:1], mv1[:, 0, 1:2], LN_EPS, None, ALU.add)\
                .then_inc(S["l2_eps"], 1)

        def dve_norm_apply(dve, b, k, src, dst, done):
            dve.wait_ge(S["l2_rstd"], 2 * b + k + 1)
            nc.vector.tensor_scalar(dst, src, mv1[:, 0, 0:1], ve1[:, 0:1], ALU.subtract, ALU.mult)\
                .then_inc(S[done], 1)

        def dve_second_sum(dve, b):
            dve.wait_ge(S["rnorm_ok"], b + 1)
            dve.wait_ge(S["sq_ok"], 2 * b + 2)
            nc.vector.scalar_tensor_tensor(ob, rnorm, 1e12, ob, ALU.min, ALU.mult).then_inc(S["y2a"], 1)
            dve.wait_ge(S["y2a"], b + 1)
            dve.wait_ge(S["xres_loaded"], 16 * b + 16)
            dve.wait_ge(S["x3_add"], 2 * b + ONE)
            nc.vector.tensor_tensor(x2, ob, xres, ALU.add).then_inc(S["y2_ok"], 1)
            dve.wait_ge(S["y2_ok"], b + 1)
            dve_norm_stats(dve, b, 0, x2)

        def dve_second_norm(dve, b):
            dve_norm_apply(dve, b, 0, x2, x2, "x2_ok")

        def dve_gates(dve, b):
            step = [0]

            def small(ins):
                step[0] += 1
                ins.then_inc(S["gate_step"], 1)
                dve.wait_ge(S["gate_step"], GATE_STEPS * b + step[0])

            ra = bank(5)[:, 0:RA]
            of_j = lg[:, :][:, None, :].broadcast_to([P, NE, NE])
            of_e = lg[:, :][:, :, None].broadcast_to([P, NE, NE])
            dve.wait_ge(S["ra_mm"], b + 1)
            small(nc.vector.tensor_copy(lg[:, :], ra[:, 0:NE]))
            small(nc.vector.tensor_reduce(nlm[:, :], lg[:, :], AX_X, ALU.max))
            nc.vector.tensor_scalar(nlm[:, :], nlm[:, :], -1.0, None, ALU.mult).then_inc(S["lg_neg"], 1)
            small(nc.vector.tensor_tensor(cgt[:, :, :], of_j, of_e, ALU.is_gt))
            small(nc.vector.tensor_tensor(cge[:, :, :], of_j, of_e, ALU.is_ge))
            small(nc.vector.tensor_tensor(cgt[:, :, :], cgt[:, :, :], upper[:, :, :], ALU.mult))
            small(nc.vector.tensor_tensor(cge[:, :, :], cge[:, :, :], lower[:, :, :], ALU.mult))
            small(nc.vector.tensor_tensor(cgt[:, :, :], cgt[:, :, :], cge[:, :, :], ALU.add))
            small(nc.vector.tensor_reduce(rank[:, :], cgt[:, :, :], AX_X, ALU.add))
            dve.wait_ge(S["gate_exp"], b + 1)
            small(nc.vector.scalar_tensor_tensor(gate[:, :], rank[:, :], 2.0, lex[:, :], ALU.is_lt, ALU.mult))
            small(nc.vector.tensor_reduce(gsum[:, :], gate[:, :], AX_X, ALU.add))
            small(nc.vector.reciprocal(gsum[:, :], gsum[:, :]))
            small(nc.vector.tensor_scalar(gate[:, :], gate[:, :], gsum[:, :], 4.0, ALU.mult, ALU.mult))
            nc.vector.tensor_tensor(mg[:, 0:NE * ER].rearrange("p (e r) -> p e r", e=NE),
                                    ra[:, NE:RA].rearrange("p (e r) -> p e r", e=NE),
                                    gate[:, :][:, :, None].broadcast_to([P, NE, ER]), ALU.mult)\
                .then_inc(S["mg_ok"], 1)
            assert step[0] == GATE_STEPS

        def dve_third_sum(dve, b):
            dve.wait_ge(S["out_stored"], 16 * b + ONE)
            for h in range(2):
                half = slice(h * HALF, (h + 1) * HALF)
                dve.wait_ge(S["delta_mm"], 2 * b + h + 1)
                nc.vector.tensor_tensor(x3[:, half], bank(5 + 2 * h), x2[:, half], ALU.add)\
                    .then_inc(S["x3_add"], 1)

        def dve_third_stats(dve, b):
            dve.wait_ge(S["x3_add"], 2 * b + 2 + ONE)
            dve_norm_stats(dve, b, 1, x3)

        DVE_TAIL = {
            3: dve_second_sum,
            4: dve_second_norm,
            7: dve_gates,
            9: dve_third_sum,
            10: lambda dve, b: (dve_third_stats(dve, b), dve_norm_apply(dve, b, 1, x3, x3, "x3_ok")),
        }

        block = ctx.enter_context(nc.Block())

        @block.sync
        def _(sp):
            for name in ("out_stored", "u_stored0", "u_stored1"):
                sp.sem_inc(S[name], ONE)
            for i in range(NG):
                sp.dma_start(xT[:, :, i * GT:(i + 1) * GT], a["xT"][:, :, i * GT:(i + 1) * GT])\
                    .then_inc(S[f"xt_loaded{i}"], 16)
                if i == 0:
                    sync_tile(sp, 0, 0)
                    for dst, name in consts0:
                        sp.dma_start(dst, a[name]).then_inc(S["const_loaded"], 16)
            sync_tile(sp, 0, 1)
            sp.wait_ge(S["rows_set"], 1)
            sp.dma_start(wdt[96:97, :], a["b_dt"]).then_inc(S["bdt_loaded"], 16)
            with nc.sync.Fori(1, DT // 2) as mp:
                for par in range(2):
                    sync_tile(sp, mp, par)
                    sync_store_u(sp, mp - 1, par)
            for par in range(2):
                sync_store_u(sp, DT // 2 - 1, par)
            sp.wait_ge(S["bt_rows"], 1)
            sp.dma_start(b_d[:, 0:GT], tsb[R:R + N, 0:GT]).then_inc(S["b_stored"], 16)

            sp.wait_ge(S["b_stored"], 16)
            sp.wait_ge(S["u_stored0"], 8 * 16 + ONE)
            sp.wait_ge(S["u_stored1"], 8 * 16 + ONE)
            sp.wait_ge(S["phase0_c"], 1)
            sp.wait_ge(S["bt_mm"], TT // 4)
            sync_step(sp, 0, 0, first=True)
            sp.wait_ge(S["bt_rows"], TT // 4)
            sp.dma_start(b_d[:, GT:TOK], tsb[R:R + N, GT:TOK]).then_inc(S["b_stored"], 16)
            for q in range(1, NQ):
                sync_step(sp, 0, q)
            sp.wait_ge(S["b_stored"], 32)
            with nc.sync.Fori(1, NG) as g:
                for q in range(NQ):
                    sync_step(sp, g, q)
            sp.wait_ge(S["o_mm"], 8 * NG * NQ + ONE)
            sp.dma_start(wo, a["WoutT"][NQ - 1]).then_inc(S["wo_loaded"], 16)

            sp.wait_ge(S["fin"], 4 * NG * NQ + FIN)
            sp.wait_ge(S["x1_stored"], 16 * NG)
            for dst, name in consts2:
                sp.dma_start(dst, a[name]).then_inc(S["p2_const"], 16)
            sync_context(sp, 0)
            for b in range(2):
                sync_seq(sp, b)
            sp.wait_ge(S["ln_ok"], GB * (NG + 1))
            sp.dma_start(x1_d[NG].rearrange("b p h -> p b h"), rbuf[:, :, :]).then_inc(S["x1_stored"], 16)
            sp.wait_ge(S["x1_stored"], 16 * (NG + 1))
            with nc.sync.Fori(2, BATCH - 1) as b:
                sync_seq(sp, b, store=b - 2)
            sync_seq(sp, BATCH - 1, store=BATCH - 3, context=False)
            sync_store(sp, BATCH - 2)
            sync_store(sp, BATCH - 1)
            sp.wait_ge(S["out_stored"], 16 * BATCH + ONE)

        @block.tensor
        def _(pe):
            pe.sem_inc(S["x_mm"], X_MM)
            for name in ("ss_mm", "o_mm", "yt_mm"):
                pe.sem_inc(S[name], ONE)
            pe.sem_inc(S["t_done"], T_DONE)
            pe.sem_inc(S["z_mm"], Z_MM)

            def through_wx(mp, par):
                m = 2 * mp + par
                for j in range(4):
                    pe.wait_ge(S["u_done"], 4 * m + j + 1)
                    pe.wait_ge(S["ss_added"], 4 * m + j + 1)
                    for i in range(4):
                        t = 4 * j + i
                        last = nc.tensor.matmul(bank(4 + j)[:, i * SS:(i + 1) * SS],
                                                ust[par][:, t * P:(t + 1) * P],
                                                wxT[:, bass.ds(m, 1), :].rearrange("p a s -> p (a s)"),
                                                start=True, stop=True)
                    last.then_inc(S["ss_mm"], 1)

            pe.wait_ge(S["const_loaded"], C0)
            with nc.tensor.Fori(0, DT // 2) as mp:
                for par in range(2):
                    m = 2 * mp + par
                    pe.wait_ge(S[f"wx_loaded{par}"], 16 * mp + 16)
                    for tg in range(NG):
                        if par == 0:
                            pe.wait_ge(S[f"xt_loaded{tg}"], 16)
                        if par == 1 and tg == 2:
                            through_wx(mp, 0)
                        pe.wait_ge(S["conv_done"], 4 * m + tg - 3 + CONV)
                        for k in range(KC):
                            last = nc.tensor.matmul(bank(tg), wx[par][:, k, :],
                                                    xT[:, k, tg * GT:(tg + 1) * GT],
                                                    start=(k == 0), stop=(k == KC - 1))
                        last.then_inc(S["x_mm"], 1)
                through_wx(mp, 1)
            pe.wait_ge(S["pool_const"], 1)
            pe.wait_ge(S["ss_normed"], 3)
            for j in range(TT // 4):
                for i in range(4):
                    last = nc.tensor.transpose(bank(BT_BANKS[j])[0:SS, i * P:(i + 1) * P],
                                               ssacc[:, 4 * j + i, :], ident[:, :])
                last.then_inc(S["bt_mm"], 1)

            pe.wait_ge(S["bt_rows"], 1)
            pe.wait_ge(S["bdt_loaded"], 16)
            pe.wait_ge(S["rows_set"], 2)
            for i in range(QD):
                if i >= 2:
                    pe.wait_ge(S["dt_ok"], i - 1)
                pe_dt(pe, 0, 0, i)
            with nc.tensor.Fori(0, NG - 1) as g:
                for q in range(NQ):
                    pe_step(pe, g, q)
            for q in range(NQ):
                pe_step(pe, NG - 1, q, last=(q == NQ - 1))
            pe.wait_ge(S["fin"], 4 * NG * NQ + FIN)
            pe.wait_ge(S["wo_loaded"], 16 * (NG * NQ + 1))
            for c in range(4):
                pe_out(pe, NG * NQ, c, range(4), last_quad=True)

            pe.wait_ge(S["p2_const"], C2)
            for h in range(HEADS):
                last = nc.tensor.matmul(bank(h // 4)[:, (h % 4) * P:(h % 4 + 1) * P], wvh[0:DH, h, :],
                                        woh[0:DH, h, :], start=True, stop=True)
            last.then_inc(S["ph_mm"], 1)
            for o in range(OT):
                pe_keys(pe, 0, o)
                pe_out(pe, NG * NQ, 4 + o, range(4), last_quad=True)
            pe.wait_ge(S["rows_set"], 4)
            pe.wait_ge(S["ph_ok"], 1)
            pe.wait_ge(S["r_added"], 8 * (NG * NQ + 1) + R_ADD)
            pe_sequence(pe, 0, keys=True, tail=False)
            with nc.tensor.Fori(1, BATCH - 1) as b:
                pe_sequence(pe, b, keys=True, tail=True)
            pe_sequence(pe, BATCH - 1, keys=False, tail=True)
            for _, part in sorted({**PE_TAIL, **PE_TAIL_LATE}.items()):
                part(pe, BATCH - 1)

        @block.scalar
        def _(act):
            act.wait_ge(S["const_loaded"], C0)
            act.preload_act_table_set(LN_EXP_SET)
            nc.scalar.activation(a_sb[:, :, :], a_sb[:, :, :], ACT.Exp).then_inc(S["a_exp"], 1)
            act.preload_act_table_set(SILU_SET)
            with nc.scalar.Fori(0, DT // 2) as mp:
                for x in range(8):
                    par, tg = divmod(x, 4)
                    m = 2 * mp + par
                    count = 8 * mp + x + 1
                    act.wait_ge(S["x_mm"], count + X_MM)
                    nc.scalar.activation(cv[x % 2], bank(tg), ACT.Identity, bias=wxc[par][:, H + 4:H + 5],
                                         scale=wxc[par][:, H + 3:H + 4])\
                        .then_inc(S["conv_base"], 1)
                    if tg == 0:
                        act.wait_ge(S[f"u_stored{par}"], 16 * mp + ONE)
                        act.wait_ge(S["ss_mm"], 8 * mp + ONE)
                    act.wait_ge(S["conv_done"], count + CONV)
                    nc.scalar.activation(ust[par][:, tg * GT:(tg + 1) * GT], cv[x % 2], ACT.Silu)\
                        .then_inc(S["u_done"], 1)

            act.preload_act_table_set(LN_EXP_SET)
            act.wait_ge(S["ss_mean"], 2)
            nc.scalar.activation(ss3[:, :, :], ss3[:, :, :], ACT.Ln).then_inc(S["ss_ln"], 1)
            act.wait_ge(S["ss_ln"], 1)
            nc.scalar.activation(ss3[:, :, :], ss3[:, :, :], ACT.Exp, scale=-0.5).then_inc(S["ss_rstd"], 1)
            act.wait_ge(S["da_zero"], 1)
            act.wait_ge(S["a_neg"], 1)
            act_softplus(act, 0, 0, range(QD))
            with nc.scalar.Fori(0, NG - 1) as g:
                for q in range(NQ):
                    act_step(act, g, q)
            for q in range(NQ):
                act_step(act, NG - 1, q, last=(q == NQ - 1))

            act.wait_ge(S["p2_const"], C2)
            for o in range(OT):
                act_keys(act, 0, o)
            act_sequence(act, 0, keys=True, tail=False)
            with nc.scalar.Fori(1, BATCH - 1) as b:
                act_sequence(act, b, keys=True, tail=True)
            act_sequence(act, BATCH - 1, keys=False, tail=True)
            for _, part in sorted({**ACT_TAIL, **ACT_TAIL_LATE}.items()):
                part(act, BATCH - 1)

        @block.gpsimd
        def _(pool):
            pool.sem_inc(S["bm_ok"], BM)
            for name in ("dtu_ok",):
                pool.sem_inc(S[name], ONE)
            nc.gpsimd.memset(ident[:, :], 0.0)
            nc.gpsimd.memset(ones[:, :], 1.0)
            nc.gpsimd.memset(mhalf[:, :], -0.5)
            nc.gpsimd.memset(rbuf[:, :, :], 0.0)
            nc.gpsimd.memset(upper[:, :, :], 0.0)
            nc.gpsimd.memset(lower[:, :, :], 0.0).then_inc(S["phase0_zero"], 1)
            pool.wait_ge(S["phase0_zero"], 1)
            for e in range(NE):
                if e < NE - 1:
                    nc.gpsimd.memset(upper[:, e, e + 1:NE], 1.0)
                if e > 0:
                    nc.gpsimd.memset(lower[:, e, 0:e], 1.0)
            nc.gpsimd.affine_select(out=ident[:, :], in_=ident[:, :], compare_op=ALU.not_equal, fill=1.0,
                                    base=0, pattern=[[-1, P]], channel_multiplier=1)\
                .then_inc(S["pool_const"], 1)

            nc.gpsimd.memset(yq, 0.0).then_inc(S["phase0_zero"], 1)
            with nc.gpsimd.Fori(0, NG) as g:
                for q in range(NQ):
                    s = NQ * g + q
                    pool.wait_ge(S["dt_ok"], 4 * s + 4)
                    pool.wait_ge(S[f"u_loaded{q % 2}"], 16 * (2 * g + q // 2 + 1))
                    pool.wait_ge(S["bm_ok"], N * s + BM)
                    nc.gpsimd.tensor_tensor(dtu, dt[q % 2], uq[q % 2], ALU.mult).then_inc(S["dtu_ok"], 1)
                    pool.wait_ge(S["dtu_ok"], s + 1 + ONE)
                    for n in range(N):
                        if q == 0 and n % 4 == 0:
                            pool.wait_ge(S[f"brep_loaded{n // 4}"], 16 * g + 16)
                        pool.wait_ge(S["t_done"], 4 * (N * s + n) - 12 + T_DONE)
                        nc.gpsimd.tensor_tensor(
                            hb[n % 4].rearrange("p (i t) -> p i t", i=QD), dtu,
                            brep[:, n:n + 1, :].broadcast_to([P, QD, GT]), ALU.mult)\
                            .then_inc(S["bm_ok"], 1)
                        if q == 1 and n == 4:
                            pool_rstd(pool, g)

            pool_sequence(pool, 0, tail=False)
            pool_rstd(pool, NG)
            with nc.gpsimd.Fori(1, BATCH) as b:
                pool_sequence(pool, b, tail=True)
            pool_rstd2(pool, BATCH - 1, 0)
            pool_rstd2(pool, BATCH - 1, 1)

        @block.vector
        def _(dve):
            dve.sem_inc(S["conv_done"], CONV)
            for name in ("x3_add",):
                dve.sem_inc(S[name], ONE)
            dve.sem_inc(S["ss_added"], SS_ADD)
            dve.sem_inc(S["scan_ok"], SCAN)
            dve.sem_inc(S["acc_ok"], ACCD)
            dve.sem_inc(S["r_added"], R_ADD)
            dve.sem_inc(S["fin1"], FIN1)
            dve.sem_inc(S["fin"], FIN)
            nc.vector.memset(wdt[R:P, :], 0.0).then_inc(S["rows_set"], 1)
            nc.vector.memset(tsb[SS:P, :], 1.0).then_inc(S["rows_set"], 1)
            dve.wait_ge(S["const_loaded"], C0)
            dve.wait_ge(S["a_exp"], 1)
            nc.vector.tensor_scalar(a_sb[:, :, :], a_sb[:, :, :], -1.0, None, ALU.mult).then_inc(S["a_neg"], 1)
            nc.vector.memset(ssacc, 0.0).then_inc(S["ss_square"], 1)
            dve.wait_ge(S["ss_square"], 1)

            def add_ss(m):
                for j in range(4):
                    dve.wait_ge(S["ss_mm"], 4 * m + j + 1 + ONE)
                    dve.wait_ge(S["ss_added"], 4 * m + j + 1)
                    v = ssacc[:, 4 * j:4 * j + 4, :].rearrange("p a s -> p (a s)")
                    nc.vector.tensor_tensor(v, v, bank(4 + j)[:, 0:4 * SS], ALU.add)\
                        .then_inc(S["ss_added"], 1)

            with nc.vector.Fori(0, DT // 2) as mp:
                for x in range(8):
                    par, tg = divmod(x, 4)
                    m = 2 * mp + par
                    count = 8 * mp + x
                    dve.wait_ge(S["conv_base"], count + 1)
                    c = by_seq(cv[x % 2])
                    for sh in range(1, 4):
                        if sh > 1:
                            dve.wait_ge(S["conv_tap"], 2 * count + sh - 1)
                        last = nc.vector.scalar_tensor_tensor(
                            c[:, :, sh:SEQ], by_seq(bank(tg))[:, :, 0:SEQ - sh],
                            wxc[par][:, H + 3 - sh:H + 4 - sh],
                            c[:, :, sh:SEQ], ALU.mult, ALU.add)
                        last.then_inc(S["conv_tap" if sh < 3 else "conv_done"], 1)
                    if x == 5:
                        add_ss(2 * mp)
                add_ss(2 * mp + 1)
            dve.wait_ge(S["ss_added"], 4 * DT + SS_ADD)
            nc.vector.tensor_tensor(sssq, ssacc, ssacc, ALU.mult).then_inc(S["ss_square"], 1)
            dve.wait_ge(S["ss_square"], 2)
            parts = ((0, R), (R, R + N), (R + N, SS))
            for j, (lo, hi) in enumerate(parts):
                nc.vector.tensor_reduce(ss3[:, j, :], sssq[:, :, lo:hi], AX_X, ALU.add)\
                    .then_inc(S["ss_sum"], 1)
            dve.wait_ge(S["ss_sum"], 3)
            nc.vector.tensor_scalar(ss3[:, 0, :], ss3[:, 0, :], 1.0 / R, RMS_EPS, ALU.mult, ALU.add)\
                .then_inc(S["ss_mean"], 1)
            nc.vector.tensor_scalar(ss3[:, 1:3, :], ss3[:, 1:3, :], 1.0 / N, RMS_EPS, ALU.mult, ALU.add)\
                .then_inc(S["ss_mean"], 1)
            dve.wait_ge(S["ss_rstd"], 1)
            for j, (lo, hi) in enumerate(parts):
                v = ssacc[:, :, lo:hi]
                nc.vector.tensor_tensor(v, v, ss3[:, j, :][:, :, None].broadcast_to([P, TT, hi - lo]),
                                        ALU.mult).then_inc(S["ss_normed"], 1)
            dve.wait_ge(S["ss_normed"], 3)
            nc.vector.tensor_copy(cbt[:, :, :], ssacc[:, :, R + N:SS]).then_inc(S["phase0_c"], 1)
            dve.wait_ge(S["pool_const"], 1)
            for j in range(TT // 4):
                dve.wait_ge(S["bt_mm"], j + 1)
                nc.vector.tensor_copy(tsb[0:SS, j * HALF:(j + 1) * HALF], bank(BT_BANKS[j])[0:SS, :])\
                    .then_inc(S["bt_rows"], 1)

            for i in range(2):
                last = nc.vector.memset(by_seq(bank(i))[:, :, 0:1], 0.0)
            last.then_inc(S["da_zero"], 1)
            dve.wait_ge(S["phase0_c"], 1)
            dve.wait_ge(S["phase0_zero"], 2)
            dve_dt(dve, 0, 0, range(QD))
            for i in range(2 * QD):
                dve_scan(dve, 0, 0, i // QD, i % QD)

            with nc.vector.Fori(0, NG - 1) as g:
                dve_group(dve, g, last=False)
            dve_group(dve, NG - 1, last=True)
            for c in range(4):
                dve_out(dve, NG * NQ, c)

            dve.wait_ge(S["p2_const"], C2)
            nc.vector.memset(bful[NE * ER:P, :], 0.0).then_inc(S["rows_set"], 1)
            nc.vector.memset(mg[:, NE * ER:P], 0.0).then_inc(S["rows_set"], 1)
            dve.wait_ge(S["ph_mm"], 1)
            nc.vector.tensor_copy(ph, banks[0][:, :].rearrange("p (h c) -> p h c", h=HEADS))\
                .then_inc(S["ph_ok"], 1)
            nc.vector.tensor_scalar(gs[:, :], bov[:, 1:2], float(np.sqrt(SEQ)), None, ALU.mult)\
                .then_inc(S["gs_ok"], 1)
            dve.wait_ge(S["gs_ok"], 1)
            nc.vector.tensor_tensor(gb[:, :], gs[:, :], bov[:, 0:1], ALU.mult).then_inc(S["gs_ok"], 1)
            for o in range(OT):
                dve_keys(dve, 0, o)
                dve_out(dve, NG * NQ, 4 + o)
            dve_sequence(dve, 0, keys=True, tail=False)
            dve_ln_stats(dve, NG)
            dve_ln_apply(dve, NG)
            with nc.vector.Fori(1, BATCH - 1) as b:
                dve_sequence(dve, b, keys=True, tail=True)
            dve_sequence(dve, BATCH - 1, keys=False, tail=True)
            for t in sorted(DVE_TAIL):
                DVE_TAIL[t](dve, BATCH - 1)


def _layouts(i):
    f = np.ascontiguousarray
    x = np.asarray(i["x"])
    ctx = np.asarray(i["ctx_4096"])
    tok = x.reshape(TOK, H)
    win = np.asarray(i["L0_attn_W_in"])
    tiles = win.reshape(2 * DT, P, KC, P).transpose(0, 3, 2, 1)
    taps = np.concatenate([np.asarray(i["L0_attn_conv_w"]), np.asarray(i["L0_attn_conv_b"])[:, None]],
                          axis=1).reshape(DT, P, 5)
    per_tile = lambda v: f(np.asarray(v).reshape(DT, P, -1).transpose(1, 0, 2))
    heads = lambda w: f(w.reshape(HEADS, DH, P).transpose(1, 0, 2))
    return {
        "xT": f(tok.T.reshape(KC, P, TOK).transpose(1, 0, 2)),
        "x": f(x.reshape(NG, GB, SEQ, H).transpose(0, 2, 1, 3)),
        "ctx": f(ctx),
        "ctxT": f(ctx.reshape(BATCH, SEQ, NT, P).transpose(0, 3, 2, 1)),
        "WinX": f(np.concatenate([tiles[:DT].reshape(DT, P, H), taps], axis=2)),
        "WinZ": f(tiles[DT:]),
        "WxT": f(np.asarray(i["L0_attn_W_x"]).reshape(SS, DT, P).transpose(2, 1, 0)),
        "WdtT": f(np.asarray(i["L0_attn_W_dt"]).T),
        "b_dt": f(np.asarray(i["L0_attn_b_dt"]).reshape(1, D_IN)),
        "A_log": per_tile(i["L0_attn_A_log"]),
        "D": per_tile(i["L0_attn_D"]).reshape(P, DT),
        "WoutT": f(np.asarray(i["L0_attn_W_out"]).T.reshape(NQ, QD, P, H).transpose(0, 2, 1, 3)),
        "WqT": f(np.asarray(i["L0_xattn_Wq"]).T),
        "WkT": f(np.asarray(i["L0_xattn_Wk"]).T),
        "Wvh": heads(np.asarray(i["L0_xattn_Wv"])),
        "Woh": heads(f(np.asarray(i["L0_xattn_Wo"]).T)),
        "bo": f(np.asarray(i["L0_xattn_bo"]).reshape(P, 1)),
        "g": f(np.asarray(i["L0_xattn_g"]).reshape(P, 1)),
        "RAT": f(np.concatenate([np.asarray(i["L0_ffn_router_w"]),
                                 np.asarray(i["L0_ffn_A"]).reshape(NE * ER, H)])
                 .T.reshape(KC, P, RA).transpose(1, 0, 2)),
        "Bf": f(np.asarray(i["L0_ffn_B"]).transpose(0, 2, 1).reshape(NE * ER, H)),
    }


def kernel(**inputs):
    import concourse.bacc as bacc
    from concourse.bass_utils import run_bass_kernel_spmd

    nc = bacc.Bacc("TRN2", target_bir_lowering=False, num_devices=1)
    arrays = {f"in_{k}": v for k, v in _layouts(inputs).items()}
    aps = {k[3:]: nc.dram_tensor(k, v.shape, mybir.dt.from_np(v.dtype), kind="ExternalInput").ap()
           for k, v in arrays.items()}
    out = nc.dram_tensor("out", (BATCH, SEQ, H), F32, kind="ExternalOutput").ap()
    program(nc, aps, out)
    r = run_bass_kernel_spmd(nc, [arrays], core_ids=[0])
    return r.results[0]["out"]
```
